# Optimizing a Trainium2 kernel written in Bass

```python
import numpy as np
import jax
import jax.numpy as jnp

def _softmax(x, axis=-1):
    return jax.nn.softmax(x, axis=axis)

def _gelu(x):
    return jax.nn.gelu(x, approximate=True)

def _silu(x):
    return jax.nn.silu(x)

def _sigmoid(x):
    return jax.nn.sigmoid(x)

def _layernorm(x, axis=-1, eps=1e-05):
    m = jnp.mean(x, axis=axis, keepdims=True)
    v = jnp.var(x, axis=axis, keepdims=True)
    return (x - m) / jnp.sqrt(v + eps)

def _scatter_add(tgt, idx, src, axis=0):
    return tgt.at[idx].add(src)

def _segment_sum(src, seg, n):
    return jax.ops.segment_sum(src, seg, n)
kernel_name = 'mk_adj_resnorm_d4_adj_r2_cdf92f'

def setup_inputs(seed: int=0):
    np.random.seed(seed)
    _w = jnp.asarray

    def _rec_inputs():
        import jax
        import jax.numpy as jnp
        _gk = jax.random.key(seed)
        x = -0.0002928 + 1 * jax.random.normal(jax.random.fold_in(_gk, 1), (8, 1024, 64), jnp.float32)
        _a = jax.random.bernoulli(jax.random.fold_in(_gk, 2), 0.00195312, (1024, 1024))
        _a = jnp.logical_or(_a, jnp.swapaxes(_a, -1, -2))
        _a = jnp.logical_or(_a, jnp.eye(1024, dtype=bool))
        _af = _a.astype(jnp.float32)
        _af = _af / jnp.maximum(_af.sum(-1, keepdims=True), 1.0)
        adj = _af
        return (x, adj)
    x, adj = _rec_inputs()

    def _L0_gnn_setup():
        import jax, jax.numpy as jnp
        import numpy as np
        key = jax.random.key(seed)
        ks = jax.random.split(key, 5)
        B, N, IN, OUT, K, D = (32, 1024, 64, 64, 3, 16)
        x = jax.random.normal(ks[0], (B, N, IN), dtype=jnp.float32)
        A = jax.random.uniform(ks[1], (N, N), dtype=jnp.float32)
        A = A / jnp.sum(A, axis=-1, keepdims=True)
        embedding = jax.random.normal(ks[2], (N, D), dtype=jnp.float32) * 0.3
        weight = jax.random.normal(ks[3], (D, K, IN, OUT), dtype=jnp.float32) * 0.1
        bias = jax.random.normal(ks[4], (D, OUT), dtype=jnp.float32) * 0.1
        return {'x': x, 'A': A, 'embedding': embedding, 'weight': weight, 'bias': bias}
    _L0_gnn_all = _L0_gnn_setup()
    _L0_gnn_in = {k: v for k, v in _L0_gnn_all.items() if k in ('embedding', 'weight', 'bias')}
    del _L0_gnn_all

    def _L1_gnn_setup():
        import jax, jax.numpy as jnp
        import numpy as np
        B, N, F, L = (4, 4096, 64, 2)
        key = jax.random.key(seed)
        k1, k2, k3 = jax.random.split(key, 3)
        x = jax.random.normal(k1, (B, N, F), dtype=jnp.float32)
        net_params = jax.random.normal(k2, (L * F * F,), dtype=jnp.float32)
        A = jax.random.normal(k3, (N, N), dtype=jnp.float32)
        return {'x': x, 't': 0, 'net_params': net_params, 'A': A}
    _L1_gnn_all = _L1_gnn_setup()
    _L1_gnn_in = {k: v for k, v in _L1_gnn_all.items() if k in ('net_params',)}
    del _L1_gnn_all

    def _L2_gnn_setup():
        import jax, jax.numpy as jnp
        import numpy as np
        NEG_INF = -1e+16

        def gat_layer(x, graph, W, b):
            h = x @ W
            s = jnp.einsum('bnd,bmd->bnm', h, h) * graph
            s = jnp.where(s == 0.0, NEG_INF, s)
            a = jax.nn.softmax(s, axis=2)
            return jnp.einsum('bnm,bmd->bnd', a, h) + b
        key = jax.random.key(seed)
        k1, k2, k3, k4, k5, k6 = jax.random.split(key, 6)
        B, N, C_IN, HID, HEADS, C_OUT = (16, 512, 64, 128, 8, 64)
        flow_x = jax.random.normal(k1, (B, N, C_IN), dtype=jnp.float32)
        graph = jax.random.randint(k2, (N, N), 0, 2).astype(jnp.float32)
        Wh = jax.random.normal(k3, (HEADS, C_IN, HID), dtype=jnp.float32)
        bh = jax.random.normal(k4, (HEADS, HID), dtype=jnp.float32)
        W_out = jax.random.normal(k5, (HID * HEADS, C_OUT), dtype=jnp.float32)
        b_out = jax.random.normal(k6, (C_OUT,), dtype=jnp.float32)
        return {'flow_x': flow_x, 'graph': graph, 'Wh': Wh, 'bh': bh, 'W_out': W_out, 'b_out': b_out}
    _L2_gnn_all = _L2_gnn_setup()
    _L2_gnn_in = {k: v for k, v in _L2_gnn_all.items() if k in ('Wh', 'bh', 'W_out', 'b_out')}
    del _L2_gnn_all

    def _L3_gnn_setup():
        import jax, jax.numpy as jnp
        import numpy as np
        NEG = -1000000000.0
        key = jax.random.key(seed)
        ks = jax.random.split(key, 14)
        B, N, E, NF, NH = (8, 1024, 64, 64, 64)
        x = jax.random.normal(ks[0], (B, N, NF), dtype=jnp.float32)
        base = jax.nn.one_hot(jax.random.randint(ks[1], (N,), 0, E), E, dtype=jnp.float32)
        extra = (jax.random.uniform(ks[2], (N, E)) < 0.03).astype(jnp.float32)
        H = jnp.clip(base + extra, 0.0, 1.0)
        adj = (jax.random.uniform(ks[3], (N, N)) < 0.01).astype(jnp.float32)
        adj = jnp.clip(adj + jnp.eye(N, dtype=jnp.float32), 0.0, 1.0)
        s_in = 1.0 / np.sqrt(NF)
        s_h = 1.0 / np.sqrt(NH)
        W = jax.random.normal(ks[4], (NF, NH), dtype=jnp.float32) * s_in
        W_ind = jax.random.normal(ks[5], (NF, NH), dtype=jnp.float32) * s_in
        a_node = jax.random.normal(ks[6], (NH,), dtype=jnp.float32) * s_h
        a_gn = jax.random.normal(ks[7], (NH,), dtype=jnp.float32) * s_h
        a_ge = jax.random.normal(ks[8], (NH,), dtype=jnp.float32) * s_h
        fcW = jax.random.normal(ks[9], (NH, 2 * NH), dtype=jnp.float32) * s_h
        fcb = jnp.zeros((2 * NH,), dtype=jnp.float32)
        av = jax.random.normal(ks[10], (2 * NH,), dtype=jnp.float32) / np.sqrt(2 * NH)
        return {'x': x, 'H': H, 'adj': adj, 'nhid': NH, 'W': W, 'W_ind': W_ind, 'a_node': a_node, 'a_gn': a_gn, 'a_ge': a_ge, 'fcW': fcW, 'fcb': fcb, 'av': av}
    _L3_gnn_all = _L3_gnn_setup()
    _L3_gnn_in = {k: v for k, v in _L3_gnn_all.items() if k in ('H', 'W', 'W_ind', 'a_node', 'a_gn', 'a_ge', 'fcW', 'fcb', 'av')}
    del _L3_gnn_all
    return {'x': x, 'adj': adj, 'L0_gnn_embedding': _L0_gnn_in['embedding'], 'L0_gnn_weight': _L0_gnn_in['weight'], 'L0_gnn_bias': _L0_gnn_in['bias'], 'L1_gnn_net_params': _L1_gnn_in['net_params'], 'L2_gnn_Wh': _L2_gnn_in['Wh'], 'L2_gnn_bh': _L2_gnn_in['bh'], 'L2_gnn_W_out': _L2_gnn_in['W_out'], 'L2_gnn_b_out': _L2_gnn_in['b_out'], 'L3_gnn_H': _L3_gnn_in['H'], 'L3_gnn_W': _L3_gnn_in['W'], 'L3_gnn_W_ind': _L3_gnn_in['W_ind'], 'L3_gnn_a_node': _L3_gnn_in['a_node'], 'L3_gnn_a_gn': _L3_gnn_in['a_gn'], 'L3_gnn_a_ge': _L3_gnn_in['a_ge'], 'L3_gnn_fcW': _L3_gnn_in['fcW'], 'L3_gnn_fcb': _L3_gnn_in['fcb'], 'L3_gnn_av': _L3_gnn_in['av']}

def reference(x, adj, L0_gnn_embedding, L0_gnn_weight, L0_gnn_bias, L1_gnn_net_params, L2_gnn_Wh, L2_gnn_bh, L2_gnn_W_out, L2_gnn_b_out, L3_gnn_H, L3_gnn_W, L3_gnn_W_ind, L3_gnn_a_node, L3_gnn_a_gn, L3_gnn_a_ge, L3_gnn_fcW, L3_gnn_fcb, L3_gnn_av):
    import jax
    import jax.numpy as jnp

    def _L0_gnn_ref(x, A, embedding, weight, bias):
        import jax, jax.numpy as jnp
        import numpy as np
        K = weight.shape[1]
        N = A.shape[-2]
        w = jnp.einsum('nd,dkio->nkio', embedding, weight)
        b = jnp.einsum('nd,do->no', embedding, bias)
        As = [jnp.eye(N, dtype=x.dtype)]
        if K > 1:
            As.append(A)
        for _ in range(2, K):
            As.append(2.0 * (A @ As[-1]) - As[-2])
        A_stack = jnp.stack(As, 0)
        x_g = jnp.einsum('knm,bmc->bnkc', A_stack, x)
        out = jnp.einsum('bnki,nkio->bno', x_g, w)
        return out + b

    def _L1_gnn_ref(x, t, net_params, A):
        import jax, jax.numpy as jnp
        import numpy as np
        B, N, F, L = (4, 4096, 64, 2)
        weights = net_params.reshape(L, F, F)
        z = x.reshape(-1, A.shape[1], F)
        for i in range(L):
            h = jnp.einsum('mn,bnf->bmf', A, z)
            z = jnp.einsum('bmf,fg->bmg', h, weights[i])
            z = jax.nn.relu(z)
        return z

    def _L2_gnn_ref(flow_x, graph, Wh, bh, W_out, b_out):
        import jax, jax.numpy as jnp
        import numpy as np
        NEG_INF = -1e+16

        def gat_layer(x, graph, W, b):
            h = x @ W
            s = jnp.einsum('bnd,bmd->bnm', h, h) * graph
            s = jnp.where(s == 0.0, NEG_INF, s)
            a = jax.nn.softmax(s, axis=2)
            return jnp.einsum('bnm,bmd->bnd', a, h) + b
        heads = jax.vmap(lambda W, b: gat_layer(flow_x, graph, W, b))(Wh, bh)
        H, B, N, D = heads.shape
        cat = jnp.moveaxis(heads, 0, 2).reshape(B, N, H * D)
        x = jax.nn.leaky_relu(cat, negative_slope=0.01)
        out = gat_layer(x, graph, W_out, b_out)
        return jax.nn.leaky_relu(out, negative_slope=0.01)

    def _L3_gnn_ref(x, H, adj, nhid, W, W_ind, a_node, a_gn, a_ge, fcW, fcb, av):
        import jax, jax.numpy as jnp
        import numpy as np
        NEG = -1000000000.0
        h = x @ W
        maskEN = H.T
        s = jax.nn.leaky_relu(h @ a_node, 0.2)
        logits = jnp.where(maskEN[None, :, :] > 0, s[:, None, :], NEG)
        alpha = jax.nn.softmax(logits, axis=-1)
        agg = jnp.einsum('ben,bnf->bef', alpha, h)
        beta = jax.nn.sigmoid((h @ a_gn)[:, None, :] + (agg @ a_ge)[:, :, None])
        all_he = beta[..., None] * h[:, None, :, :] + (1.0 - beta[..., None]) * agg[:, :, None, :]
        deg = jnp.maximum(adj.sum(-1), 1.0)[:, None]
        industry = jnp.einsum('nm,bmf->bnf', adj / deg, x @ W_ind)
        all_he = jax.nn.elu(all_he)
        he = jax.nn.elu(agg)

        def attn_scores(f):
            return jnp.tanh(f @ fcW + fcb) @ av
        se = attn_scores(he)
        logits2 = jnp.where(H[None, :, :] > 0, se[:, None, :], NEG)
        coefs1 = jax.nn.softmax(logits2, axis=-1)
        g = jnp.einsum('bne,benf->bnf', coefs1, all_he)
        pair = jnp.stack([industry, g], axis=2)
        coefs2 = jax.nn.softmax(attn_scores(pair), axis=-1)
        out = jnp.einsum('bnk,bnkf->bnf', coefs2, pair)
        return out
    x = _layernorm(x + _L0_gnn_ref(x, adj, L0_gnn_embedding, L0_gnn_weight, L0_gnn_bias), axis=-1)
    x = _layernorm(x + _L1_gnn_ref(x, 0, L1_gnn_net_params, adj), axis=-1)
    x = _layernorm(x + _L2_gnn_ref(x, adj, L2_gnn_Wh, L2_gnn_bh, L2_gnn_W_out, L2_gnn_b_out), axis=-1)
    x = _layernorm(x + _L3_gnn_ref(x, L3_gnn_H, adj, 64, L3_gnn_W, L3_gnn_W_ind, L3_gnn_a_node, L3_gnn_a_gn, L3_gnn_a_ge, L3_gnn_fcW, L3_gnn_fcb, L3_gnn_av), axis=-1)
    return x

_drawn_inputs = setup_inputs


def setup_inputs(seed=0):
    import zlib

    import numpy as np

    out = dict(_drawn_inputs(seed))
    spreads = {'L3_gnn_fcb': (0.0, 0.498)}
    factors = {'L2_gnn_b_out': 8.0, 'L3_gnn_H': 3.764, 'L3_gnn_a_node': 3.277}
    for name, (base, spread) in spreads.items():
        noise = np.random.default_rng([zlib.crc32(name.encode()), seed]).standard_normal(out[name].shape)
        drawn = base * np.exp(spread * noise) if base else spread * noise
        out[name] = jnp.asarray(drawn.astype(out[name].dtype))
    for name, factor in factors.items():
        out[name] = (out[name] * factor).astype(out[name].dtype)
    return out
```

```python
from contextlib import ExitStack

import concourse.bass as bass
from concourse import mybir

F32 = mybir.dt.float32
F32R = mybir.dt.float32r
ALU = mybir.AluOpType
ACT = mybir.ActivationFunctionType
AX_X = mybir.AxisListType.X

P = 128
EPS = 1e-5
MASKED = -1e16
NEG = -1e9


class Ctx:
    pass



def f32(ap):
    return ap.bitcast(F32)



def load_and_transpose_adjacency(nc, k, adj, x, params):
    N, NC = k.N, k.NC
    emb, weight, bias = params
    D, K, F, O = weight.shape
    with ExitStack() as ctx:
        sb = lambda n, s, d=F32: ctx.enter_context(nc.sbuf_tensor(n, s, d))
        sem = k.sem
        an = sb("adj_rows", [P, NC, N])
        w_raw = sb("w_raw", [P, K, D, O])
        embT = sb("embT", [D, N])
        bias_sb = sb("bias_sb", [D, O])
        adj_loaded = [sem(f"adj_loaded{c}") for c in range(NC)]
        x_loaded, w_loaded = sem("x_loaded"), sem("w_loaded")
        zeroed, ident_ready = sem("ident_zeroed"), sem("ident_ready")
        at_transposed, at_hi_ready, at_lo_ready = sem("at_transposed"), sem("at_hi_ready"), sem("at_lo_ready")
        embT_in_psum, embT_ready, nbias_in_psum, setup_done = (
            sem("embT_in_psum"), sem("embT_ready"), sem("nbias_in_psum"), sem("setup_done"))
        split_ready = sem("split0_hi_ready")

        with nc.Block() as block:
            @block.sync
            def _(sp):
                for c in range(NC):
                    sp.dma_start(an[:, c, :], adj[c * P:(c + 1) * P, :]).then_inc(adj_loaded[c], 16)
                for c in range(NC):
                    sp.dma_start(k.xn[:, c, :, :], x[:, c * P:(c + 1) * P, :].rearrange("b p f -> p b f")).then_inc(x_loaded, 16)

            @block.gpsimd
            def _(pool):
                nc.gpsimd.memset(k.ident[:, :], 0.0).then_inc(zeroed, 1)
                pool.wait_ge(zeroed, 1)
                nc.gpsimd.affine_select(out=k.ident[:, :], in_=k.ident[:, :], compare_op=ALU.not_equal, fill=1.0,
                                        base=0, pattern=[[-1, P]], channel_multiplier=1).then_inc(ident_ready, 1)
                pool.dma_start(k.emb[:, :, :], emb.rearrange("(c p) d -> p c d", p=P)).then_inc(w_loaded, 16)
                pool.dma_start(bias_sb[:, :], bias).then_inc(w_loaded, 16)
                for half in range(2):
                    for t in range(K):
                        pool.dma_start(w_raw[half * F:(half + 1) * F, t, :, :],
                                       weight[:, t, :, :].rearrange("d i o -> i d o")).then_inc(w_loaded, 16)

            @block.tensor
            def _(pe):
                pe.wait_ge(ident_ready, 1)
                for mc in range(NC):
                    if mc == 0:
                        for c in range(NC):
                            pe.wait_ge(adj_loaded[c], 16)
                    if mc >= 2:
                        pe.wait_ge(at_lo_ready, mc - 1)
                    for c in range(NC):
                        last = nc.tensor.transpose(k.wide[mc % 2][:, c * P:(c + 1) * P], an[:, c, mc * P:(mc + 1) * P], k.ident[:, :])
                    last.then_inc(at_transposed, 1)
                pe.wait_ge(w_loaded, 16 * (2 + 2 * K))
                for c in range(NC):
                    last = nc.tensor.transpose(k.pair[0:D, c * P:(c + 1) * P], k.emb[:, c, :], k.ident[:, :])
                last.then_inc(embT_in_psum, 1)
                pe.wait_ge(embT_ready, 1)
                for c in range(NC):
                    last = nc.tensor.matmul(k.bank_u[:, c * O:(c + 1) * O], embT[:, c * P:(c + 1) * P], bias_sb[:, :], start=True, stop=True)
                last.then_inc(nbias_in_psum, 1)

            @block.scalar
            def _(act):
                act.wait_ge(x_loaded, 16 * NC)
                nc.scalar.activation(k.split[0][:, :, :, 0, :].rearrange("p c b f -> p (c b) f"),
                                     k.xn[:, :, :, :].rearrange("p c b f -> p (c b) f"), ACT.Copy).then_inc(split_ready, 1)
                for mc in range(NC):
                    act.wait_ge(at_transposed, mc + 1)
                    nc.scalar.activation(k.at_hi[:, mc, :], k.wide[mc % 2][:, :], ACT.Copy).then_inc(at_hi_ready, 1)
                act.wait_ge(w_loaded, 16 * (2 + 2 * K))
                for t in range(K):
                    nc.scalar.activation(k.w_split[:, t, 0, :].rearrange("p (o d) -> p o d", d=D),
                                         w_raw[:, t, :, :].rearrange("p d o -> p o d"), ACT.Copy).then_inc(split_ready, 1)
                act.wait_ge(embT_in_psum, 1)
                nc.scalar.activation(embT[:, :], k.pair[0:D, :], ACT.Copy).then_inc(embT_ready, 1)
                act.wait_ge(nbias_in_psum, 1)
                nc.scalar.activation(k.node_bias[:, :, :].rearrange("p c o -> p (c o)"), k.bank_u[:, :], ACT.Copy).then_inc(setup_done, 1)

            @block.vector
            def _(dve):
                dve.wait_ge(split_ready, 1)
                nc.vector.tensor_tensor(k.split[0][:, :, :, 1, :].rearrange("p c b f -> p (c b) f"),
                                        k.xn[:, :, :, :].rearrange("p c b f -> p (c b) f"),
                                        f32(k.split[0][:, :, :, 0, :]).rearrange("p c b f -> p (c b) f"), ALU.subtract).then_inc(setup_done, 1)
                for mc in range(NC):
                    dve.wait_ge(at_hi_ready, mc + 1)
                    nc.vector.tensor_tensor(k.at_lo[:, mc, :], k.wide[mc % 2][:, :], f32(k.at_hi[:, mc, :]), ALU.subtract).then_inc(at_lo_ready, 1)
                for c in range(NC):
                    dve.wait_ge(adj_loaded[c], 16)
                    nc.vector.reduce_sum(k.deg[:, c:c + 1], an[:, c, :], axis=AX_X).then_inc(setup_done, 1)
                for t in range(K):
                    dve.wait_ge(split_ready, 2 + t)
                    nc.vector.tensor_tensor(k.w_split[:, t, 1, :].rearrange("p (o d) -> p o d", d=D),
                                            w_raw[:, t, :, :].rearrange("p d o -> p o d"),
                                            f32(k.w_split[:, t, 0, :]).rearrange("p (o d) -> p o d", d=D), ALU.subtract).then_inc(setup_done, 1)



def layer_norm(nc, k, tag, add=None):
    G, F = k.NC * k.B, k.F
    with ExitStack() as ctx:
        sb = lambda n, s, d=F32: ctx.enter_context(nc.sbuf_tensor(n + tag, s, d))
        sem = lambda n: k.sem(n + tag)
        sq = sb("ln_sq", [P, G, F])
        total, mean, var, std, rstd = (sb(n, [P, G]) for n in ("ln_total", "ln_mean", "ln_var", "ln_std", "ln_rstd"))
        step, centred, squared, var_ready, std_ready = (
            sem(n) for n in ("ln_step", "ln_centred", "ln_squared", "ln_var_ready", "ln_std_ready"))
        x = k.xn[:, :, :, :].rearrange("p c b f -> p (c b) f")
        with nc.Block() as block:
            @block.scalar
            def _(act):
                act.wait_ge(centred, 1)
                nc.scalar.activation(sq[:, :, :], x, ACT.Square).then_inc(squared, 1)
                act.wait_ge(var_ready, 1)
                nc.scalar.activation(std[:, :], var[:, :], ACT.Sqrt).then_inc(std_ready, 1)

            @block.vector
            def _(dve):
                n = 0
                if add is not None:
                    nc.vector.tensor_tensor(k.xn[:, :, :, :], k.xn[:, :, :, :], add, ALU.add).then_inc(step, 1)
                    n += 1
                    dve.wait_ge(step, n)
                nc.vector.reduce_sum(total[:, :], x, axis=AX_X).then_inc(step, 1)
                dve.wait_ge(step, n + 1)
                nc.vector.tensor_scalar(mean[:, :], total[:, :], 1.0 / F, None, ALU.mult).then_inc(step, 1)
                dve.wait_ge(step, n + 2)
                nc.vector.tensor_tensor(x, x, mean[:, :].unsqueeze(2).broadcast_to([P, G, F]), ALU.subtract).then_inc(centred, 1)
                dve.wait_ge(squared, 1)
                nc.vector.reduce_sum(total[:, :], sq[:, :, :], axis=AX_X).then_inc(step, 1)
                dve.wait_ge(step, n + 3)
                nc.vector.tensor_scalar(var[:, :], total[:, :], 1.0 / F, EPS, ALU.mult, ALU.add).then_inc(var_ready, 1)
                dve.wait_ge(std_ready, 1)
                nc.vector.reciprocal(rstd[:, :], std[:, :]).then_inc(step, 1)
                dve.wait_ge(step, n + 4)
                nc.vector.tensor_tensor(std[:, :], rstd[:, :], rstd[:, :], ALU.mult).then_inc(step, 1)
                dve.wait_ge(step, n + 5)
                nc.vector.tensor_tensor(std[:, :], std[:, :], var[:, :], ALU.mult).then_inc(step, 1)
                dve.wait_ge(step, n + 6)
                nc.vector.tensor_scalar(std[:, :], std[:, :], -0.5, 1.5, ALU.mult, ALU.add).then_inc(step, 1)
                dve.wait_ge(step, n + 7)
                nc.vector.tensor_tensor(rstd[:, :], rstd[:, :], std[:, :], ALU.mult).then_inc(step, 1)
                dve.wait_ge(step, n + 8)
                nc.vector.tensor_tensor(x, x, rstd[:, :].unsqueeze(2).broadcast_to([P, G, F]), ALU.mult).then_inc(step, 1)



def node_weight_convolution(nc, k):
    NC, B, F, D, K, O = k.NC, k.B, k.F, k.D, k.K, k.F
    CH = O * D // 512
    with ExitStack() as ctx:
        sb = lambda n, s, d=F32: ctx.enter_context(nc.sbuf_tensor(n, s, d))
        sem = k.sem
        cheb1 = k.split[1]
        cheb2 = [sb(f"cheb2_{i}", [P, B, 2, F], F32R) for i in range(2)]
        cheb2_full = sb("cheb2_full", [P, B, F])
        stat = [sb(f"l0_stat{i}", [P, K, P], F32R) for i in range(2)]
        weighted = [sb(f"l0_weighted{i}", [P, O, D]) for i in range(2)]
        summed = [sb(f"l0_summed{i}", [P, B, O]) for i in range(2)]
        prod_ready, hi_ready, cheb1_ready = sem("l0_prod_ready"), sem("l0_hi_ready"), sem("l0_cheb1_ready")
        full_ready, cheb2_ready = sem("l0_full_ready"), sem("l0_cheb2_ready")
        stat_in_psum, stat_ready, y_ready, weighted_ready, summed_ready, step = (
            sem(n) for n in ("l0_stat_in_psum", "l0_stat_ready", "l0_y_ready", "l0_weighted_ready", "l0_summed_ready", "l0_step"))
        prod = [k.bank_u, k.bank_m]
        tpos = [k.pair[:, 0:512], k.pair[:, 512:1024]]

        def product(pe, c, src, bank):
            n = 0
            for a, s in ((k.at_hi, 0), (k.at_hi, 1), (k.at_lo, 0)):
                for mc in range(NC):
                    last = nc.tensor.matmul(bank[:, :].rearrange("p (b f) -> p b f", f=F), a[:, mc, c * P:(c + 1) * P],
                                            src[:, mc, :, s, :], start=n == 0, stop=n == 3 * NC - 1)
                    n += 1
            return last

        with nc.Block() as block:
            @block.tensor
            def _(pe):
                for c in range(NC):
                    if c >= 2:
                        pe.wait_ge(cheb1_ready, c - 1)
                    product(pe, c, k.split[0], prod[c % 2]).then_inc(prod_ready, 1)
                pe.wait_ge(cheb1_ready, NC)
                product(pe, 0, cheb1, prod[0]).then_inc(prod_ready, 1)
                for c in range(NC):
                    if c + 1 < NC:
                        if c >= 1:
                            pe.wait_ge(full_ready, c)
                        product(pe, c + 1, cheb1, prod[(c + 1) % 2]).then_inc(prod_ready, 1)
                    pe.wait_ge(cheb2_ready, c + 1)

                    def turn(t):
                        b = t % B
                        if t >= 2:
                            pe.wait_ge(stat_ready, t - 1)
                        for i, s in enumerate((k.split[0][:, c, b, :, :], cheb1[:, c, b, :, :], cheb2[c % 2][:, b, :, :])):
                            last = nc.tensor.transpose(tpos[t % 2][:, i * P:(i + 1) * P],
                                                       f32(s).rearrange("p s f -> p (s f)"), k.ident[:, :])
                        last.then_inc(stat_in_psum, 1)

                    turn(c * B)
                    for b in range(B):
                        t = c * B + b
                        if b + 1 < B:
                            turn(t + 1)
                        pe.wait_ge(stat_ready, t + 1)
                        if t >= 2:
                            pe.wait_ge(weighted_ready, t - 1)
                        for j in range(CH):
                            for i in range(K):
                                for part in range(2):
                                    last = nc.tensor.matmul(k.wide[t % 2][:, j * 512:(j + 1) * 512], stat[t % 2][:, i, :],
                                                            k.w_split[:, i, part, j * 512:(j + 1) * 512],
                                                            start=i + part == 0, stop=i == K - 1 and part == 1)
                        last.then_inc(y_ready, 1)

            @block.scalar
            def _(act):
                for c in range(NC):
                    act.wait_ge(prod_ready, c + 1)
                    nc.scalar.activation(cheb1[:, c, :, 0, :], prod[c % 2][:, :].rearrange("p (b f) -> p b f", f=F), ACT.Copy).then_inc(hi_ready, 1)

                def cheb2_hi(c):
                    act.wait_ge(full_ready, c + 1)
                    if c >= 2:
                        act.wait_ge(stat_in_psum, (c - 1) * B)
                    nc.scalar.activation(cheb2[c % 2][:, :, 0, :], cheb2_full[:, :, :], ACT.Copy).then_inc(hi_ready, 1)

                cheb2_hi(0)
                for c in range(NC):
                    for b in range(B):
                        t = c * B + b
                        if b == 5 and c + 1 < NC:
                            cheb2_hi(c + 1)
                        act.wait_ge(stat_in_psum, t + 1)
                        if t >= 2:
                            act.wait_ge(y_ready, t - 1)
                        nc.scalar.activation(stat[t % 2][:, :, :].rearrange("p k n -> p (k n)"), tpos[t % 2][:, 0:K * P], ACT.Copy).then_inc(stat_ready, 1)

            @block.vector
            def _(dve):
                for c in range(NC):
                    dve.wait_ge(hi_ready, c + 1)
                    nc.vector.tensor_tensor(cheb1[:, c, :, 1, :], prod[c % 2][:, :].rearrange("p (b f) -> p b f", f=F),
                                            f32(cheb1[:, c, :, 0, :]), ALU.subtract).then_inc(cheb1_ready, 1)

                def cheb2_parts(c):
                    dve.wait_ge(prod_ready, NC + c + 1)
                    if c >= 1:
                        dve.wait_ge(cheb2_ready, c)
                    nc.vector.scalar_tensor_tensor(out=cheb2_full[:, :, :], in0=prod[c % 2][:, :].rearrange("p (b f) -> p b f", f=F),
                                                   scalar=2.0, in1=k.xn[:, c, :, :], op0=ALU.mult, op1=ALU.subtract).then_inc(full_ready, 1)
                    dve.wait_ge(hi_ready, NC + c + 1)
                    if c >= 2:
                        dve.wait_ge(stat_in_psum, (c - 1) * B)
                    nc.vector.tensor_tensor(cheb2[c % 2][:, :, 1, :], cheb2_full[:, :, :], f32(cheb2[c % 2][:, :, 0, :]), ALU.subtract).then_inc(cheb2_ready, 1)

                n = 0
                cheb2_parts(0)
                for c in range(NC):
                    emb_b = k.emb[:, c, :].unsqueeze(1).broadcast_to([P, O, D])
                    for b in range(B):
                        t = c * B + b
                        if b == 5 and c + 1 < NC:
                            cheb2_parts(c + 1)
                        dve.wait_ge(y_ready, t + 1)
                        if t >= 1:
                            dve.wait_ge(summed_ready, t)
                        nc.vector.tensor_tensor(weighted[t % 2][:, :, :], k.wide[t % 2][:, :].rearrange("p (o d) -> p o d", d=D), emb_b, ALU.mult).then_inc(weighted_ready, 1)
                        dve.wait_ge(weighted_ready, t + 1)
                        nc.vector.reduce_sum(summed[c % 2][:, b, :], weighted[t % 2][:, :, :], axis=AX_X).then_inc(summed_ready, 1)
                    dve.wait_ge(summed_ready, (c + 1) * B)
                    nc.vector.tensor_tensor(k.xn[:, c, :, :], k.xn[:, c, :, :], summed[c % 2][:, :, :], ALU.add).then_inc(step, 1)
                    n += 1
                    dve.wait_ge(step, n)
                    nc.vector.tensor_tensor(k.xn[:, c, :, :], k.xn[:, c, :, :],
                                            k.node_bias[:, c, :].unsqueeze(1).broadcast_to([P, B, O]), ALU.add).then_inc(step, 1)
                    n += 1



def product_transposed(nc, k, pe, src, out_bank, bp, half):
    n, NC = 0, k.NC
    for a, s in ((k.at_hi, 0), (k.at_lo, 0), (k.at_hi, 1)):
        for mc in range(NC):
            last = nc.tensor.matmul(out_bank, src[:, mc, s, 2 * bp:2 * bp + 2, :].rearrange("p b f -> p (b f)"),
                                    a[:, mc, half * 512:(half + 1) * 512], start=n == 0, stop=n == 3 * NC - 1)
            n += 1
    return last


def relu_diffusion(nc, k, net_params):
    NC, B, F, L = k.NC, k.B, k.F, 2
    BP, HV = B // 2, k.N // 512
    with ExitStack() as ctx:
        sb = lambda n, s, d=F32: ctx.enter_context(nc.sbuf_tensor(n, s, d))
        sem = k.sem
        w2 = sb("l1_w2", [P, L, P])
        aggT = sb("l1_aggT", [P, BP, k.N])
        zeroed, w_loaded = sem("l1_zeroed"), sem("l1_w_loaded")
        hi_ready, lo_ready, prod_ready, agg_ready, z_in_psum, z_read = (
            sem(n) for n in ("l1_hi_ready", "l1_lo_ready", "l1_prod_ready", "l1_agg_ready", "l1_z_in_psum", "l1_z_read"))
        z = k.split[0]
        prod = [k.bank_u[:, :], k.bank_m[:, :]]
        zb = [k.pair[:, 0:512], k.pair[:, 512:1024]]
        w_dram = net_params.rearrange("(l f g) -> f l g", l=L, f=F)
        with nc.Block() as block:
            @block.sync
            def _(sp):
                sp.wait_ge(zeroed, 1)
                for i in range(2):
                    sp.dma_start(w2[i * F:(i + 1) * F, :, i * F:(i + 1) * F], w_dram).then_inc(w_loaded, 16)

            @block.gpsimd
            def _(pool):
                nc.gpsimd.memset(w2[:, :, :], 0.0).then_inc(zeroed, 1)

            @block.tensor
            def _(pe):
                pe.wait_ge(w_loaded, 32)
                for l in range(L):
                    pe.wait_ge(lo_ready, 1 if l == 0 else 1 + NC)
                    for g in range(BP * HV):
                        t = l * BP * HV + g
                        if t >= 2:
                            pe.wait_ge(agg_ready, t - 1)
                        product_transposed(nc, k, pe, z, prod[t % 2], g // HV, g % HV).then_inc(prod_ready, 1)
                    pe.wait_ge(agg_ready, (l + 1) * BP * HV)
                    for c in range(NC):
                        t = l * NC + c
                        if t >= 2 and t < NC + 2:
                            pe.wait_ge(lo_ready, t)
                        elif t >= 2:
                            pe.wait_ge(z_read, t - NC - 1)
                        for bp in range(BP):
                            last = nc.tensor.matmul(zb[t % 2][:, bp * P:(bp + 1) * P], aggT[:, bp, c * P:(c + 1) * P], w2[:, l, :], start=True, stop=True)
                        last.then_inc(z_in_psum, 1)

            @block.scalar
            def _(act):
                nc.scalar.activation(z[:, :, 0, :, :].rearrange("p c b f -> p c (b f)"),
                                     k.xn[:, :, :, :].rearrange("p c b f -> p c (b f)"), ACT.Copy).then_inc(hi_ready, 1)
                for l in range(L):
                    for g in range(BP * HV):
                        t = l * BP * HV + g
                        act.wait_ge(prod_ready, t + 1)
                        nc.scalar.activation(aggT[:, g // HV, (g % HV) * 512:(g % HV + 1) * 512], prod[t % 2], ACT.Copy).then_inc(agg_ready, 1)
                    if l == 0:
                        for c in range(NC):
                            act.wait_ge(z_in_psum, c + 1)
                            nc.scalar.activation(z[:, c, 0, :, :], zb[c % 2].rearrange("p (b f) -> p b f", f=F), ACT.Relu).then_inc(hi_ready, 1)

            @block.vector
            def _(dve):
                dve.wait_ge(hi_ready, 1)
                nc.vector.tensor_tensor(z[:, :, 1, :, :].rearrange("p c b f -> p c (b f)"),
                                        k.xn[:, :, :, :].rearrange("p c b f -> p c (b f)"),
                                        f32(z[:, :, 0, :, :]).rearrange("p c b f -> p c (b f)"), ALU.subtract).then_inc(lo_ready, 1)
                for c in range(NC):
                    dve.wait_ge(hi_ready, 2 + c)
                    nc.vector.scalar_tensor_tensor(out=z[:, c, 1, :, :], in0=zb[c % 2].rearrange("p (b f) -> p b f", f=F), scalar=0.0,
                                                   in1=f32(z[:, c, 0, :, :]), op0=ALU.max, op1=ALU.subtract).then_inc(lo_ready, 1)
                for c in range(NC):
                    dve.wait_ge(z_in_psum, NC + c + 1)
                    nc.vector.scalar_tensor_tensor(out=k.xn[:, c, :, :], in0=zb[c % 2].rearrange("p (b f) -> p b f", f=F), scalar=0.0,
                                                   in1=k.xn[:, c, :, :], op0=ALU.max, op1=ALU.add).then_inc(z_read, 1)



OUT = "out"


def attention_slots(insts):
    slots = [(-1, "project", 0, h) for h in range(2) if insts[0] != OUT]
    for i in range(len(insts) + 1):
        for c in range(8):
            step, prev = 8 * i + c, (insts[i - 1] if i else None)
            if c == 0 and i:
                slots.append((step, "sums", i - 1, 1))
            if c in (1, 5) and i and prev != OUT:
                slots.append((step, "head", i - 1, c // 4))
            if c in (2, 6) and i:
                slots.append((step, "mix" if prev != OUT else "turn", i - 1, c // 4))
            if c in (3, 4) and i + 1 < len(insts) and insts[i + 1] != OUT:
                slots.append((step, "project", i + 1, c - 3))
            if c == 7 and i < len(insts):
                slots.append((step, "sums", i, 0))
    return slots


def attention_tensor(nc, k, a, pe, insts, b, at):
    slots = attention_slots(insts)
    order = [i for i in insts if i != OUT]
    NI, ST = len(insts), 8 * len(insts)

    def nth_head(i):
        return order.index(insts[i])

    def misc_bank_free(m):
        if m == 0:
            return
        _, kind, i, h = slots[m - 1]
        if kind == "project":
            pe.wait_ge(a.keys_ready, at("keys_ready", 2 * nth_head(i) + h + 1))
        elif kind == "sums":
            pe.wait_ge(a.inv_ready, at("inv_ready", 2 * i + h + 1))
        elif kind == "head":
            pe.wait_ge(a.biased_ready, at("biased_ready", 2 * i + h + 1))
        elif kind == "mix":
            pe.wait_ge(a.mixed, at("mixed", 2 * nth_head(i) + h + 1))
        else:
            pe.wait_ge(a.out_stored, at("out_stored", h + 1))

    def slot(step):
        for m, (st, kind, i, h) in enumerate(slots):
            if st != step:
                continue
            misc_bank_free(m)
            inst = insts[i]
            if kind == "project":
                if h == 0:
                    pe.wait_ge(a.xt_lo_ready, at("xt_lo_ready", 1))
                nc.tensor.matmul(k.bank_m[:, :], a.gram_hi[:, inst, :], a.xt[:, h * 512:(h + 1) * 512], start=True, stop=False)
                last = nc.tensor.matmul(k.bank_m[:, :], a.gram_lo[:, inst, :], a.xt[:, h * 512:(h + 1) * 512], start=False, stop=True)
            elif kind == "sums":
                pe.wait_ge(a.rinv_ready, at("rinv_ready", 2 * i + h + 1))
                for j in range(4):
                    col = 8 * (i % 2) + 4 * h + j
                    last = nc.tensor.matmul(k.bank_m[:, j * P:(j + 1) * P], a.rinv[:, col:col + 1].broadcast_to([P, P]),
                                            k.ident[:, :], start=True, stop=True)
            elif kind == "head":
                pe.wait_ge(a.ctx_ready, at("ctx_ready", 2 * i + h + 1))
                last = nc.tensor.matmul(k.bank_m[:, :], a.wh[:, inst, :], a.ctx[h][:, :], start=True, stop=True)
            elif kind == "mix":
                pe.wait_ge(a.leaky_ready, at("leaky_ready", 2 * i + h + 1))
                last = nc.tensor.matmul(k.bank_m[:, :], a.wo[:, inst, :, :].rearrange("p t o -> p (t o)"), a.leaky[:, :], start=True, stop=True)
            else:
                pe.wait_ge(a.leaky_ready, at("leaky_ready", 2 * i + h + 1))
                for j in range(4):
                    last = nc.tensor.transpose(k.bank_m[:, j * P:(j + 1) * P], a.leaky[:, j * P:(j + 1) * P], k.ident[:, :])
            last.then_inc(a.slot_done, 1)

    def scores(q):
        i, c = divmod(q, 8)
        out = insts[i] == OUT
        if q == 0 and insts[0] != OUT:
            pass
        elif q == 1 and insts[0] != OUT:
            pe.wait_ge(a.vo_ready, at("vo_ready", 1))
        elif q >= 2:
            pe.wait_ge(a.scaled, at("scaled", q - 1))
        if c == 0:
            if out:
                pe.wait_ge(a.ko_lo_ready, at("ko_lo_ready", 1))
                pe.wait_ge(a.xo_lo_ready, at("xo_lo_ready", 1))
            else:
                pe.wait_ge(a.keys_ready, at("keys_ready", 2 * nth_head(i) + 2))
        if out and insts[0] == OUT and q < 2:
            pe.wait_ge(a.vo_ready, at("vo_ready", 1))
        xt = a.xo if out else a.xt
        hi, lo = (a.ko_hi, a.ko_lo) if out else (a.keys_hi[nth_head(i) % 2], a.keys_lo[nth_head(i) % 2])
        for j in range(2):
            o = k.wide[q % 2][:, j * 512:(j + 1) * 512]
            nc.tensor.matmul(o, xt[:, c * P:(c + 1) * P], hi[:, j * 512:(j + 1) * 512], start=True, stop=False)
            last = nc.tensor.matmul(o, xt[:, c * P:(c + 1) * P], lo[:, j * 512:(j + 1) * 512], start=False, stop=True)
        last.then_inc(a.scores_ready, 1)

    def turn_probs(q):
        pe.wait_ge(a.probs_ready, at("probs_ready", q + 1))
        for j in range(2):
            if q >= 1:
                pe.wait_ge(a.turned_read, at("turned_read", 2 * (q - 1) + j + 1))
            for m in range(4):
                mc = 4 * j + m
                last = nc.tensor.transpose(k.pair[:, mc * P:(mc + 1) * P], a.probs[q % 2][:, mc * P:(mc + 1) * P], k.ident[:, :])
            last.then_inc(a.turned, 1)

    def values(i, g, piece):
        if piece == 0:
            pe.wait_ge(a.turned_read, at("turned_read", 2 * (8 * i + 4 * g + 4)))
            if 2 * i + g >= 1:
                pe.wait_ge(a.ctx_ready, at("ctx_ready", 2 * i + g))
        v = a.vo if insts[i] == OUT else a.v
        for mc in (2 * piece, 2 * piece + 1):
            last = nc.tensor.matmul(k.bank_u[0:k.F, :], v[:, mc, 0:k.F], a.probsT[g][:, mc, :], start=mc == 0, stop=mc == 7)
        if piece == 3:
            last.then_inc(a.values_done, 1)

    if insts[0] != OUT:
        pe.wait_ge(a.v_ready, at("v_ready", 1))
        for c in range(8):
            last = nc.tensor.transpose(k.wide[0][:, c * P:(c + 1) * P], a.v[:, c, :], k.ident[:, :])
        last.then_inc(a.xt_in_psum, 1)
    else:
        pe.wait_ge(a.mixed, at("mixed", 0))
    for c in range(8):
        last = nc.tensor.transpose(k.wide[1][:, c * P:(c + 1) * P], a.h2[:, c * P:(c + 1) * P], k.ident[:, :])
    last.then_inc(a.vo_in_psum, 1)
    slot(-1)
    scores(0)
    scores(1)
    for step in range(ST + 7):
        i, c = divmod(step, 8)
        if step + 2 < ST:
            scores(step + 2)
        slot(step)
        if step < ST:
            turn_probs(step)
        if c >= 4 and i < NI:
            values(i, 0, c - 4)
        elif c < 4 and i >= 1:
            values(i - 1, 1, c)


def attention_scalar(nc, k, a, act, insts, b, at):
    slots = attention_slots(insts)
    order = [i for i in insts if i != OUT]
    ST = 8 * len(insts)

    def exponentials(q):
        i, c = divmod(q, 8)
        act.wait_ge(a.shifted, at("shifted", q + 1))
        if q >= 2:
            act.wait_ge(a.turned, at("turned", 2 * (q - 2) + 2))
        col = 8 * (i % 2) + c
        nc.scalar.activation(a.probs[q % 2][:, :], a.neg_scores[q % 2][:, :], ACT.Exp, bias=a.neg_max[:, col:col + 1],
                             scale=-1.0, accum_out=a.sums[:, col:col + 1]).then_inc(a.probs_ready, 1)

    def read_turned(q):
        i, c = divmod(q, 8)
        g = c // 4
        if c % 4 == 0 and i >= 1:
            act.wait_ge(a.values_done, at("values_done", 2 * (i - 1) + g + 1))
        for j in range(2):
            act.wait_ge(a.turned, at("turned", 2 * q + j + 1))
            nc.scalar.activation(a.probsT[g][:, 4 * j:4 * j + 4, (c % 4) * P:(c % 4 + 1) * P],
                                 k.pair[:, j * 512:(j + 1) * 512].rearrange("p (m n) -> p m n", n=P), ACT.Copy).then_inc(a.turned_read, 1)

    def slot(step):
        for m, (st, kind, i, h) in enumerate(slots):
            if st != step:
                continue
            inst = insts[i]
            if kind == "project":
                act.wait_ge(a.slot_done, at("slot_done", m + 1))
                n = order.index(inst)
                nc.scalar.activation(a.keys_hi[n % 2][:, h * 512:(h + 1) * 512], k.bank_m[:, :], ACT.Copy).then_inc(a.keys_hi_ready, 1)
            elif kind == "sums":
                act.wait_ge(a.slot_done, at("slot_done", m + 1))
                nc.scalar.activation(a.inv[h][:, :], k.bank_m[0:k.F, :], ACT.Copy).then_inc(a.inv_ready, 1)
            elif kind == "head":
                act.wait_ge(a.slot_done, at("slot_done", m + 1))
                nc.scalar.activation(a.biased[:, :], k.bank_m[:, :], ACT.Identity, bias=a.bh[:, inst:inst + 1]).then_inc(a.biased_ready, 1)
        i, c = divmod(step, 8)
        if c in (1, 5) and i >= 1 and insts[i - 1] == OUT:
            h = c // 4
            act.wait_ge(a.ctx_ready, at("ctx_ready", 2 * (i - 1) + h + 1))
            nc.scalar.activation(a.biased[0:k.F, :], a.ctx[h][:, :], ACT.Identity, bias=a.b_out[:, 0:1]).then_inc(a.biased_ready, 1)

    if insts[0] != OUT:
        act.wait_ge(a.xt_in_psum, at("xt_in_psum", 1))
        nc.scalar.activation(a.xt[:, :], k.wide[0][:, :], ACT.Copy).then_inc(a.xt_hi_ready, 1)
    else:
        act.wait_ge(a.mixed, at("mixed", 0))
    nc.scalar.activation(a.ko_hi[:, :], a.h2[:, :], ACT.Copy).then_inc(a.ko_hi_ready, 1)
    act.wait_ge(a.vo_in_psum, at("vo_in_psum", 1))
    nc.scalar.activation(a.vo[:, :, :].rearrange("p c f -> p (c f)"), k.wide[1][:, :], ACT.Copy).then_inc(a.vo_ready, 1)
    slot(-1)
    exponentials(0)
    for step in range(ST + 7):
        slot(step)
        if step + 1 < ST:
            exponentials(step + 1)
        if step < ST:
            read_turned(step)


def attention_vector(nc, k, a, dve, insts, b, at):
    slots = attention_slots(insts)
    order = [i for i in insts if i != OUT]
    NI, ST = len(insts), 8 * len(insts)

    def shifted_scores(q):
        i, c = divmod(q, 8)
        dve.wait_ge(a.scores_ready, at("scores_ready", q + 1))
        nc.vector.tensor_tensor(a.scaled_scores[:, :], k.wide[q % 2][:, :], k.adj[:, c, :], ALU.mult).then_inc(a.scaled, 1)
        dve.wait_ge(a.scaled, at("scaled", q + 1))
        if q >= 2:
            dve.wait_ge(a.probs_ready, at("probs_ready", q - 1))
        nc.vector.tensor_scalar(a.fill[:, :], a.scaled_scores[:, :], 0.0, MASKED, ALU.is_equal, ALU.mult).then_inc(a.filled, 1)
        dve.wait_ge(a.filled, 1)
        dve.wait_ge(a.filled, at("filled", q + 1))
        col = 8 * (i % 2) + c
        nc.vector.tensor_tensor_reduce(out=a.neg_scores[q % 2][:, :], in0=a.scaled_scores[:, :], in1=a.fill[:, :], scale=-1.0,
                                       scalar=3.0e38, op0=ALU.add, op1=ALU.min, accum_out=a.neg_max[:, col:col + 1]).then_inc(a.shifted, 1)
        dve.wait_ge(a.shifted, at("shifted", q + 1))

    def rinv(i, g):
        dve.wait_ge(a.probs_ready, at("probs_ready", 8 * i + 4 * g + 4))
        col = 8 * (i % 2) + 4 * g
        nc.vector.reciprocal(a.rinv[:, col:col + 4], a.sums[:, col:col + 4]).then_inc(a.rinv_ready, 1)

    def context(i, g):
        dve.wait_ge(a.values_done, at("values_done", 2 * i + g + 1))
        dve.wait_ge(a.inv_ready, at("inv_ready", 2 * i + g + 1))
        nc.vector.tensor_tensor(a.ctx[g][:, :], k.bank_u[0:k.F, :], a.inv[g][:, :], ALU.mult).then_inc(a.ctx_ready, 1)

    def leaky(i, g):
        dve.wait_ge(a.biased_ready, at("biased_ready", 2 * i + g + 1))
        rows = k.F if insts[i] == OUT else P
        nc.vector.scalar_tensor_tensor(out=a.leaky[0:rows, :], in0=a.biased[0:rows, :], scalar=0.01, in1=a.biased[0:rows, :],
                                       op0=ALU.mult, op1=ALU.max).then_inc(a.leaky_ready, 1)

    def slot(step):
        i, c = divmod(step, 8)
        if c == 0 and i >= 1:
            context(i - 1, 0)
        if c == 4 and i >= 1:
            context(i - 1, 1)
        if c in (1, 5) and i >= 1:
            leaky(i - 1, c // 4)
        for m, (st, kind, j, h) in enumerate(slots):
            if st != step or kind in ("sums", "head"):
                continue
            inst = insts[j]
            if kind == "project":
                n = order.index(inst)
                dve.wait_ge(a.keys_hi_ready, at("keys_hi_ready", 2 * n + h + 1))
                nc.vector.tensor_tensor(a.keys_lo[n % 2][:, h * 512:(h + 1) * 512], k.bank_m[:, :],
                                        f32(a.keys_hi[n % 2][:, h * 512:(h + 1) * 512]), ALU.subtract).then_inc(a.keys_ready, 1)
            elif kind == "mix":
                dve.wait_ge(a.slot_done, at("slot_done", m + 1))
                acc = a.h2[:, h * 512:(h + 1) * 512]
                if inst == order[0]:
                    nc.vector.tensor_copy(acc, k.bank_m[:, :]).then_inc(a.mixed, 1)
                else:
                    nc.vector.tensor_tensor(acc, acc, k.bank_m[:, :], ALU.add).then_inc(a.mixed, 1)
                dve.wait_ge(a.mixed, at("mixed", 2 * order.index(inst) + h + 1))
            else:
                dve.wait_ge(a.slot_done, at("slot_done", m + 1))
                slot_b = bass.ds(b, 1) if not isinstance(b, int) else slice(b, b + 1)
                nc.vector.tensor_copy(a.delta[:, slot_b, 4 * h:4 * h + 4, :].rearrange("p b c f -> p (b c) f"),
                                      k.bank_m[:, :].rearrange("p (c f) -> p c f", f=P)[:, :, 0:k.F]).then_inc(a.out_stored, 1)
        if c == 5 and 0 <= i < NI:
            rinv(i, 0)
        if c == 7 and 0 <= i < NI:
            rinv(i, 1)

    if insts[0] != OUT:
        nc.vector.tensor_copy(a.v[:, :, :].rearrange("p c (t f) -> p c t f", t=2),
                              k.xn[:, :, bass.ds(b, 1), :].broadcast_to([P, k.NC, 2, k.F])).then_inc(a.v_ready, 1)
        dve.wait_ge(a.xt_hi_ready, at("xt_hi_ready", 1))
        nc.vector.tensor_tensor(a.xt[k.F:P, :], k.wide[0][k.F:P, :], f32(a.xt[k.F:P, :]), ALU.subtract).then_inc(a.xt_lo_ready, 1)
        slot(-1)
    dve.wait_ge(a.ko_hi_ready, at("ko_hi_ready", 1))
    nc.vector.tensor_copy(a.xo[0:k.F, :], f32(a.ko_hi[0:k.F, :])).then_inc(a.xo_hi_ready, 1)
    nc.vector.tensor_tensor(a.ko_lo[:, :], a.h2[:, :], f32(a.ko_hi[:, :]), ALU.subtract).then_inc(a.ko_lo_ready, 1)
    dve.wait_ge(a.ko_lo_ready, at("ko_lo_ready", 1))
    nc.vector.tensor_copy(a.xo[k.F:P, :], f32(a.ko_lo[k.F:P, :])).then_inc(a.xo_lo_ready, 1)
    shifted_scores(0)
    for step in range(ST + 7):
        if step + 1 < ST:
            shifted_scores(step + 1)
        slot(step)


def graph_attention(nc, k, adj, Wh, bh, W_out, b_out):
    NC, B, N, F, HEADS = k.NC, k.B, k.N, k.F, Wh.shape[0]
    with ExitStack() as ctx:
        def sb(n, s, d=F32):
            return ctx.enter_context(nc.sbuf_tensor("l2_" + n, s, d))

        def sem(n):
            return k.sem("l2_" + n)

        a = Ctx()
        a.gram_hi, a.gram_lo = sb("gram_hi", [P, HEADS, P], F32R), sb("gram_lo", [P, HEADS, P], F32R)
        a.wh, a.wo = sb("wh", [F, HEADS, P]), sb("wo", [P, HEADS, 2, F])
        a.bh, a.b_out = sb("bh", [P, HEADS]), sb("b_out", [F, 1])
        a.v, a.vo = sb("v", [P, NC, P]), sb("vo", [P, NC, P])
        a.xt, a.xo = sb("xt", [P, N], F32R), sb("xo", [P, N], F32R)
        a.keys_hi, a.keys_lo = ([sb(f"keys_{w}{i}", [P, N], F32R) for i in range(2)] for w in ("hi", "lo"))
        a.ko_hi, a.ko_lo = sb("ko_hi", [P, N], F32R), sb("ko_lo", [P, N], F32R)
        a.scaled_scores, a.fill = sb("scaled_scores", [P, N]), sb("fill", [P, N])
        a.neg_scores = [sb(f"neg_scores{i}", [P, N]) for i in range(2)]
        a.probs = [sb(f"probs{i}", [P, N]) for i in range(2)]
        a.probsT = [sb(f"probsT{i}", [P, NC, 512]) for i in range(2)]
        a.neg_max, a.sums, a.rinv = sb("neg_max", [P, 16]), sb("sums", [P, 16]), sb("rinv", [P, 16])
        a.inv = [sb(f"inv{i}", [F, 512]) for i in range(2)]
        a.ctx = [sb(f"ctx{i}", [F, 512]) for i in range(2)]
        a.biased, a.leaky, a.h2 = sb("biased", [P, 512]), sb("leaky", [P, 512]), sb("h2", [P, N])
        a.delta = k.delta
        whT = sb("whT", [P, HEADS, 2, F])

        insts = [0, OUT] + list(range(1, HEADS))
        ni, nh = len(insts), HEADS
        per = {"keys_ready": 2 * nh, "keys_hi_ready": 2 * nh, "inv_ready": 2 * ni, "biased_ready": 2 * ni, "mixed": 2 * nh,
               "out_stored": 2, "xt_lo_ready": 1, "xt_hi_ready": 1, "rinv_ready": 2 * ni, "ctx_ready": 2 * ni,
               "leaky_ready": 2 * ni, "vo_ready": 1, "scaled": 8 * ni, "ko_lo_ready": 1, "xo_lo_ready": 1,
               "probs_ready": 8 * ni, "turned_read": 16 * ni, "v_ready": 1, "turned": 16 * ni, "shifted": 8 * ni,
               "scores_ready": 8 * ni, "filled": 8 * ni, "values_done": 2 * ni, "slot_done": len(attention_slots(insts)),
               "xt_in_psum": 1, "vo_in_psum": 1, "ko_hi_ready": 1, "xo_hi_ready": 1}
        a.keys_ready, a.keys_hi_ready, a.inv_ready, a.biased_ready, a.mixed, a.out_stored = (
            sem(n) for n in ("keys_ready", "keys_hi_ready", "inv_ready", "biased_ready", "mixed", "out_stored"))
        a.xt_lo_ready, a.xt_hi_ready, a.rinv_ready, a.ctx_ready, a.leaky_ready, a.vo_ready = (
            sem(n) for n in ("xt_lo_ready", "xt_hi_ready", "rinv_ready", "ctx_ready", "leaky_ready", "vo_ready"))
        a.scaled, a.ko_lo_ready, a.xo_lo_ready, a.probs_ready, a.turned_read, a.v_ready = (
            sem(n) for n in ("scaled", "ko_lo_ready", "xo_lo_ready", "probs_ready", "turned_read", "v_ready"))
        a.turned, a.shifted, a.scores_ready, a.filled, a.values_done, a.slot_done = (
            sem(n) for n in ("turned", "shifted", "scores_ready", "filled", "values_done", "slot_done"))
        a.xt_in_psum, a.vo_in_psum, a.ko_hi_ready, a.xo_hi_ready = (
            sem(n) for n in ("xt_in_psum", "vo_in_psum", "ko_hi_ready", "xo_hi_ready"))
        adj_loaded, w_loaded, h2_zeroed, whT_in_psum, whT_ready, gram_in_psum, gram_hi_ready, gram_ready = (
            sem(n) for n in ("adj_loaded", "w_loaded", "h2_zeroed", "whT_in_psum", "whT_ready", "gram_in_psum", "gram_hi_ready", "gram_ready"))

        def counted(b):
            return lambda name, n: b * per[name] + n

        with nc.Block() as block:
            @block.sync
            def _(sp):
                sp.dma_start(a.wh[:, :, :], Wh.rearrange("h c d -> c h d")).then_inc(w_loaded, 16)
                for t in range(2):
                    sp.dma_start(a.wo[:, :, t, :], W_out.rearrange("(h d) o -> d h o", d=P)).then_inc(w_loaded, 16)
                sp.dma_start(a.bh[:, :], bh.rearrange("h d -> d h"), allow_slow_non_contiguous=True).then_inc(w_loaded, 16)
                sp.dma_start(a.b_out[:, :], b_out.rearrange("(o a) -> o a", a=1), allow_slow_non_contiguous=True).then_inc(w_loaded, 16)
                for c in range(NC):
                    sp.dma_start(k.adj[:, c, :], adj[c * P:(c + 1) * P, :]).then_inc(adj_loaded, 16)

            @block.tensor
            def _(pe):
                pe.wait_ge(w_loaded, 80)
                for h in range(HEADS):
                    last = nc.tensor.transpose(k.bank_u[:, h * F:(h + 1) * F], a.wh[:, h, :], k.ident[0:F, 0:F])
                last.then_inc(whT_in_psum, 1)
                pe.wait_ge(whT_ready, 2)
                for h in range(HEADS):
                    w = whT[:, h, :, :].rearrange("p t c -> p (t c)")
                    last = nc.tensor.matmul(k.wide[0][:, h * P:(h + 1) * P], w, w, start=True, stop=True)
                last.then_inc(gram_in_psum, 1)

            @block.scalar
            def _(act):
                act.wait_ge(whT_in_psum, 1)
                for t in range(2):
                    nc.scalar.activation(whT[:, :, t, :], k.bank_u[:, :].rearrange("p (h c) -> p h c", c=F), ACT.Copy).then_inc(whT_ready, 1)
                act.wait_ge(gram_in_psum, 1)
                nc.scalar.activation(a.gram_hi[:, :, :].rearrange("p h c -> p (h c)"), k.wide[0][:, :], ACT.Copy).then_inc(gram_hi_ready, 1)
                nc.scalar.preload_act_table(ACT.Exp)

            @block.vector
            def _(dve):
                nc.vector.memset(a.h2[:, :], 0.0).then_inc(h2_zeroed, 1)
                dve.wait_ge(gram_hi_ready, 1)
                nc.vector.tensor_tensor(a.gram_lo[:, :, :].rearrange("p h c -> p (h c)"), k.wide[0][:, :],
                                        f32(a.gram_hi[:, :, :]).rearrange("p h c -> p (h c)"), ALU.subtract).then_inc(gram_ready, 1)
                dve.wait_ge(adj_loaded, 16 * NC)

        with nc.Block() as block:
            @block.tensor
            def _(pe):
                with pe.Fori(0, B) as b:
                    attention_tensor(nc, k, a, pe, insts, b, counted(b))
                attention_tensor(nc, k, a, pe, [OUT], B, counted(B))

            @block.scalar
            def _(act):
                with act.Fori(0, B) as b:
                    attention_scalar(nc, k, a, act, insts, b, counted(b))
                attention_scalar(nc, k, a, act, [OUT], B, counted(B))

            @block.vector
            def _(dve):
                with dve.Fori(0, B) as b:
                    attention_vector(nc, k, a, dve, insts, b, counted(b))
                attention_vector(nc, k, a, dve, [OUT], B, counted(B))



def industry_messages(nc, k, W_ind, ind_dram):
    NC, B, F, N = k.NC, k.B, k.F, k.N
    BP, HV = B // 2, N // 512
    with ExitStack() as ctx:
        sb = lambda n, s, d=F32: ctx.enter_context(nc.sbuf_tensor("ind_" + n, s, d))
        sem = lambda n: k.sem("ind_" + n)
        k.at_hi, k.at_lo = sb("at_hi", [P, NC, N], F32R), sb("at_lo", [P, NC, N], F32R)
        z = sb("split", [P, NC, 2, B, F], F32R)
        w2, rdeg = sb("w2", [P, P]), sb("rdeg", [P, NC])
        agg = [sb(f"agg{i}", [P, 512]) for i in range(2)]
        ind = [sb(f"ind{i}", [P, 512]) for i in range(2)]
        rdeg_rows = sb("rdeg_rows", [P, N])
        zeroed, w_loaded, transposed, hi_ready, lo_ready, z_hi, z_lo, rdeg_ready, rdeg_in_psum, rdeg_rows_ready = (
            sem(n) for n in ("zeroed", "w_loaded", "transposed", "hi_ready", "lo_ready", "z_hi", "z_lo", "rdeg_ready", "rdeg_in_psum", "rdeg_rows_ready"))
        prod_ready, agg_ready, ind_in_psum, ind_ready = (sem(n) for n in ("prod_ready", "agg_ready", "ind_in_psum", "ind_ready"))
        stored = [sem(f"stored{i}") for i in range(2)]
        prod = [k.bank_u[:, :], k.bank_m[:, :]]
        indp = [k.pair[:, 0:512], k.pair[:, 512:1024]]
        with nc.Block() as block:
            @block.sync
            def _(sp):
                sp.wait_ge(zeroed, 1)
                for i in range(2):
                    sp.dma_start(w2[i * F:(i + 1) * F, i * F:(i + 1) * F], W_ind).then_inc(w_loaded, 16)
                for g in range(BP * HV):
                    bp, half = g // HV, g % HV
                    sp.wait_ge(ind_ready, g + 1)
                    sp.dma_start(ind_dram[2 * bp:2 * bp + 2, :, half * 512:(half + 1) * 512].rearrange("b f n -> (b f) n"),
                                 ind[g % 2][:, :]).then_inc(stored[g % 2], 16)
                for i in range(2):
                    sp.wait_ge(stored[i], 16 * BP * HV // 2)

            @block.gpsimd
            def _(pool):
                nc.gpsimd.memset(w2[:, :], 0.0).then_inc(zeroed, 1)

            @block.tensor
            def _(pe):
                for mc in range(NC):
                    if mc >= 2:
                        pe.wait_ge(lo_ready, mc - 1)
                    for c in range(NC):
                        last = nc.tensor.transpose(k.wide[mc % 2][:, c * P:(c + 1) * P], k.adj[:, c, mc * P:(mc + 1) * P], k.ident[:, :])
                    last.then_inc(transposed, 1)
                pe.wait_ge(rdeg_ready, 2)
                for c in range(NC):
                    last = nc.tensor.matmul(k.pair[:, c * P:(c + 1) * P], rdeg[:, c:c + 1].broadcast_to([P, P]), k.ident[:, :], start=True, stop=True)
                last.then_inc(rdeg_in_psum, 1)
                pe.wait_ge(w_loaded, 32)
                pe.wait_ge(lo_ready, NC)
                pe.wait_ge(z_lo, 1)
                pe.wait_ge(rdeg_rows_ready, 1)

                def message(g):
                    pe.wait_ge(agg_ready, g + 1)
                    if g >= 2:
                        pe.wait_ge(ind_ready, g - 1)
                    nc.tensor.matmul(indp[g % 2], w2[:, :], agg[g % 2][:, :], start=True, stop=True).then_inc(ind_in_psum, 1)

                for g in range(BP * HV):
                    if g >= 2:
                        pe.wait_ge(agg_ready, g - 1)
                    product_transposed(nc, k, pe, z, prod[g % 2], g // HV, g % HV).then_inc(prod_ready, 1)
                    if g >= 1:
                        message(g - 1)
                message(BP * HV - 1)

            @block.scalar
            def _(act):
                nc.scalar.activation(z[:, :, 0, :, :].rearrange("p c b f -> p c (b f)"),
                                     k.xn[:, :, :, :].rearrange("p c b f -> p c (b f)"), ACT.Copy).then_inc(z_hi, 1)
                for mc in range(NC):
                    act.wait_ge(transposed, mc + 1)
                    nc.scalar.activation(k.at_hi[:, mc, :], k.wide[mc % 2][:, :], ACT.Copy).then_inc(hi_ready, 1)
                act.wait_ge(rdeg_in_psum, 1)
                nc.scalar.activation(rdeg_rows[:, :], k.pair[:, :], ACT.Copy).then_inc(rdeg_rows_ready, 1)
                for g in range(BP * HV):
                    act.wait_ge(prod_ready, g + 1)
                    if g >= 2:
                        act.wait_ge(ind_in_psum, g - 1)
                    nc.scalar.activation(agg[g % 2][:, :], prod[g % 2], ACT.Copy).then_inc(agg_ready, 1)

            @block.vector
            def _(dve):
                nc.vector.tensor_scalar(rdeg[:, :], k.deg[:, :], 1.0, None, ALU.max).then_inc(rdeg_ready, 1)
                dve.wait_ge(rdeg_ready, 1)
                nc.vector.reciprocal(rdeg[:, :], rdeg[:, :]).then_inc(rdeg_ready, 1)
                dve.wait_ge(z_hi, 1)
                nc.vector.tensor_tensor(z[:, :, 1, :, :].rearrange("p c b f -> p c (b f)"),
                                        k.xn[:, :, :, :].rearrange("p c b f -> p c (b f)"),
                                        f32(z[:, :, 0, :, :]).rearrange("p c b f -> p c (b f)"), ALU.subtract).then_inc(z_lo, 1)
                for mc in range(NC):
                    dve.wait_ge(hi_ready, mc + 1)
                    nc.vector.tensor_tensor(k.at_lo[:, mc, :], k.wide[mc % 2][:, :], f32(k.at_hi[:, mc, :]), ALU.subtract).then_inc(lo_ready, 1)
                for g in range(BP * HV):
                    dve.wait_ge(ind_in_psum, g + 1)
                    if g >= 2:
                        dve.wait_ge(stored[g % 2], 16 * (g // 2))
                    half = g % HV
                    nc.vector.tensor_tensor(ind[g % 2][:, :], indp[g % 2], rdeg_rows[:, half * 512:(half + 1) * 512], ALU.mult).then_inc(ind_ready, 1)


def hypergraph_attention(nc, k, params, ind_dram):
    H, W, a_node, a_gn, a_ge, fcW, fcb, av = params
    NC, B, F, N, E = k.NC, k.B, k.F, k.N, H.shape[1]
    EP = E // 2
    HS = [slice(0, 512), slice(512, 1024)]
    with ExitStack() as ctx:
        sb = lambda n, s, d=F32: ctx.enter_context(nc.sbuf_tensor("l3_" + n, s, d))
        sem = lambda n: k.sem("l3_" + n)
        w_dup, fcw = sb("w_dup", [F, 2, F]), sb("fcw", [F, P])
        cols = sb("cols", [P, 8])
        h_raw = sb("h_raw", [P, NC, E])
        mask, fill = sb("mask", [P, NC, 2, E]), sb("fill", [P, NC, E])
        maskT, fillT = sb("maskT", [P, N]), sb("fillT", [P, N])
        pick, fold, ones = sb("pick", [P, EP, 2, F], F32R), sb("fold", [P, 2, F]), sb("ones", [F, P])
        dup_ident = sb("dup_ident", [P, E])
        x2, xT, hT, hn = sb("x2", [P, NC, P]), sb("xT", [P, N]), sb("hT", [P, N]), sb("hn", [P, NC, P])
        t0, t1, t2 = sb("t0", [P, N]), sb("t1", [P, N]), sb("t2", [P, N])
        alphaT = sb("alphaT", [P, NC, P])
        small = sb("small", [P, 16])
        aggT, agg_e, nagg_e = sb("aggT", [P, 2, E]), sb("agg_e", [P, EP]), sb("nagg_e", [P, EP])
        agg_less_1, neg_agg = sb("agg_less_1", [P, P]), sb("neg_agg", [P, P])
        agg_min, he, tanh_e = sb("agg_min", [P, E]), sb("he", [P, E]), sb("tanh_e", [P, E])
        beta, beta_s = sb("beta", [P, N]), sb("beta_s", [P, N], F32R)
        lg, coef = sb("lg", [P, NC, E]), sb("coef", [P, NC, 2, E])
        c8 = sb("c8", [P, 3, NC])
        cT, c_s, cbeta, hsum = sb("cT", [P, N]), sb("c_s", [P, N], F32R), sb("cbeta", [P, N]), sb("hsum", [P, N])
        w_t, r_t, e_t = ([sb(f"{n}_{i}", [P, N]) for i in range(3)] for n in ("w", "r", "e"))
        u_t, p_t = ([sb(f"{n}_{i}", [P, N]) for i in range(2)] for n in ("u", "p"))
        LEAD = 3
        fetches = [("beta", e) for e in range(LEAD)]
        for e in range(EP):
            fetches += [("beta", e + LEAD)] * (e + LEAD < EP) + [("c", e)]
        rows_of = {fetch: k.wide[f % 2] for f, fetch in enumerate(fetches)}
        ind = sb("ind", [P, N])
        g, tanh_i, tanh_g = sb("g", [P, N]), w_t[0], w_t[1]

        s = Ctx()
        s.loaded, s.consts, s.maskT_in_psum, s.x_ready, s.xT_in_psum, s.xT_ready = (
            sem(n) for n in ("loaded", "consts", "maskT_in_psum", "x_ready", "xT_in_psum", "xT_ready"))
        s.hT_in_psum, s.hn_in_psum, s.hT_ready, s.hn_ready, s.node_logits, s.gate_logits = (
            sem(n) for n in ("hT_in_psum", "hn_in_psum", "hT_ready", "hn_ready", "node_logits", "gate_logits"))
        s.logits_copied, s.alpha_step, s.alpha_shifted, s.alpha_exp, s.alpha_ready, s.alphaT_in_psum = (
            sem(n) for n in ("logits_copied", "alpha_step", "alpha_shifted", "alpha_exp", "alpha_ready", "alphaT_in_psum"))
        s.alphaT_ready, s.agg_in_psum, s.agg_step, s.agg_exp, s.he_ready, s.edge_in_psum = (
            sem(n) for n in ("alphaT_ready", "agg_in_psum", "agg_step", "agg_exp", "he_ready", "edge_in_psum"))
        s.tanh_e_ready, s.half_age_ready, s.score_in_psum, s.gate_tanh, s.beta_ready, s.beta_hi = (
            sem(n) for n in ("tanh_e_ready", "half_age_ready", "score_in_psum", "gate_tanh", "beta_ready", "beta_hi"))
        s.beta_split, s.coef_step, s.coef_exp, s.coef_ready, s.cT_in_psum, s.cT_ready = (
            sem(n) for n in ("beta_split", "coef_step", "coef_exp", "coef_ready", "cT_in_psum", "cT_ready"))
        s.c_split, s.cbeta_ready, s.hsum_in_psum, s.hsum_ready, s.beta_rows, s.c_rows = (
            sem(n) for n in ("c_split", "cbeta_ready", "hsum_in_psum", "hsum_ready", "beta_rows", "c_rows"))
        s.w_done, s.r_done, s.e_done, s.u_done, s.p_done, s.summed = (
            sem(n) for n in ("w_done", "r_done", "e_done", "u_done", "p_done", "summed"))
        s.g_ready, s.ind_loaded, s.tanh_in_psum, s.tanh_ready, s.mix_in_psum, s.mix_tanh = (
            sem(n) for n in ("g_ready", "ind_loaded", "tanh_in_psum", "tanh_ready", "mix_in_psum", "mix_tanh"))
        s.mix_step, s.outT_ready, s.out_in_psum, s.out_stored, s.coef_masked, s.coef_rinv = (
            sem(n) for n in ("mix_step", "outT_ready", "out_in_psum", "out_stored", "coef_masked", "coef_rinv"))
        s.coef_half = sem("coef_half")

        with nc.Block() as block:
            @block.sync
            def _(sp):
                for i in range(2):
                    sp.dma_start(w_dup[:, i, :], W).then_inc(s.loaded, 16)
                sp.dma_start(fcw[:, :], fcW).then_inc(s.loaded, 16)
                for i, v in enumerate((a_node, a_gn, a_ge, fcb, av)):
                    sp.dma_start(cols[0:v.shape[0], i:i + 1], v.rearrange("(f a) -> f a", a=1), allow_slow_non_contiguous=True).then_inc(s.loaded, 16)
                sp.dma_start(h_raw[:, :, :], H.rearrange("(c p) e -> p c e", p=P)).then_inc(s.loaded, 16)

            @block.vector
            def _(dve):
                dve.wait_ge(s.loaded, 16 * 9)
                nc.vector.tensor_scalar(cols[:, 5:6], cols[:, 4:5], -1.0, None, ALU.mult).then_inc(s.consts, 1)
                for i in range(2):
                    nc.vector.tensor_scalar(mask[:, :, i, :], h_raw[:, :, :], 0.0, None, ALU.is_gt).then_inc(s.consts, 1)
                nc.vector.memset(ones[:, :], 1.0).then_inc(s.consts, 1)
                nc.vector.tensor_tensor(dup_ident[:, :], k.ident[:, 0:E], k.ident[:, E:2 * E], ALU.add).then_inc(s.consts, 1)
                dve.wait_ge(s.consts, 5)
                nc.vector.tensor_scalar(fill[:, :, :], mask[:, :, 0, :], -1.0, -NEG, ALU.add, ALU.mult).then_inc(s.consts, 1)
                for i in range(2):
                    nc.vector.tensor_copy(fold[:, i, :], dup_ident[:, :]).then_inc(s.consts, 1)
                nc.vector.tensor_copy(pick[:, :, :, :], dup_ident[:, :].rearrange("p (j e) -> p e j", j=2).unsqueeze(3).broadcast_to([P, EP, 2, F])).then_inc(s.consts, 1)
                dve.wait_ge(s.maskT_in_psum, 1)
                nc.vector.tensor_copy(maskT[:, :], k.wide[0][:, :]).then_inc(s.consts, 1)
                dve.wait_ge(s.consts, 10)
                nc.vector.tensor_scalar(fillT[:, :], maskT[:, :], -1.0, -NEG, ALU.add, ALU.mult).then_inc(s.consts, 1)

            @block.tensor
            def _(pe):
                pe.wait_ge(s.consts, 5)
                for c in range(NC):
                    last = nc.tensor.transpose(k.wide[0][:, c * P:(c + 1) * P], mask[:, c, :, :].rearrange("p t e -> p (t e)"), k.ident[:, :])
                last.then_inc(s.maskT_in_psum, 1)

            @block.scalar
            def _(act):
                nc.scalar.preload_act_table(ACT.Exp)

        with nc.Block() as block:
            @block.sync
            def _(sp):
                with sp.Fori(0, B) as b:
                    sp.wait_ge(s.x_ready, b + 1)
                    for i in range(2):
                        sp.dma_start(ind[i * F:(i + 1) * F, :], ind_dram[bass.ds(b, 1), :, :].rearrange("b f n -> (b f) n")).then_inc(s.ind_loaded, 16)

            @block.tensor
            def _(pe):
                with pe.Fori(0, B) as b:
                    pe.wait_ge(s.x_ready, b + 1)
                    for c in range(NC):
                        last = nc.tensor.transpose(k.wide[0][:, c * P:(c + 1) * P], x2[:, c, :], k.ident[:, :])
                    last.then_inc(s.xT_in_psum, 1)
                    pe.wait_ge(s.xT_ready, b + 1)
                    w_flat = w_dup[:, :, :].rearrange("p t f -> p (t f)")
                    for hs in HS:
                        last = nc.tensor.matmul(k.wide[1][:, hs], w_flat, xT[0:F, hs], start=True, stop=True)
                    last.then_inc(s.hT_in_psum, 1)
                    for c in range(NC):
                        last = nc.tensor.matmul(k.wide[0][:, c * P:(c + 1) * P], xT[0:F, c * P:(c + 1) * P], w_flat, start=True, stop=True)
                    last.then_inc(s.hn_in_psum, 1)
                    pe.wait_ge(s.hT_ready, b + 1)
                    for hs in HS:
                        last = nc.tensor.matmul(k.wide[1][:, hs], cols[0:F, 0:1].broadcast_to([F, P]), hT[0:F, hs], start=True, stop=True)
                    last.then_inc(s.node_logits, 1)
                    for i, hs in enumerate(HS):
                        last = nc.tensor.matmul((k.bank_u, k.bank_m)[i][:, :], cols[0:F, 1:2].broadcast_to([F, P]), hT[0:F, hs], start=True, stop=True)
                    last.then_inc(s.gate_logits, 1)
                    pe.wait_ge(s.alpha_ready, b + 1)
                    for c in range(NC):
                        last = nc.tensor.transpose(k.wide[1][:, c * P:(c + 1) * P], t2[:, c * P:(c + 1) * P], k.ident[:, :])
                    last.then_inc(s.alphaT_in_psum, 1)
                    pe.wait_ge(s.hn_ready, b + 1)
                    pe.wait_ge(s.alphaT_ready, b + 1)
                    for c in range(NC):
                        nc.tensor.matmul(k.wide[0][:, 0:E], hn[:, c, :], alphaT[:, c, 0:E], start=c == 0, stop=c == NC - 1)
                    for c in range(NC):
                        last = nc.tensor.matmul(k.wide[0][:, 512:512 + P], alphaT[:, c, :], hn[:, c, :], start=c == 0, stop=c == NC - 1)
                    last.then_inc(s.agg_in_psum, 1)
                    pe.wait_ge(s.he_ready, b + 1)
                    nc.tensor.matmul(k.wide[0][:, 0:E], fcw[:, :], he[0:F, :], start=True, stop=True)
                    nc.tensor.matmul(k.wide[0][:, 512:513], aggT[0:F, :, :].rearrange("p t e -> p (t e)"), cols[0:F, 2:3], start=True, stop=True).then_inc(s.edge_in_psum, 1)
                    pe.wait_ge(s.tanh_e_ready, b + 1)
                    nc.tensor.matmul(k.wide[0][:, 0:E], cols[:, 4:5].broadcast_to([P, P]), tanh_e[:, :], start=True, stop=True).then_inc(s.score_in_psum, 1)
                    pe.wait_ge(s.coef_ready, b + 1)
                    for c in range(NC):
                        last = nc.tensor.transpose(k.wide[1][:, c * P:(c + 1) * P], coef[:, c, :, :].rearrange("p t e -> p (t e)"), k.ident[:, :])
                    last.then_inc(s.cT_in_psum, 1)
                    pe.wait_ge(s.cbeta_ready, b + 1)
                    for i, hs in enumerate(HS):
                        nc.tensor.matmul(k.pair[:, hs], agg_less_1[0:E, :], cT[0:E, hs], start=True, stop=False)
                        nc.tensor.matmul(k.pair[:, hs], neg_agg[0:E, :], cbeta[0:E, hs], start=False, stop=False)
                        last = nc.tensor.matmul((k.bank_u, k.bank_m)[i][:, :], ones[:, :], cbeta[0:E, hs], start=True, stop=True)
                    last.then_inc(s.hsum_in_psum, 1)

                    def spread(f):
                        kind, e = fetches[f]
                        if f >= 2:
                            before, e2 = fetches[f - 2]
                            if before == "beta":
                                pe.wait_ge(s.w_done, b * EP + e2 + 1)
                            else:
                                pe.wait_ge(s.p_done, b * EP + e2 + 1)
                        src = beta_s if kind == "beta" else c_s
                        for hs in HS:
                            last = nc.tensor.matmul(rows_of[kind, e][:, hs], pick[:, e, :, :].rearrange("p j f -> p (j f)"), src[:, hs], start=True, stop=True)
                        last.then_inc(s.beta_rows if kind == "beta" else s.c_rows, 1)

                    def add_up(e, half):
                        if half == 0:
                            pe.wait_ge(s.p_done, b * EP + e + 1)
                        last = nc.tensor.matmul(k.pair[:, HS[half]], fold[:, :, :].rearrange("p t f -> p (t f)"), p_t[e % 2][:, HS[half]], start=False, stop=e == EP - 1)
                        if half == 1:
                            last.then_inc(s.summed, 1)

                    pe.wait_ge(s.beta_split, b + 1)
                    pe.wait_ge(s.c_split, b + 1)
                    for f in range(LEAD + 1):
                        spread(f)
                    for e in range(EP):
                        spread(fetches.index(("c", e)))
                        if e >= 1:
                            add_up(e - 1, 0)
                        if e + LEAD + 1 < EP:
                            spread(fetches.index(("beta", e + LEAD + 1)))
                        if e >= 1:
                            add_up(e - 1, 1)
                    for half in range(2):
                        add_up(EP - 1, half)
                    pe.wait_ge(s.g_ready, b + 1)
                    pe.wait_ge(s.ind_loaded, b * 32 + 32)
                    for hs in HS:
                        last = nc.tensor.matmul(k.wide[0][:, hs], fcw[:, :], ind[0:F, hs], start=True, stop=True)
                    for hs in HS:
                        last = nc.tensor.matmul(k.wide[1][:, hs], fcw[:, :], g[0:F, hs], start=True, stop=True)
                    last.then_inc(s.tanh_in_psum, 1)
                    pe.wait_ge(s.tanh_ready, b * 2 + 2)
                    for hs in HS:
                        nc.tensor.matmul(k.pair[:, hs], cols[:, 4:5].broadcast_to([P, P]), tanh_g[:, hs], start=True, stop=False)
                        last = nc.tensor.matmul(k.pair[:, hs], cols[:, 5:6].broadcast_to([P, P]), tanh_i[:, hs], start=False, stop=True)
                    last.then_inc(s.mix_in_psum, 1)
                    pe.wait_ge(s.outT_ready, b + 1)
                    for c in range(NC):
                        last = nc.tensor.transpose(k.wide[0][:, c * P:(c + 1) * P], t1[:, c * P:(c + 1) * P], k.ident[:, :])
                    last.then_inc(s.out_in_psum, 1)

            @block.scalar
            def _(act):
                with act.Fori(0, B) as b:
                    act.wait_ge(s.xT_in_psum, b + 1)
                    nc.scalar.activation(xT[:, :], k.wide[0][:, :], ACT.Copy).then_inc(s.xT_ready, 1)
                    act.wait_ge(s.hT_in_psum, b + 1)
                    nc.scalar.activation(hT[:, :], k.wide[1][:, :], ACT.Copy).then_inc(s.hT_ready, 1)
                    act.wait_ge(s.node_logits, b + 1)
                    nc.scalar.activation(t0[:, :], k.wide[1][:, :], ACT.Copy).then_inc(s.logits_copied, 1)
                    act.wait_ge(s.alpha_shifted, b + 1)
                    nc.scalar.activation(t1[:, :], t0[:, :], ACT.Exp, bias=small[:, 0:1], scale=-1.0, accum_out=small[:, 1:2]).then_inc(s.alpha_exp, 1)
                    act.wait_ge(s.alphaT_in_psum, b + 1)
                    nc.scalar.activation(alphaT[:, :, :].rearrange("p c e -> p (c e)"), k.wide[1][:, :], ACT.Copy).then_inc(s.alphaT_ready, 1)
                    act.wait_ge(s.agg_step, b * 7 + 7)
                    nc.scalar.activation(agg_min[:, :], agg_min[:, :], ACT.Exp).then_inc(s.agg_exp, 1)
                    act.wait_ge(s.edge_in_psum, b + 1)
                    nc.scalar.activation(tanh_e[:, :], k.wide[0][:, 0:E], ACT.Tanh, bias=cols[:, 3:4]).then_inc(s.tanh_e_ready, 1)
                    act.wait_ge(s.half_age_ready, b + 1)
                    act.wait_ge(s.gate_logits, b + 1)
                    for i, hs in enumerate(HS):
                        nc.scalar.activation(beta[:, hs], (k.bank_u, k.bank_m)[i][:, :], ACT.Tanh, bias=small[:, 3:4], scale=0.5).then_inc(s.gate_tanh, 1)
                    act.wait_ge(s.coef_step, b * 4 + 4)
                    nc.scalar.activation(lg[:, :, :], lg[:, :, :], ACT.Exp).then_inc(s.coef_exp, 1)
                    act.wait_ge(s.beta_ready, b + 1)
                    nc.scalar.activation(beta_s[:, :], beta[:, :], ACT.Copy).then_inc(s.beta_hi, 1)
                    act.wait_ge(s.cT_in_psum, b + 1)
                    nc.scalar.activation(c_s[:, :], k.wide[1][:, :], ACT.Copy).then_inc(s.cT_ready, 1)
                    nc.scalar.activation(cT[:, :], k.wide[1][:, :], ACT.Copy).then_inc(s.cT_ready, 1)
                    for e in range(EP):
                        act.wait_ge(s.w_done, b * EP + e + 1)
                        if e >= 3:
                            act.wait_ge(s.u_done, b * EP + e - 2)
                        nc.scalar.activation(r_t[e % 3][:, :], w_t[e % 3][:, :], ACT.Relu, bias=nagg_e[:, e:e + 1], scale=-1.0).then_inc(s.r_done, 1)
                        act.wait_ge(s.r_done, b * EP + e + 1)
                        nc.scalar.activation(e_t[e % 3][:, :], r_t[e % 3][:, :], ACT.Exp, scale=-1.0).then_inc(s.e_done, 1)
                    act.wait_ge(s.tanh_in_psum, b + 1)
                    nc.scalar.activation(tanh_i[:, :], k.wide[0][:, :], ACT.Tanh, bias=cols[:, 3:4]).then_inc(s.tanh_ready, 1)
                    nc.scalar.activation(tanh_g[:, :], k.wide[1][:, :], ACT.Tanh, bias=cols[:, 3:4]).then_inc(s.tanh_ready, 1)
                    act.wait_ge(s.mix_in_psum, b + 1)
                    nc.scalar.activation(t0[:, :], k.pair[:, :], ACT.Tanh, scale=0.5).then_inc(s.mix_tanh, 1)

            @block.gpsimd
            def _(pool):
                with pool.Fori(0, B) as b:
                    for e in range(EP):
                        pool.wait_ge(s.e_done, b * EP + e + 1)
                        if e >= 2:
                            pool.wait_ge(s.p_done, b * EP + e - 1)
                        nc.gpsimd.tensor_tensor(u_t[e % 2][:, :], r_t[e % 3][:, :], e_t[e % 3][:, :], ALU.add).then_inc(s.u_done, 1)

            @block.vector
            def _(dve):
                with dve.Fori(0, B) as b:
                    nc.vector.tensor_copy(x2[:, :, :].rearrange("p c (t f) -> p c t f", t=2),
                                          k.xn[:, :, bass.ds(b, 1), :].broadcast_to([P, NC, 2, F])).then_inc(s.x_ready, 1)
                    dve.wait_ge(s.logits_copied, b + 1)
                    nc.vector.scalar_tensor_tensor(out=t1[:, :], in0=t0[:, :], scalar=0.2, in1=t0[:, :], op0=ALU.mult, op1=ALU.max).then_inc(s.alpha_step, 1)
                    dve.wait_ge(s.alpha_step, b * 3 + 1)
                    nc.vector.tensor_tensor(t2[:, :], t1[:, :], maskT[:, :], ALU.mult).then_inc(s.alpha_step, 1)
                    dve.wait_ge(s.alpha_step, b * 3 + 2)
                    dve.wait_ge(s.hn_in_psum, b + 1)
                    nc.vector.tensor_copy(hn[:, :, :].rearrange("p c f -> p (c f)"), k.wide[0][:, :]).then_inc(s.hn_ready, 1)
                    nc.vector.tensor_tensor_reduce(out=t0[:, :], in0=t2[:, :], in1=fillT[:, :], scale=-1.0, scalar=3.0e38,
                                                   op0=ALU.add, op1=ALU.min, accum_out=small[:, 0:1]).then_inc(s.alpha_shifted, 1)
                    dve.wait_ge(s.alpha_exp, b + 1)
                    nc.vector.reciprocal(small[:, 2:3], small[:, 1:2]).then_inc(s.alpha_step, 1)
                    dve.wait_ge(s.alpha_step, b * 3 + 3)
                    nc.vector.tensor_scalar(t2[:, :], t1[:, :], small[:, 2:3], None, ALU.mult).then_inc(s.alpha_ready, 1)
                    dve.wait_ge(s.agg_in_psum, b + 1)
                    for i in range(2):
                        nc.vector.tensor_copy(aggT[:, i, :], k.wide[0][:, 0:E]).then_inc(s.agg_step, 1)
                    nc.vector.tensor_scalar(agg_less_1[:, :], k.wide[0][:, 512:512 + P], -1.0, None, ALU.add).then_inc(s.agg_step, 1)
                    nc.vector.tensor_scalar(neg_agg[:, :], k.wide[0][:, 512:512 + P], -1.0, None, ALU.mult).then_inc(s.agg_step, 1)
                    for i in range(2):
                        nc.vector.tensor_copy(agg_e[i * F:(i + 1) * F, :], k.wide[0][i * F:(i + 1) * F, i * EP:(i + 1) * EP]).then_inc(s.agg_step, 1)
                    nc.vector.tensor_scalar(agg_min[:, :], k.wide[0][:, 0:E], 0.0, None, ALU.min).then_inc(s.agg_step, 1)
                    dve.wait_ge(s.agg_exp, b + 1)
                    nc.vector.scalar_tensor_tensor(out=he[:, :], in0=aggT[:, 0, :], scalar=0.0, in1=agg_min[:, :], op0=ALU.max, op1=ALU.add).then_inc(s.coef_step, 1)
                    nc.vector.tensor_scalar(nagg_e[:, :], agg_e[:, :], -1.0, None, ALU.mult).then_inc(s.coef_step, 1)
                    dve.wait_ge(s.coef_step, b * 4 + 1)
                    nc.vector.tensor_scalar(he[:, :], he[:, :], -1.0, None, ALU.add).then_inc(s.he_ready, 1)
                    dve.wait_ge(s.edge_in_psum, b + 1)
                    nc.vector.tensor_scalar(small[:, 3:4], k.wide[0][:, 512:513], 0.5, None, ALU.mult).then_inc(s.half_age_ready, 1)
                    dve.wait_ge(s.score_in_psum, b + 1)
                    nc.vector.tensor_tensor(lg[:, :, :], mask[:, :, 0, :], k.wide[0][:, 0:E].unsqueeze(1).broadcast_to([P, NC, E]), ALU.mult).then_inc(s.coef_step, 1)
                    dve.wait_ge(s.coef_step, b * 4 + 3)
                    nc.vector.tensor_tensor(coef[:, :, 0, :], lg[:, :, :], fill[:, :, :], ALU.add).then_inc(s.coef_masked, 1)
                    dve.wait_ge(s.coef_masked, b * 3 + 1)
                    nc.vector.reduce_max(c8[:, 0, :], coef[:, :, 0, :], axis=AX_X).then_inc(s.coef_masked, 1)
                    dve.wait_ge(s.coef_masked, b * 3 + 2)
                    nc.vector.tensor_tensor(lg[:, :, :], coef[:, :, 0, :], c8[:, 0, :].unsqueeze(2).broadcast_to([P, NC, E]), ALU.subtract).then_inc(s.coef_step, 1)
                    dve.wait_ge(s.gate_tanh, b * 2 + 2)
                    nc.vector.tensor_scalar(beta[:, :], beta[:, :], 0.5, 0.5, ALU.mult, ALU.add).then_inc(s.beta_ready, 1)
                    dve.wait_ge(s.coef_exp, b + 1)
                    nc.vector.reduce_sum(c8[:, 1, :], lg[:, :, :], axis=AX_X).then_inc(s.coef_masked, 1)
                    dve.wait_ge(s.coef_masked, b * 3 + 3)
                    nc.vector.reciprocal(c8[:, 2, :], c8[:, 1, :]).then_inc(s.coef_rinv, 1)
                    dve.wait_ge(s.coef_rinv, b + 1)
                    for i in range(2):
                        last = nc.vector.tensor_tensor(coef[:, :, i, :], lg[:, :, :], c8[:, 2, :].unsqueeze(2).broadcast_to([P, NC, E]), ALU.mult)
                        if i == 0:
                            last.then_inc(s.coef_half, 1)
                    last.then_inc(s.coef_ready, 1)
                    dve.wait_ge(s.beta_hi, b + 1)
                    nc.vector.tensor_tensor(beta_s[E:P, :], beta[E:P, :], f32(beta_s[E:P, :]), ALU.subtract).then_inc(s.beta_split, 1)
                    dve.wait_ge(s.cT_ready, b * 2 + 2)
                    nc.vector.tensor_tensor(cbeta[:, :], cT[:, :], beta[:, :], ALU.mult).then_inc(s.cbeta_ready, 1)
                    nc.vector.tensor_tensor(c_s[E:P, :], cT[E:P, :], f32(c_s[E:P, :]), ALU.subtract).then_inc(s.c_split, 1)

                    def gated(e):
                        dve.wait_ge(s.beta_rows, b * EP + e + 1)
                        if e >= 3:
                            dve.wait_ge(s.r_done, b * EP + e - 2)
                        nc.vector.scalar_tensor_tensor(out=w_t[e % 3][:, :], in0=hT[:, :], scalar=agg_e[:, e:e + 1], in1=rows_of["beta", e][:, :],
                                                       op0=ALU.subtract, op1=ALU.mult).then_inc(s.w_done, 1)

                    for e in range(LEAD):
                        gated(e)
                    dve.wait_ge(s.hsum_in_psum, b + 1)
                    for i, hs in enumerate(HS):
                        nc.vector.tensor_tensor(hsum[:, hs], hT[:, hs], (k.bank_u, k.bank_m)[i][:, :], ALU.mult).then_inc(s.hsum_ready, 1)
                    for e in range(EP):
                        if e + LEAD < EP:
                            gated(e + LEAD)
                        dve.wait_ge(s.u_done, b * EP + e + 1)
                        dve.wait_ge(s.c_rows, b * EP + e + 1)
                        if e >= 2:
                            dve.wait_ge(s.summed, b * EP + e - 1)
                        nc.vector.tensor_tensor(p_t[e % 2][:, :], u_t[e % 2][:, :], rows_of["c", e][:, :], ALU.mult).then_inc(s.p_done, 1)
                    dve.wait_ge(s.summed, b * EP + EP)
                    nc.vector.tensor_tensor(g[:, :], hsum[:, :], k.pair[:, :], ALU.add).then_inc(s.g_ready, 1)
                    dve.wait_ge(s.g_ready, b + 1)
                    dve.wait_ge(s.ind_loaded, b * 32 + 32)
                    nc.vector.tensor_tensor(t1[:, :], ind[:, :], g[:, :], ALU.subtract).then_inc(s.mix_step, 1)
                    dve.wait_ge(s.mix_tanh, b + 1)
                    nc.vector.tensor_scalar(t2[:, :], t0[:, :], -0.5, 0.5, ALU.mult, ALU.add).then_inc(s.mix_step, 1)
                    dve.wait_ge(s.mix_step, b * 3 + 2)
                    nc.vector.tensor_tensor(t0[:, :], t1[:, :], t2[:, :], ALU.mult).then_inc(s.mix_step, 1)
                    dve.wait_ge(s.mix_step, b * 3 + 3)
                    nc.vector.tensor_tensor(t1[:, :], t0[:, :], g[:, :], ALU.add).then_inc(s.outT_ready, 1)
                    dve.wait_ge(s.out_in_psum, b + 1)
                    nc.vector.tensor_copy(k.delta[:, bass.ds(b, 1), :, :].rearrange("p b c f -> p (b c) f"),
                                          k.wide[0][:, :].rearrange("p (c f) -> p c f", f=P)[:, :, 0:F]).then_inc(s.out_stored, 1)
                    dve.wait_ge(s.out_stored, b + 1)



def build(nc, x, adj, emb, weight, bias, net_params, Wh, bh, W_out, b_out, H, W, W_ind, a_node, a_gn, a_ge, fcW, fcb, av, out):
    k = Ctx()
    k.B, k.N, k.F = x.shape
    k.NC, k.D, k.K = k.N // P, weight.shape[0], weight.shape[1]
    with ExitStack() as ctx:
        def sb(n, s, d=F32):
            return ctx.enter_context(nc.sbuf_tensor(n, s, d))

        def ps(n, s):
            return ctx.enter_context(nc.psum_tensor(n, s, F32))

        in_use = []

        def sem(n):
            in_use.append(nc.alloc_semaphore(name=n))
            return in_use[-1]

        def retire_semaphores():
            with nc.Block() as block:
                @block.gpsimd
                def _(pool):
                    nc.clear_and_free_semaphores(in_use)
            in_use.clear()

        k.sem = sem
        k.wide = [ps("wide0", [P, 1024]), ps("wide1", [P, 1024])]
        k.pair = ps("pair", [P, 1024])
        k.bank_u, k.bank_m = ps("bank_u", [P, 512]), ps("bank_m", [P, 512])

        k.ident = sb("ident", [P, P])
        k.xn = sb("xn", [P, k.NC, k.B, k.F])
        k.deg = sb("deg", [P, k.NC])
        with ExitStack() as front:
            k.at_hi = front.enter_context(nc.sbuf_tensor("at_hi", [P, k.NC, k.N], F32R))
            k.at_lo = front.enter_context(nc.sbuf_tensor("at_lo", [P, k.NC, k.N], F32R))
            with ExitStack() as inner:
                k.split = [inner.enter_context(nc.sbuf_tensor(f"split{i}", [P, k.NC, k.B, 2, k.F], F32R)) for i in range(1)]
                k.w_split = inner.enter_context(nc.sbuf_tensor("w_split", [P, k.K, 2, k.F * k.D], F32R))
                k.emb = inner.enter_context(nc.sbuf_tensor("emb", [P, k.NC, k.D], F32))
                k.node_bias = inner.enter_context(nc.sbuf_tensor("node_bias", [P, k.NC, k.F], F32))
                load_and_transpose_adjacency(nc, k, adj, x, (emb, weight, bias))
                k.split.append(inner.enter_context(nc.sbuf_tensor("split1", [P, k.NC, k.B, 2, k.F], F32R)))
                node_weight_convolution(nc, k)
            layer_norm(nc, k, "_0")
            with ExitStack() as inner:
                k.split = [inner.enter_context(nc.sbuf_tensor("split2", [P, k.NC, 2, k.B, k.F], F32R))]
                relu_diffusion(nc, k, net_params)
            layer_norm(nc, k, "_1")
        retire_semaphores()
        k.delta = sb("delta", [P, k.B + 1, k.NC, k.F])
        ind_dram = nc.dram_tensor("industry", [k.B, k.F, k.N], F32)
        with ExitStack() as rows:
            k.adj = rows.enter_context(nc.sbuf_tensor("adj_rows2", [P, k.NC, k.N], F32))
            graph_attention(nc, k, adj, Wh, bh, W_out, b_out)
            layer_norm(nc, k, "_2", add=k.delta[:, 1:k.B + 1, :, :].rearrange("p b c f -> p c b f"))
            retire_semaphores()
            industry_messages(nc, k, W_ind, ind_dram)
        hypergraph_attention(nc, k, (H, W, a_node, a_gn, a_ge, fcW, fcb, av), ind_dram)
        layer_norm(nc, k, "_3", add=k.delta[:, 0:k.B, :, :].rearrange("p b c f -> p c b f"))
        stored = k.sem("stored")
        with nc.Block() as block:
            @block.sync
            def _(sp):
                for c in range(k.NC):
                    sp.dma_start(out[:, c * P:(c + 1) * P, :].rearrange("b p f -> p b f"), k.xn[:, c, :, :]).then_inc(stored, 16)
                sp.wait_ge(stored, 16 * k.NC)


_INS = ['x', 'adj', 'L0_gnn_embedding', 'L0_gnn_weight', 'L0_gnn_bias', 'L1_gnn_net_params', 'L2_gnn_Wh', 'L2_gnn_bh',
        'L2_gnn_W_out', 'L2_gnn_b_out', 'L3_gnn_H', 'L3_gnn_W', 'L3_gnn_W_ind', 'L3_gnn_a_node', 'L3_gnn_a_gn',
        'L3_gnn_a_ge', 'L3_gnn_fcW', 'L3_gnn_fcb', 'L3_gnn_av']


def kernel(**inputs):
    import numpy as _np
    import concourse.bacc as _bacc
    from concourse import mybir as _mybir
    from concourse.bass_utils import run_bass_kernel_spmd as _run

    nc = _bacc.Bacc("TRN2", target_bir_lowering=False, num_devices=1)
    arrays, args = {}, []
    for name in _INS:
        a = _np.ascontiguousarray(inputs[name])
        arrays[f"in_{name}_dram"] = a
        args.append(nc.dram_tensor(f"in_{name}_dram", a.shape, _mybir.dt.from_np(a.dtype), kind="ExternalInput").ap())
    args.append(nc.dram_tensor("out_0_dram", inputs["x"].shape, _mybir.dt.float32, kind="ExternalOutput").ap())
    build(nc, *args)
    r = _run(nc, [arrays], core_ids=[0])
    return r.results[0]["out_0_dram"]
```

```python
from contextlib import ExitStack

import concourse.bass as bass
from concourse import mybir

F32 = mybir.dt.float32
F32R = mybir.dt.float32r
ALU = mybir.AluOpType
ACT = mybir.ActivationFunctionType
AX_X = mybir.AxisListType.X

P = 128
EPS = 1e-5
MASKED = -1e16
NEG = -1e9


class Ctx:
    pass



def f32(ap):
    return ap.bitcast(F32)



def load_and_transpose_adjacency(nc, k, adj, x, params):
    N, NC = k.N, k.NC
    emb, weight, bias = params
    D, K, F, O = weight.shape
    with ExitStack() as ctx:
        sb = lambda n, s, d=F32: ctx.enter_context(nc.sbuf_tensor(n, s, d))
        sem = k.sem
        an = sb("adj_rows", [P, NC, N])
        w_raw = sb("w_raw", [P, K, D, O])
        embT = sb("embT", [D, N])
        bias_sb = sb("bias_sb", [D, O])
        adj_loaded = [sem(f"adj_loaded{c}") for c in range(NC)]
        x_loaded, w_loaded = sem("x_loaded"), sem("w_loaded")
        zeroed, ident_ready = sem("ident_zeroed"), sem("ident_ready")
        at_transposed, at_hi_ready, at_lo_ready = sem("at_transposed"), sem("at_hi_ready"), sem("at_lo_ready")
        embT_in_psum, embT_ready, nbias_in_psum, setup_done = (
            sem("embT_in_psum"), sem("embT_ready"), sem("nbias_in_psum"), sem("setup_done"))
        split_ready = sem("split0_hi_ready")

        with nc.Block() as block:
            @block.sync
            def _(sp):
                for c in range(NC):
                    sp.dma_start(an[:, c, :], adj[c * P:(c + 1) * P, :]).then_inc(adj_loaded[c], 16)
                for c in range(NC):
                    sp.dma_start(k.xn[:, c, :, :], x[:, c * P:(c + 1) * P, :].rearrange("b p f -> p b f")).then_inc(x_loaded, 16)

            @block.gpsimd
            def _(pool):
                nc.gpsimd.memset(k.ident[:, :], 0.0).then_inc(zeroed, 1)
                pool.wait_ge(zeroed, 1)
                nc.gpsimd.affine_select(out=k.ident[:, :], in_=k.ident[:, :], compare_op=ALU.not_equal, fill=1.0,
                                        base=0, pattern=[[-1, P]], channel_multiplier=1).then_inc(ident_ready, 1)
                pool.dma_start(k.emb[:, :, :], emb.rearrange("(c p) d -> p c d", p=P)).then_inc(w_loaded, 16)
                pool.dma_start(bias_sb[:, :], bias).then_inc(w_loaded, 16)
                for half in range(2):
                    for t in range(K):
                        pool.dma_start(w_raw[half * F:(half + 1) * F, t, :, :],
                                       weight[:, t, :, :].rearrange("d i o -> i d o")).then_inc(w_loaded, 16)

            @block.tensor
            def _(pe):
                pe.wait_ge(ident_ready, 1)
                for mc in range(NC):
                    if mc == 0:
                        for c in range(NC):
                            pe.wait_ge(adj_loaded[c], 16)
                    if mc >= 2:
                        pe.wait_ge(at_lo_ready, mc - 1)
                    for c in range(NC):
                        last = nc.tensor.transpose(k.wide[mc % 2][:, c * P:(c + 1) * P], an[:, c, mc * P:(mc + 1) * P], k.ident[:, :])
                    last.then_inc(at_transposed, 1)
                pe.wait_ge(w_loaded, 16 * (2 + 2 * K))
                for c in range(NC):
                    last = nc.tensor.transpose(k.pair[0:D, c * P:(c + 1) * P], k.emb[:, c, :], k.ident[:, :])
                last.then_inc(embT_in_psum, 1)
                pe.wait_ge(embT_ready, 1)
                for c in range(NC):
                    last = nc.tensor.matmul(k.bank_u[:, c * O:(c + 1) * O], embT[:, c * P:(c + 1) * P], bias_sb[:, :], start=True, stop=True)
                last.then_inc(nbias_in_psum, 1)

            @block.scalar
            def _(act):
                act.wait_ge(x_loaded, 16 * NC)
                nc.scalar.activation(k.split[0][:, :, :, 0, :].rearrange("p c b f -> p (c b) f"),
                                     k.xn[:, :, :, :].rearrange("p c b f -> p (c b) f"), ACT.Copy).then_inc(split_ready, 1)
                for mc in range(NC):
                    act.wait_ge(at_transposed, mc + 1)
                    nc.scalar.activation(k.at_hi[:, mc, :], k.wide[mc % 2][:, :], ACT.Copy).then_inc(at_hi_ready, 1)
                act.wait_ge(w_loaded, 16 * (2 + 2 * K))
                for t in range(K):
                    nc.scalar.activation(k.w_split[:, t, 0, :].rearrange("p (o d) -> p o d", d=D),
                                         w_raw[:, t, :, :].rearrange("p d o -> p o d"), ACT.Copy).then_inc(split_ready, 1)
                act.wait_ge(embT_in_psum, 1)
                nc.scalar.activation(embT[:, :], k.pair[0:D, :], ACT.Copy).then_inc(embT_ready, 1)
                act.wait_ge(nbias_in_psum, 1)
                nc.scalar.activation(k.node_bias[:, :, :].rearrange("p c o -> p (c o)"), k.bank_u[:, :], ACT.Copy).then_inc(setup_done, 1)

            @block.vector
            def _(dve):
                dve.wait_ge(split_ready, 1)
                nc.vector.tensor_tensor(k.split[0][:, :, :, 1, :].rearrange("p c b f -> p (c b) f"),
                                        k.xn[:, :, :, :].rearrange("p c b f -> p (c b) f"),
                                        f32(k.split[0][:, :, :, 0, :]).rearrange("p c b f -> p (c b) f"), ALU.subtract).then_inc(setup_done, 1)
                for mc in range(NC):
                    dve.wait_ge(at_hi_ready, mc + 1)
                    nc.vector.tensor_tensor(k.at_lo[:, mc, :], k.wide[mc % 2][:, :], f32(k.at_hi[:, mc, :]), ALU.subtract).then_inc(at_lo_ready, 1)
                for c in range(NC):
                    dve.wait_ge(adj_loaded[c], 16)
                    nc.vector.reduce_sum(k.deg[:, c:c + 1], an[:, c, :], axis=AX_X).then_inc(setup_done, 1)
                for t in range(K):
                    dve.wait_ge(split_ready, 2 + t)
                    nc.vector.tensor_tensor(k.w_split[:, t, 1, :].rearrange("p (o d) -> p o d", d=D),
                                            w_raw[:, t, :, :].rearrange("p d o -> p o d"),
                                            f32(k.w_split[:, t, 0, :]).rearrange("p (o d) -> p o d", d=D), ALU.subtract).then_inc(setup_done, 1)



def layer_norm(nc, k, tag, add=None):
    G, F = k.NC * k.B, k.F
    with ExitStack() as ctx:
        sb = lambda n, s, d=F32: ctx.enter_context(nc.sbuf_tensor(n + tag, s, d))
        sem = lambda n: k.sem(n + tag)
        sq = sb("ln_sq", [P, G, F])
        total, mean, var, std, rstd = (sb(n, [P, G]) for n in ("ln_total", "ln_mean", "ln_var", "ln_std", "ln_rstd"))
        step, centred, squared, var_ready, std_ready = (
            sem(n) for n in ("ln_step", "ln_centred", "ln_squared", "ln_var_ready", "ln_std_ready"))
        x = k.xn[:, :, :, :].rearrange("p c b f -> p (c b) f")
        with nc.Block() as block:
            @block.scalar
            def _(act):
                act.wait_ge(centred, 1)
                nc.scalar.activation(sq[:, :, :], x, ACT.Square).then_inc(squared, 1)
                act.wait_ge(var_ready, 1)
                nc.scalar.activation(std[:, :], var[:, :], ACT.Sqrt).then_inc(std_ready, 1)

            @block.vector
            def _(dve):
                n = 0
                if add is not None:
                    nc.vector.tensor_tensor(k.xn[:, :, :, :], k.xn[:, :, :, :], add, ALU.add).then_inc(step, 1)
                    n += 1
                    dve.wait_ge(step, n)
                nc.vector.reduce_sum(total[:, :], x, axis=AX_X).then_inc(step, 1)
                dve.wait_ge(step, n + 1)
                nc.vector.tensor_scalar(mean[:, :], total[:, :], 1.0 / F, None, ALU.mult).then_inc(step, 1)
                dve.wait_ge(step, n + 2)
                nc.vector.tensor_tensor(x, x, mean[:, :].unsqueeze(2).broadcast_to([P, G, F]), ALU.subtract).then_inc(centred, 1)
                dve.wait_ge(squared, 1)
                nc.vector.reduce_sum(total[:, :], sq[:, :, :], axis=AX_X).then_inc(step, 1)
                dve.wait_ge(step, n + 3)
                nc.vector.tensor_scalar(var[:, :], total[:, :], 1.0 / F, EPS, ALU.mult, ALU.add).then_inc(var_ready, 1)
                dve.wait_ge(std_ready, 1)
                nc.vector.reciprocal(rstd[:, :], std[:, :]).then_inc(step, 1)
                dve.wait_ge(step, n + 4)
                nc.vector.tensor_tensor(std[:, :], rstd[:, :], rstd[:, :], ALU.mult).then_inc(step, 1)
                dve.wait_ge(step, n + 5)
                nc.vector.tensor_tensor(std[:, :], std[:, :], var[:, :], ALU.mult).then_inc(step, 1)
                dve.wait_ge(step, n + 6)
                nc.vector.tensor_scalar(std[:, :], std[:, :], -0.5, 1.5, ALU.mult, ALU.add).then_inc(step, 1)
                dve.wait_ge(step, n + 7)
                nc.vector.tensor_tensor(rstd[:, :], rstd[:, :], std[:, :], ALU.mult).then_inc(step, 1)
                dve.wait_ge(step, n + 8)
                nc.vector.tensor_tensor(x, x, rstd[:, :].unsqueeze(2).broadcast_to([P, G, F]), ALU.mult).then_inc(step, 1)



def node_weight_convolution(nc, k):
    NC, B, F, D, K, O = k.NC, k.B, k.F, k.D, k.K, k.F
    CH = O * D // 512
    with ExitStack() as ctx:
        sb = lambda n, s, d=F32: ctx.enter_context(nc.sbuf_tensor(n, s, d))
        sem = k.sem
        cheb1 = k.split[1]
        cheb2 = [sb(f"cheb2_{i}", [P, B, 2, F], F32R) for i in range(2)]
        cheb2_full = sb("cheb2_full", [P, B, F])
        stat = [sb(f"l0_stat{i}", [P, K, P], F32R) for i in range(2)]
        weighted = [sb(f"l0_weighted{i}", [P, O, D]) for i in range(2)]
        summed = [sb(f"l0_summed{i}", [P, B, O]) for i in range(2)]
        prod_ready, hi_ready, cheb1_ready = sem("l0_prod_ready"), sem("l0_hi_ready"), sem("l0_cheb1_ready")
        full_ready, cheb2_ready = sem("l0_full_ready"), sem("l0_cheb2_ready")
        stat_in_psum, stat_ready, y_ready, weighted_ready, summed_ready, step = (
            sem(n) for n in ("l0_stat_in_psum", "l0_stat_ready", "l0_y_ready", "l0_weighted_ready", "l0_summed_ready", "l0_step"))
        prod = [k.bank_u, k.bank_m]
        tpos = [k.pair[:, 0:512], k.pair[:, 512:1024]]

        def product(pe, c, src, bank):
            n = 0
            for a, s in ((k.at_hi, 0), (k.at_hi, 1), (k.at_lo, 0)):
                for mc in range(NC):
                    last = nc.tensor.matmul(bank[:, :].rearrange("p (b f) -> p b f", f=F), a[:, mc, c * P:(c + 1) * P],
                                            src[:, mc, :, s, :], start=n == 0, stop=n == 3 * NC - 1)
                    n += 1
            return last

        with nc.Block() as block:
            @block.tensor
            def _(pe):
                for c in range(NC):
                    if c >= 2:
                        pe.wait_ge(cheb1_ready, c - 1)
                    product(pe, c, k.split[0], prod[c % 2]).then_inc(prod_ready, 1)
                pe.wait_ge(cheb1_ready, NC)
                product(pe, 0, cheb1, prod[0]).then_inc(prod_ready, 1)
                for c in range(NC):
                    if c + 1 < NC:
                        if c >= 1:
                            pe.wait_ge(full_ready, c)
                        product(pe, c + 1, cheb1, prod[(c + 1) % 2]).then_inc(prod_ready, 1)
                    pe.wait_ge(cheb2_ready, c + 1)

                    def turn(t):
                        b = t % B
                        if t >= 2:
                            pe.wait_ge(stat_ready, t - 1)
                        for i, s in enumerate((k.split[0][:, c, b, :, :], cheb1[:, c, b, :, :], cheb2[c % 2][:, b, :, :])):
                            last = nc.tensor.transpose(tpos[t % 2][:, i * P:(i + 1) * P],
                                                       f32(s).rearrange("p s f -> p (s f)"), k.ident[:, :])
                        last.then_inc(stat_in_psum, 1)

                    turn(c * B)
                    for b in range(B):
                        t = c * B + b
                        if b + 1 < B:
                            turn(t + 1)
                        pe.wait_ge(stat_ready, t + 1)
                        if t >= 2:
                            pe.wait_ge(weighted_ready, t - 1)
                        for j in range(CH):
                            for i in range(K):
                                for part in range(2):
                                    last = nc.tensor.matmul(k.wide[t % 2][:, j * 512:(j + 1) * 512], stat[t % 2][:, i, :],
                                                            k.w_split[:, i, part, j * 512:(j + 1) * 512],
                                                            start=i + part == 0, stop=i == K - 1 and part == 1)
                        last.then_inc(y_ready, 1)

            @block.scalar
            def _(act):
                for c in range(NC):
                    act.wait_ge(prod_ready, c + 1)
                    nc.scalar.activation(cheb1[:, c, :, 0, :], prod[c % 2][:, :].rearrange("p (b f) -> p b f", f=F), ACT.Copy).then_inc(hi_ready, 1)

                def cheb2_hi(c):
                    act.wait_ge(full_ready, c + 1)
                    if c >= 2:
                        act.wait_ge(stat_in_psum, (c - 1) * B)
                    nc.scalar.activation(cheb2[c % 2][:, :, 0, :], cheb2_full[:, :, :], ACT.Copy).then_inc(hi_ready, 1)

                cheb2_hi(0)
                for c in range(NC):
                    for b in range(B):
                        t = c * B + b
                        if b == 5 and c + 1 < NC:
                            cheb2_hi(c + 1)
                        act.wait_ge(stat_in_psum, t + 1)
                        if t >= 2:
                            act.wait_ge(y_ready, t - 1)
                        nc.scalar.activation(stat[t % 2][:, :, :].rearrange("p k n -> p (k n)"), tpos[t % 2][:, 0:K * P], ACT.Copy).then_inc(stat_ready, 1)

            @block.vector
            def _(dve):
                for c in range(NC):
                    dve.wait_ge(hi_ready, c + 1)
                    nc.vector.tensor_tensor(cheb1[:, c, :, 1, :], prod[c % 2][:, :].rearrange("p (b f) -> p b f", f=F),
                                            f32(cheb1[:, c, :, 0, :]), ALU.subtract).then_inc(cheb1_ready, 1)

                def cheb2_parts(c):
                    dve.wait_ge(prod_ready, NC + c + 1)
                    if c >= 1:
                        dve.wait_ge(cheb2_ready, c)
                    nc.vector.scalar_tensor_tensor(out=cheb2_full[:, :, :], in0=prod[c % 2][:, :].rearrange("p (b f) -> p b f", f=F),
                                                   scalar=2.0, in1=k.xn[:, c, :, :], op0=ALU.mult, op1=ALU.subtract).then_inc(full_ready, 1)
                    dve.wait_ge(hi_ready, NC + c + 1)
                    if c >= 2:
                        dve.wait_ge(stat_in_psum, (c - 1) * B)
                    nc.vector.tensor_tensor(cheb2[c % 2][:, :, 1, :], cheb2_full[:, :, :], f32(cheb2[c % 2][:, :, 0, :]), ALU.subtract).then_inc(cheb2_ready, 1)

                n = 0
                cheb2_parts(0)
                for c in range(NC):
                    emb_b = k.emb[:, c, :].unsqueeze(1).broadcast_to([P, O, D])
                    for b in range(B):
                        t = c * B + b
                        if b == 5 and c + 1 < NC:
                            cheb2_parts(c + 1)
                        dve.wait_ge(y_ready, t + 1)
                        if t >= 1:
                            dve.wait_ge(summed_ready, t)
                        nc.vector.tensor_tensor(weighted[t % 2][:, :, :], k.wide[t % 2][:, :].rearrange("p (o d) -> p o d", d=D), emb_b, ALU.mult).then_inc(weighted_ready, 1)
                        dve.wait_ge(weighted_ready, t + 1)
                        nc.vector.reduce_sum(summed[c % 2][:, b, :], weighted[t % 2][:, :, :], axis=AX_X).then_inc(summed_ready, 1)
                    dve.wait_ge(summed_ready, (c + 1) * B)
                    nc.vector.tensor_tensor(k.xn[:, c, :, :], k.xn[:, c, :, :], summed[c % 2][:, :, :], ALU.add).then_inc(step, 1)
                    n += 1
                    dve.wait_ge(step, n)
                    nc.vector.tensor_tensor(k.xn[:, c, :, :], k.xn[:, c, :, :],
                                            k.node_bias[:, c, :].unsqueeze(1).broadcast_to([P, B, O]), ALU.add).then_inc(step, 1)
                    n += 1



def product_transposed(nc, k, pe, src, out_bank, bp, half):
    n, NC = 0, k.NC
    for a, s in ((k.at_hi, 0), (k.at_lo, 0), (k.at_hi, 1)):
        for mc in range(NC):
            last = nc.tensor.matmul(out_bank, src[:, mc, s, 2 * bp:2 * bp + 2, :].rearrange("p b f -> p (b f)"),
                                    a[:, mc, half * 512:(half + 1) * 512], start=n == 0, stop=n == 3 * NC - 1)
            n += 1
    return last


def relu_diffusion(nc, k, net_params):
    NC, B, F, L = k.NC, k.B, k.F, 2
    BP, HV = B // 2, k.N // 512
    with ExitStack() as ctx:
        sb = lambda n, s, d=F32: ctx.enter_context(nc.sbuf_tensor(n, s, d))
        sem = k.sem
        w2 = sb("l1_w2", [P, L, P])
        aggT = sb("l1_aggT", [P, BP, k.N])
        zeroed, w_loaded = sem("l1_zeroed"), sem("l1_w_loaded")
        hi_ready, lo_ready, prod_ready, agg_ready, z_in_psum, z_read = (
            sem(n) for n in ("l1_hi_ready", "l1_lo_ready", "l1_prod_ready", "l1_agg_ready", "l1_z_in_psum", "l1_z_read"))
        z = k.split[0]
        prod = [k.bank_u[:, :], k.bank_m[:, :]]
        zb = [k.pair[:, 0:512], k.pair[:, 512:1024]]
        w_dram = net_params.rearrange("(l f g) -> f l g", l=L, f=F)
        with nc.Block() as block:
            @block.sync
            def _(sp):
                sp.wait_ge(zeroed, 1)
                for i in range(2):
                    sp.dma_start(w2[i * F:(i + 1) * F, :, i * F:(i + 1) * F], w_dram).then_inc(w_loaded, 16)

            @block.gpsimd
            def _(pool):
                nc.gpsimd.memset(w2[:, :, :], 0.0).then_inc(zeroed, 1)

            @block.tensor
            def _(pe):
                pe.wait_ge(w_loaded, 32)
                for l in range(L):
                    pe.wait_ge(lo_ready, 1 if l == 0 else 1 + NC)
                    for g in range(BP * HV):
                        t = l * BP * HV + g
                        if t >= 2:
                            pe.wait_ge(agg_ready, t - 1)
                        product_transposed(nc, k, pe, z, prod[t % 2], g // HV, g % HV).then_inc(prod_ready, 1)
                    pe.wait_ge(agg_ready, (l + 1) * BP * HV)
                    for c in range(NC):
                        t = l * NC + c
                        if t >= 2 and t < NC + 2:
                            pe.wait_ge(lo_ready, t)
                        elif t >= 2:
                            pe.wait_ge(z_read, t - NC - 1)
                        for bp in range(BP):
                            last = nc.tensor.matmul(zb[t % 2][:, bp * P:(bp + 1) * P], aggT[:, bp, c * P:(c + 1) * P], w2[:, l, :], start=True, stop=True)
                        last.then_inc(z_in_psum, 1)

            @block.scalar
            def _(act):
                nc.scalar.activation(z[:, :, 0, :, :].rearrange("p c b f -> p c (b f)"),
                                     k.xn[:, :, :, :].rearrange("p c b f -> p c (b f)"), ACT.Copy).then_inc(hi_ready, 1)
                for l in range(L):
                    for g in range(BP * HV):
                        t = l * BP * HV + g
                        act.wait_ge(prod_ready, t + 1)
                        nc.scalar.activation(aggT[:, g // HV, (g % HV) * 512:(g % HV + 1) * 512], prod[t % 2], ACT.Copy).then_inc(agg_ready, 1)
                    if l == 0:
                        for c in range(NC):
                            act.wait_ge(z_in_psum, c + 1)
                            nc.scalar.activation(z[:, c, 0, :, :], zb[c % 2].rearrange("p (b f) -> p b f", f=F), ACT.Relu).then_inc(hi_ready, 1)

            @block.vector
            def _(dve):
                dve.wait_ge(hi_ready, 1)
                nc.vector.tensor_tensor(z[:, :, 1, :, :].rearrange("p c b f -> p c (b f)"),
                                        k.xn[:, :, :, :].rearrange("p c b f -> p c (b f)"),
                                        f32(z[:, :, 0, :, :]).rearrange("p c b f -> p c (b f)"), ALU.subtract).then_inc(lo_ready, 1)
                for c in range(NC):
                    dve.wait_ge(hi_ready, 2 + c)
                    nc.vector.scalar_tensor_tensor(out=z[:, c, 1, :, :], in0=zb[c % 2].rearrange("p (b f) -> p b f", f=F), scalar=0.0,
                                                   in1=f32(z[:, c, 0, :, :]), op0=ALU.max, op1=ALU.subtract).then_inc(lo_ready, 1)
                for c in range(NC):
                    dve.wait_ge(z_in_psum, NC + c + 1)
                    nc.vector.scalar_tensor_tensor(out=k.xn[:, c, :, :], in0=zb[c % 2].rearrange("p (b f) -> p b f", f=F), scalar=0.0,
                                                   in1=k.xn[:, c, :, :], op0=ALU.max, op1=ALU.add).then_inc(z_read, 1)



OUT = "out"


def attention_slots(insts):
    slots = [(-1, "project", 0, h) for h in range(2) if insts[0] != OUT]
    for i in range(len(insts) + 1):
        for c in range(8):
            step, prev = 8 * i + c, (insts[i - 1] if i else None)
            if c == 0 and i:
                slots.append((step, "sums", i - 1, 1))
            if c in (1, 5) and i and prev != OUT:
                slots.append((step, "head", i - 1, c // 4))
            if c in (2, 6) and i:
                slots.append((step, "mix" if prev != OUT else "turn", i - 1, c // 4))
            if c in (3, 4) and i + 1 < len(insts) and insts[i + 1] != OUT:
                slots.append((step, "project", i + 1, c - 3))
            if c == 7 and i < len(insts):
                slots.append((step, "sums", i, 0))
    return slots


def attention_tensor(nc, k, a, pe, insts, b, at):
    slots = attention_slots(insts)
    order = [i for i in insts if i != OUT]
    NI, ST = len(insts), 8 * len(insts)

    def nth_head(i):
        return order.index(insts[i])

    def misc_bank_free(m):
        if m == 0:
            return
        _, kind, i, h = slots[m - 1]
        if kind == "project":
            pe.wait_ge(a.keys_ready, at("keys_ready", 2 * nth_head(i) + h + 1))
        elif kind == "sums":
            pe.wait_ge(a.inv_ready, at("inv_ready", 2 * i + h + 1))
        elif kind == "head":
            pe.wait_ge(a.biased_ready, at("biased_ready", 2 * i + h + 1))
        elif kind == "mix":
            pe.wait_ge(a.mixed, at("mixed", 2 * nth_head(i) + h + 1))
        else:
            pe.wait_ge(a.out_stored, at("out_stored", h + 1))

    def slot(step):
        for m, (st, kind, i, h) in enumerate(slots):
            if st != step:
                continue
            misc_bank_free(m)
            inst = insts[i]
            if kind == "project":
                if h == 0:
                    pe.wait_ge(a.xt_lo_ready, at("xt_lo_ready", 1))
                nc.tensor.matmul(k.bank_m[:, :], a.gram_hi[:, inst, :], a.xt[:, h * 512:(h + 1) * 512], start=True, stop=False)
                last = nc.tensor.matmul(k.bank_m[:, :], a.gram_lo[:, inst, :], a.xt[:, h * 512:(h + 1) * 512], start=False, stop=True)
            elif kind == "sums":
                pe.wait_ge(a.rinv_ready, at("rinv_ready", 2 * i + h + 1))
                for j in range(4):
                    col = 8 * (i % 2) + 4 * h + j
                    last = nc.tensor.matmul(k.bank_m[:, j * P:(j + 1) * P], a.rinv[:, col:col + 1].broadcast_to([P, P]),
                                            k.ident[:, :], start=True, stop=True)
            elif kind == "head":
                pe.wait_ge(a.ctx_ready, at("ctx_ready", 2 * i + h + 1))
                last = nc.tensor.matmul(k.bank_m[:, :], a.wh[:, inst, :], a.ctx[h][:, :], start=True, stop=True)
            elif kind == "mix":
                pe.wait_ge(a.leaky_ready, at("leaky_ready", 2 * i + h + 1))
                last = nc.tensor.matmul(k.bank_m[:, :], a.wo[:, inst, :, :].rearrange("p t o -> p (t o)"), a.leaky[:, :], start=True, stop=True)
            else:
                pe.wait_ge(a.leaky_ready, at("leaky_ready", 2 * i + h + 1))
                for j in range(4):
                    last = nc.tensor.transpose(k.bank_m[:, j * P:(j + 1) * P], a.leaky[:, j * P:(j + 1) * P], k.ident[:, :])
            last.then_inc(a.slot_done, 1)

    def scores(q):
        i, c = divmod(q, 8)
        out = insts[i] == OUT
        if q == 0 and insts[0] != OUT:
            pass
        elif q == 1 and insts[0] != OUT:
            pe.wait_ge(a.vo_ready, at("vo_ready", 1))
        elif q >= 2:
            pe.wait_ge(a.scaled, at("scaled", q - 1))
        if c == 0:
            if out:
                pe.wait_ge(a.ko_lo_ready, at("ko_lo_ready", 1))
                pe.wait_ge(a.xo_lo_ready, at("xo_lo_ready", 1))
            else:
                pe.wait_ge(a.keys_ready, at("keys_ready", 2 * nth_head(i) + 2))
        if out and insts[0] == OUT and q < 2:
            pe.wait_ge(a.vo_ready, at("vo_ready", 1))
        xt = a.xo if out else a.xt
        hi, lo = (a.ko_hi, a.ko_lo) if out else (a.keys_hi[nth_head(i) % 2], a.keys_lo[nth_head(i) % 2])
        for j in range(2):
            o = k.wide[q % 2][:, j * 512:(j + 1) * 512]
            nc.tensor.matmul(o, xt[:, c * P:(c + 1) * P], hi[:, j * 512:(j + 1) * 512], start=True, stop=False)
            last = nc.tensor.matmul(o, xt[:, c * P:(c + 1) * P], lo[:, j * 512:(j + 1) * 512], start=False, stop=True)
        last.then_inc(a.scores_ready, 1)

    def turn_probs(q):
        pe.wait_ge(a.probs_ready, at("probs_ready", q + 1))
        for j in range(2):
            if q >= 1:
                pe.wait_ge(a.turned_read, at("turned_read", 2 * (q - 1) + j + 1))
            for m in range(4):
                mc = 4 * j + m
                last = nc.tensor.transpose(k.pair[:, mc * P:(mc + 1) * P], a.probs[q % 2][:, mc * P:(mc + 1) * P], k.ident[:, :])
            last.then_inc(a.turned, 1)

    def values(i, g, piece):
        if piece == 0:
            pe.wait_ge(a.turned_read, at("turned_read", 2 * (8 * i + 4 * g + 4)))
            if 2 * i + g >= 1:
                pe.wait_ge(a.ctx_ready, at("ctx_ready", 2 * i + g))
        v = a.vo if insts[i] == OUT else a.v
        for mc in (2 * piece, 2 * piece + 1):
            last = nc.tensor.matmul(k.bank_u[0:k.F, :], v[:, mc, 0:k.F], a.probsT[g][:, mc, :], start=mc == 0, stop=mc == 7)
        if piece == 3:
            last.then_inc(a.values_done, 1)

    if insts[0] != OUT:
        pe.wait_ge(a.v_ready, at("v_ready", 1))
        for c in range(8):
            last = nc.tensor.transpose(k.wide[0][:, c * P:(c + 1) * P], a.v[:, c, :], k.ident[:, :])
        last.then_inc(a.xt_in_psum, 1)
    else:
        pe.wait_ge(a.mixed, at("mixed", 0))
    for c in range(8):
        last = nc.tensor.transpose(k.wide[1][:, c * P:(c + 1) * P], a.h2[:, c * P:(c + 1) * P], k.ident[:, :])
    last.then_inc(a.vo_in_psum, 1)
    slot(-1)
    scores(0)
    scores(1)
    for step in range(ST + 7):
        i, c = divmod(step, 8)
        if step + 2 < ST:
            scores(step + 2)
        slot(step)
        if step < ST:
            turn_probs(step)
        if c >= 4 and i < NI:
            values(i, 0, c - 4)
        elif c < 4 and i >= 1:
            values(i - 1, 1, c)


def attention_scalar(nc, k, a, act, insts, b, at):
    slots = attention_slots(insts)
    order = [i for i in insts if i != OUT]
    ST = 8 * len(insts)

    def exponentials(q):
        i, c = divmod(q, 8)
        act.wait_ge(a.shifted, at("shifted", q + 1))
        if q >= 2:
            act.wait_ge(a.turned, at("turned", 2 * (q - 2) + 2))
        col = 8 * (i % 2) + c
        nc.scalar.activation(a.probs[q % 2][:, :], a.neg_scores[q % 2][:, :], ACT.Exp, bias=a.neg_max[:, col:col + 1],
                             scale=-1.0, accum_out=a.sums[:, col:col + 1]).then_inc(a.probs_ready, 1)

    def read_turned(q):
        i, c = divmod(q, 8)
        g = c // 4
        if c % 4 == 0 and i >= 1:
            act.wait_ge(a.values_done, at("values_done", 2 * (i - 1) + g + 1))
        for j in range(2):
            act.wait_ge(a.turned, at("turned", 2 * q + j + 1))
            nc.scalar.activation(a.probsT[g][:, 4 * j:4 * j + 4, (c % 4) * P:(c % 4 + 1) * P],
                                 k.pair[:, j * 512:(j + 1) * 512].rearrange("p (m n) -> p m n", n=P), ACT.Copy).then_inc(a.turned_read, 1)

    def slot(step):
        for m, (st, kind, i, h) in enumerate(slots):
            if st != step:
                continue
            inst = insts[i]
            if kind == "project":
                act.wait_ge(a.slot_done, at("slot_done", m + 1))
                n = order.index(inst)
                nc.scalar.activation(a.keys_hi[n % 2][:, h * 512:(h + 1) * 512], k.bank_m[:, :], ACT.Copy).then_inc(a.keys_hi_ready, 1)
            elif kind == "sums":
                act.wait_ge(a.slot_done, at("slot_done", m + 1))
                nc.scalar.activation(a.inv[h][:, :], k.bank_m[0:k.F, :], ACT.Copy).then_inc(a.inv_ready, 1)
            elif kind == "head":
                act.wait_ge(a.slot_done, at("slot_done", m + 1))
                nc.scalar.activation(a.biased[:, :], k.bank_m[:, :], ACT.Identity, bias=a.bh[:, inst:inst + 1]).then_inc(a.biased_ready, 1)
        i, c = divmod(step, 8)
        if c in (1, 5) and i >= 1 and insts[i - 1] == OUT:
            h = c // 4
            act.wait_ge(a.ctx_ready, at("ctx_ready", 2 * (i - 1) + h + 1))
            nc.scalar.activation(a.biased[0:k.F, :], a.ctx[h][:, :], ACT.Identity, bias=a.b_out[:, 0:1]).then_inc(a.biased_ready, 1)

    if insts[0] != OUT:
        act.wait_ge(a.xt_in_psum, at("xt_in_psum", 1))
        nc.scalar.activation(a.xt[:, :], k.wide[0][:, :], ACT.Copy).then_inc(a.xt_hi_ready, 1)
    else:
        act.wait_ge(a.mixed, at("mixed", 0))
    nc.scalar.activation(a.ko_hi[:, :], a.h2[:, :], ACT.Copy).then_inc(a.ko_hi_ready, 1)
    act.wait_ge(a.vo_in_psum, at("vo_in_psum", 1))
    nc.scalar.activation(a.vo[:, :, :].rearrange("p c f -> p (c f)"), k.wide[1][:, :], ACT.Copy).then_inc(a.vo_ready, 1)
    slot(-1)
    exponentials(0)
    for step in range(ST + 7):
        slot(step)
        if step + 1 < ST:
            exponentials(step + 1)
        if step < ST:
            read_turned(step)


def attention_vector(nc, k, a, dve, insts, b, at):
    slots = attention_slots(insts)
    order = [i for i in insts if i != OUT]
    NI, ST = len(insts), 8 * len(insts)

    def shifted_scores(q):
        i, c = divmod(q, 8)
        dve.wait_ge(a.scores_ready, at("scores_ready", q + 1))
        nc.vector.tensor_tensor(a.scaled_scores[:, :], k.wide[q % 2][:, :], k.adj[:, c, :], ALU.mult).then_inc(a.scaled, 1)
        dve.wait_ge(a.scaled, at("scaled", q + 1))
        if q >= 2:
            dve.wait_ge(a.probs_ready, at("probs_ready", q - 1))
        nc.vector.tensor_scalar(a.fill[:, :], a.scaled_scores[:, :], 0.0, MASKED, ALU.is_equal, ALU.mult).then_inc(a.filled, 1)
        dve.wait_ge(a.filled, 1)
        dve.wait_ge(a.filled, at("filled", q + 1))
        col = 8 * (i % 2) + c
        nc.vector.tensor_tensor_reduce(out=a.neg_scores[q % 2][:, :], in0=a.scaled_scores[:, :], in1=a.fill[:, :], scale=-1.0,
                                       scalar=3.0e38, op0=ALU.add, op1=ALU.min, accum_out=a.neg_max[:, col:col + 1]).then_inc(a.shifted, 1)
        dve.wait_ge(a.shifted, at("shifted", q + 1))

    def rinv(i, g):
        dve.wait_ge(a.probs_ready, at("probs_ready", 8 * i + 4 * g + 4))
        col = 8 * (i % 2) + 4 * g
        nc.vector.reciprocal(a.rinv[:, col:col + 4], a.sums[:, col:col + 4]).then_inc(a.rinv_ready, 1)

    def context(i, g):
        dve.wait_ge(a.values_done, at("values_done", 2 * i + g + 1))
        dve.wait_ge(a.inv_ready, at("inv_ready", 2 * i + g + 1))
        nc.vector.tensor_tensor(a.ctx[g][:, :], k.bank_u[0:k.F, :], a.inv[g][:, :], ALU.mult).then_inc(a.ctx_ready, 1)

    def leaky(i, g):
        dve.wait_ge(a.biased_ready, at("biased_ready", 2 * i + g + 1))
        rows = k.F if insts[i] == OUT else P
        nc.vector.scalar_tensor_tensor(out=a.leaky[0:rows, :], in0=a.biased[0:rows, :], scalar=0.01, in1=a.biased[0:rows, :],
                                       op0=ALU.mult, op1=ALU.max).then_inc(a.leaky_ready, 1)

    def slot(step):
        i, c = divmod(step, 8)
        if c == 0 and i >= 1:
            context(i - 1, 0)
        if c == 4 and i >= 1:
            context(i - 1, 1)
        if c in (1, 5) and i >= 1:
            leaky(i - 1, c // 4)
        for m, (st, kind, j, h) in enumerate(slots):
            if st != step or kind in ("sums", "head"):
                continue
            inst = insts[j]
            if kind == "project":
                n = order.index(inst)
                dve.wait_ge(a.keys_hi_ready, at("keys_hi_ready", 2 * n + h + 1))
                nc.vector.tensor_tensor(a.keys_lo[n % 2][:, h * 512:(h + 1) * 512], k.bank_m[:, :],
                                        f32(a.keys_hi[n % 2][:, h * 512:(h + 1) * 512]), ALU.subtract).then_inc(a.keys_ready, 1)
            elif kind == "mix":
                dve.wait_ge(a.slot_done, at("slot_done", m + 1))
                acc = a.h2[:, h * 512:(h + 1) * 512]
                if inst == order[0]:
                    nc.vector.tensor_copy(acc, k.bank_m[:, :]).then_inc(a.mixed, 1)
                else:
                    nc.vector.tensor_tensor(acc, acc, k.bank_m[:, :], ALU.add).then_inc(a.mixed, 1)
                dve.wait_ge(a.mixed, at("mixed", 2 * order.index(inst) + h + 1))
            else:
                dve.wait_ge(a.slot_done, at("slot_done", m + 1))
                slot_b = bass.ds(b, 1) if not isinstance(b, int) else slice(b, b + 1)
                nc.vector.tensor_copy(a.delta[:, slot_b, 4 * h:4 * h + 4, :].rearrange("p b c f -> p (b c) f"),
                                      k.bank_m[:, :].rearrange("p (c f) -> p c f", f=P)[:, :, 0:k.F]).then_inc(a.out_stored, 1)
        if c == 5 and 0 <= i < NI:
            rinv(i, 0)
        if c == 7 and 0 <= i < NI:
            rinv(i, 1)

    if insts[0] != OUT:
        nc.vector.tensor_copy(a.v[:, :, :].rearrange("p c (t f) -> p c t f", t=2),
                              k.xn[:, :, bass.ds(b, 1), :].broadcast_to([P, k.NC, 2, k.F])).then_inc(a.v_ready, 1)
        dve.wait_ge(a.xt_hi_ready, at("xt_hi_ready", 1))
        nc.vector.tensor_tensor(a.xt[k.F:P, :], k.wide[0][k.F:P, :], f32(a.xt[k.F:P, :]), ALU.subtract).then_inc(a.xt_lo_ready, 1)
        slot(-1)
    dve.wait_ge(a.ko_hi_ready, at("ko_hi_ready", 1))
    nc.vector.tensor_copy(a.xo[0:k.F, :], f32(a.ko_hi[0:k.F, :])).then_inc(a.xo_hi_ready, 1)
    nc.vector.tensor_tensor(a.ko_lo[:, :], a.h2[:, :], f32(a.ko_hi[:, :]), ALU.subtract).then_inc(a.ko_lo_ready, 1)
    dve.wait_ge(a.ko_lo_ready, at("ko_lo_ready", 1))
    nc.vector.tensor_copy(a.xo[k.F:P, :], f32(a.ko_lo[k.F:P, :])).then_inc(a.xo_lo_ready, 1)
    shifted_scores(0)
    for step in range(ST + 7):
        if step + 1 < ST:
            shifted_scores(step + 1)
        slot(step)


def graph_attention(nc, k, adj, Wh, bh, W_out, b_out):
    NC, B, N, F, HEADS = k.NC, k.B, k.N, k.F, Wh.shape[0]
    with ExitStack() as ctx:
        def sb(n, s, d=F32):
            return ctx.enter_context(nc.sbuf_tensor("l2_" + n, s, d))

        def sem(n):
            return k.sem("l2_" + n)

        a = Ctx()
        a.gram_hi, a.gram_lo = sb("gram_hi", [P, HEADS, P], F32R), sb("gram_lo", [P, HEADS, P], F32R)
        a.wh, a.wo = sb("wh", [F, HEADS, P]), sb("wo", [P, HEADS, 2, F])
        a.bh, a.b_out = sb("bh", [P, HEADS]), sb("b_out", [F, 1])
        a.v, a.vo = sb("v", [P, NC, P]), sb("vo", [P, NC, P])
        a.xt, a.xo = sb("xt", [P, N], F32R), sb("xo", [P, N], F32R)
        a.keys_hi, a.keys_lo = ([sb(f"keys_{w}{i}", [P, N], F32R) for i in range(2)] for w in ("hi", "lo"))
        a.ko_hi, a.ko_lo = sb("ko_hi", [P, N], F32R), sb("ko_lo", [P, N], F32R)
        a.scaled_scores, a.fill = sb("scaled_scores", [P, N]), sb("fill", [P, N])
        a.neg_scores = [sb(f"neg_scores{i}", [P, N]) for i in range(2)]
        a.probs = [sb(f"probs{i}", [P, N]) for i in range(2)]
        a.probsT = [sb(f"probsT{i}", [P, NC, 512]) for i in range(2)]
        a.neg_max, a.sums, a.rinv = sb("neg_max", [P, 16]), sb("sums", [P, 16]), sb("rinv", [P, 16])
        a.inv = [sb(f"inv{i}", [F, 512]) for i in range(2)]
        a.ctx = [sb(f"ctx{i}", [F, 512]) for i in range(2)]
        a.biased, a.leaky, a.h2 = sb("biased", [P, 512]), sb("leaky", [P, 512]), sb("h2", [P, N])
        a.delta = k.delta
        whT = sb("whT", [P, HEADS, 2, F])

        insts = [0, OUT] + list(range(1, HEADS))
        ni, nh = len(insts), HEADS
        per = {"keys_ready": 2 * nh, "keys_hi_ready": 2 * nh, "inv_ready": 2 * ni, "biased_ready": 2 * ni, "mixed": 2 * nh,
               "out_stored": 2, "xt_lo_ready": 1, "xt_hi_ready": 1, "rinv_ready": 2 * ni, "ctx_ready": 2 * ni,
               "leaky_ready": 2 * ni, "vo_ready": 1, "scaled": 8 * ni, "ko_lo_ready": 1, "xo_lo_ready": 1,
               "probs_ready": 8 * ni, "turned_read": 16 * ni, "v_ready": 1, "turned": 16 * ni, "shifted": 8 * ni,
               "scores_ready": 8 * ni, "filled": 8 * ni, "values_done": 2 * ni, "slot_done": len(attention_slots(insts)),
               "xt_in_psum": 1, "vo_in_psum": 1, "ko_hi_ready": 1, "xo_hi_ready": 1}
        a.keys_ready, a.keys_hi_ready, a.inv_ready, a.biased_ready, a.mixed, a.out_stored = (
            sem(n) for n in ("keys_ready", "keys_hi_ready", "inv_ready", "biased_ready", "mixed", "out_stored"))
        a.xt_lo_ready, a.xt_hi_ready, a.rinv_ready, a.ctx_ready, a.leaky_ready, a.vo_ready = (
            sem(n) for n in ("xt_lo_ready", "xt_hi_ready", "rinv_ready", "ctx_ready", "leaky_ready", "vo_ready"))
        a.scaled, a.ko_lo_ready, a.xo_lo_ready, a.probs_ready, a.turned_read, a.v_ready = (
            sem(n) for n in ("scaled", "ko_lo_ready", "xo_lo_ready", "probs_ready", "turned_read", "v_ready"))
        a.turned, a.shifted, a.scores_ready, a.filled, a.values_done, a.slot_done = (
            sem(n) for n in ("turned", "shifted", "scores_ready", "filled", "values_done", "slot_done"))
        a.xt_in_psum, a.vo_in_psum, a.ko_hi_ready, a.xo_hi_ready = (
            sem(n) for n in ("xt_in_psum", "vo_in_psum", "ko_hi_ready", "xo_hi_ready"))
        adj_loaded, w_loaded, h2_zeroed, whT_in_psum, whT_ready, gram_in_psum, gram_hi_ready, gram_ready = (
            sem(n) for n in ("adj_loaded", "w_loaded", "h2_zeroed", "whT_in_psum", "whT_ready", "gram_in_psum", "gram_hi_ready", "gram_ready"))

        def counted(b):
            return lambda name, n: b * per[name] + n

        with nc.Block() as block:
            @block.sync
            def _(sp):
                sp.dma_start(a.wh[:, :, :], Wh.rearrange("h c d -> c h d")).then_inc(w_loaded, 16)
                for t in range(2):
                    sp.dma_start(a.wo[:, :, t, :], W_out.rearrange("(h d) o -> d h o", d=P)).then_inc(w_loaded, 16)
                sp.dma_start(a.bh[:, :], bh.rearrange("h d -> d h"), allow_slow_non_contiguous=True).then_inc(w_loaded, 16)
                sp.dma_start(a.b_out[:, :], b_out.rearrange("(o a) -> o a", a=1), allow_slow_non_contiguous=True).then_inc(w_loaded, 16)
                for c in range(NC):
                    sp.dma_start(k.adj[:, c, :], adj[c * P:(c + 1) * P, :]).then_inc(adj_loaded, 16)

            @block.tensor
            def _(pe):
                pe.wait_ge(w_loaded, 80)
                for h in range(HEADS):
                    last = nc.tensor.transpose(k.bank_u[:, h * F:(h + 1) * F], a.wh[:, h, :], k.ident[0:F, 0:F])
                last.then_inc(whT_in_psum, 1)
                pe.wait_ge(whT_ready, 2)
                for h in range(HEADS):
                    w = whT[:, h, :, :].rearrange("p t c -> p (t c)")
                    last = nc.tensor.matmul(k.wide[0][:, h * P:(h + 1) * P], w, w, start=True, stop=True)
                last.then_inc(gram_in_psum, 1)

            @block.scalar
            def _(act):
                act.wait_ge(whT_in_psum, 1)
                for t in range(2):
                    nc.scalar.activation(whT[:, :, t, :], k.bank_u[:, :].rearrange("p (h c) -> p h c", c=F), ACT.Copy).then_inc(whT_ready, 1)
                act.wait_ge(gram_in_psum, 1)
                nc.scalar.activation(a.gram_hi[:, :, :].rearrange("p h c -> p (h c)"), k.wide[0][:, :], ACT.Copy).then_inc(gram_hi_ready, 1)
                nc.scalar.preload_act_table(ACT.Exp)

            @block.vector
            def _(dve):
                nc.vector.memset(a.h2[:, :], 0.0).then_inc(h2_zeroed, 1)
                dve.wait_ge(gram_hi_ready, 1)
                nc.vector.tensor_tensor(a.gram_lo[:, :, :].rearrange("p h c -> p (h c)"), k.wide[0][:, :],
                                        f32(a.gram_hi[:, :, :]).rearrange("p h c -> p (h c)"), ALU.subtract).then_inc(gram_ready, 1)
                dve.wait_ge(adj_loaded, 16 * NC)

        with nc.Block() as block:
            @block.tensor
            def _(pe):
                with pe.Fori(0, B) as b:
                    attention_tensor(nc, k, a, pe, insts, b, counted(b))
                attention_tensor(nc, k, a, pe, [OUT], B, counted(B))

            @block.scalar
            def _(act):
                with act.Fori(0, B) as b:
                    attention_scalar(nc, k, a, act, insts, b, counted(b))
                attention_scalar(nc, k, a, act, [OUT], B, counted(B))

            @block.vector
            def _(dve):
                with dve.Fori(0, B) as b:
                    attention_vector(nc, k, a, dve, insts, b, counted(b))
                attention_vector(nc, k, a, dve, [OUT], B, counted(B))



def industry_messages(nc, k, W_ind, ind_dram):
    NC, B, F, N = k.NC, k.B, k.F, k.N
    BP, HV = B // 2, N // 512
    with ExitStack() as ctx:
        sb = lambda n, s, d=F32: ctx.enter_context(nc.sbuf_tensor("ind_" + n, s, d))
        sem = lambda n: k.sem("ind_" + n)
        k.at_hi, k.at_lo = sb("at_hi", [P, NC, N], F32R), sb("at_lo", [P, NC, N], F32R)
        z = sb("split", [P, NC, 2, B, F], F32R)
        w2, rdeg = sb("w2", [P, P]), sb("rdeg", [P, NC])
        agg = [sb(f"agg{i}", [P, 512]) for i in range(2)]
        ind = [sb(f"ind{i}", [P, 512]) for i in range(2)]
        rdeg_rows = sb("rdeg_rows", [P, N])
        zeroed, w_loaded, transposed, hi_ready, lo_ready, z_hi, z_lo, rdeg_ready, rdeg_in_psum, rdeg_rows_ready = (
            sem(n) for n in ("zeroed", "w_loaded", "transposed", "hi_ready", "lo_ready", "z_hi", "z_lo", "rdeg_ready", "rdeg_in_psum", "rdeg_rows_ready"))
        prod_ready, agg_ready, ind_in_psum, ind_ready = (sem(n) for n in ("prod_ready", "agg_ready", "ind_in_psum", "ind_ready"))
        stored = [sem(f"stored{i}") for i in range(2)]
        prod = [k.bank_u[:, :], k.bank_m[:, :]]
        indp = [k.pair[:, 0:512], k.pair[:, 512:1024]]
        with nc.Block() as block:
            @block.sync
            def _(sp):
                sp.wait_ge(zeroed, 1)
                for i in range(2):
                    sp.dma_start(w2[i * F:(i + 1) * F, i * F:(i + 1) * F], W_ind).then_inc(w_loaded, 16)
                for g in range(BP * HV):
                    bp, half = g // HV, g % HV
                    sp.wait_ge(ind_ready, g + 1)
                    sp.dma_start(ind_dram[2 * bp:2 * bp + 2, :, half * 512:(half + 1) * 512].rearrange("b f n -> (b f) n"),
                                 ind[g % 2][:, :]).then_inc(stored[g % 2], 16)
                for i in range(2):
                    sp.wait_ge(stored[i], 16 * BP * HV // 2)

            @block.gpsimd
            def _(pool):
                nc.gpsimd.memset(w2[:, :], 0.0).then_inc(zeroed, 1)

            @block.tensor
            def _(pe):
                for mc in range(NC):
                    if mc >= 2:
                        pe.wait_ge(lo_ready, mc - 1)
                    for c in range(NC):
                        last = nc.tensor.transpose(k.wide[mc % 2][:, c * P:(c + 1) * P], k.adj[:, c, mc * P:(mc + 1) * P], k.ident[:, :])
                    last.then_inc(transposed, 1)
                pe.wait_ge(rdeg_ready, 2)
                for c in range(NC):
                    last = nc.tensor.matmul(k.pair[:, c * P:(c + 1) * P], rdeg[:, c:c + 1].broadcast_to([P, P]), k.ident[:, :], start=True, stop=True)
                last.then_inc(rdeg_in_psum, 1)
                pe.wait_ge(w_loaded, 32)
                pe.wait_ge(lo_ready, NC)
                pe.wait_ge(z_lo, 1)
                pe.wait_ge(rdeg_rows_ready, 1)

                def message(g):
                    pe.wait_ge(agg_ready, g + 1)
                    if g >= 2:
                        pe.wait_ge(ind_ready, g - 1)
                    nc.tensor.matmul(indp[g % 2], w2[:, :], agg[g % 2][:, :], start=True, stop=True).then_inc(ind_in_psum, 1)

                for g in range(BP * HV):
                    if g >= 2:
                        pe.wait_ge(agg_ready, g - 1)
                    product_transposed(nc, k, pe, z, prod[g % 2], g // HV, g % HV).then_inc(prod_ready, 1)
                    if g >= 1:
                        message(g - 1)
                message(BP * HV - 1)

            @block.scalar
            def _(act):
                nc.scalar.activation(z[:, :, 0, :, :].rearrange("p c b f -> p c (b f)"),
                                     k.xn[:, :, :, :].rearrange("p c b f -> p c (b f)"), ACT.Copy).then_inc(z_hi, 1)
                for mc in range(NC):
                    act.wait_ge(transposed, mc + 1)
                    nc.scalar.activation(k.at_hi[:, mc, :], k.wide[mc % 2][:, :], ACT.Copy).then_inc(hi_ready, 1)
                act.wait_ge(rdeg_in_psum, 1)
                nc.scalar.activation(rdeg_rows[:, :], k.pair[:, :], ACT.Copy).then_inc(rdeg_rows_ready, 1)
                for g in range(BP * HV):
                    act.wait_ge(prod_ready, g + 1)
                    if g >= 2:
                        act.wait_ge(ind_in_psum, g - 1)
                    nc.scalar.activation(agg[g % 2][:, :], prod[g % 2], ACT.Copy).then_inc(agg_ready, 1)

            @block.vector
            def _(dve):
                nc.vector.tensor_scalar(rdeg[:, :], k.deg[:, :], 1.0, None, ALU.max).then_inc(rdeg_ready, 1)
                dve.wait_ge(rdeg_ready, 1)
                nc.vector.reciprocal(rdeg[:, :], rdeg[:, :]).then_inc(rdeg_ready, 1)
                dve.wait_ge(z_hi, 1)
                nc.vector.tensor_tensor(z[:, :, 1, :, :].rearrange("p c b f -> p c (b f)"),
                                        k.xn[:, :, :, :].rearrange("p c b f -> p c (b f)"),
                                        f32(z[:, :, 0, :, :]).rearrange("p c b f -> p c (b f)"), ALU.subtract).then_inc(z_lo, 1)
                for mc in range(NC):
                    dve.wait_ge(hi_ready, mc + 1)
                    nc.vector.tensor_tensor(k.at_lo[:, mc, :], k.wide[mc % 2][:, :], f32(k.at_hi[:, mc, :]), ALU.subtract).then_inc(lo_ready, 1)
                for g in range(BP * HV):
                    dve.wait_ge(ind_in_psum, g + 1)
                    if g >= 2:
                        dve.wait_ge(stored[g % 2], 16 * (g // 2))
                    half = g % HV
                    nc.vector.tensor_tensor(ind[g % 2][:, :], indp[g % 2], rdeg_rows[:, half * 512:(half + 1) * 512], ALU.mult).then_inc(ind_ready, 1)


def hypergraph_attention(nc, k, params, ind_dram):
    H, W, a_node, a_gn, a_ge, fcW, fcb, av = params
    NC, B, F, N, E = k.NC, k.B, k.F, k.N, H.shape[1]
    EP = E // 2
    HS = [slice(0, 512), slice(512, 1024)]
    with ExitStack() as ctx:
        sb = lambda n, s, d=F32: ctx.enter_context(nc.sbuf_tensor("l3_" + n, s, d))
        sem = lambda n: k.sem("l3_" + n)
        w_dup, fcw = sb("w_dup", [F, 2, F]), sb("fcw", [F, P])
        cols = sb("cols", [P, 8])
        h_raw = sb("h_raw", [P, NC, E])
        mask, fill = sb("mask", [P, NC, 2, E]), sb("fill", [P, NC, E])
        maskT, fillT = sb("maskT", [P, N]), sb("fillT", [P, N])
        pick, fold, ones = sb("pick", [P, EP, 2, F], F32R), sb("fold", [P, 2, F]), sb("ones", [F, P])
        dup_ident = sb("dup_ident", [P, E])
        xT, hn = sb("xT", [P, N]), sb("hn", [P, NC, P])
        hT, hsum, beta_s, c_s = ([sb(f"{n}{i}", [P, N], d) for i in range(2)] for n, d in (("hT", F32), ("hsum", F32), ("beta_s", F32R), ("c_s", F32R)))
        agg_e, nagg_e = ([sb(f"{n}{i}", [P, EP]) for i in range(2)] for n in ("agg_e", "nagg_e"))
        t0, t1, t2 = sb("t0", [P, N]), sb("t1", [P, N]), sb("t2", [P, N])
        x2 = t1[:, :].rearrange("p (c f) -> p c f", f=P)
        alphaT = xT[:, :].rearrange("p (c e) -> p c e", e=P)
        small = sb("small", [P, 16])
        aggT = sb("aggT", [P, 2, E])
        agg_less_1, neg_agg = sb("agg_less_1", [P, P]), sb("neg_agg", [P, P])
        agg_min, he, tanh_e = sb("agg_min", [P, E]), sb("he", [P, E]), sb("tanh_e", [P, E])
        beta, gate = sb("beta", [P, N]), sb("gate", [P, N])
        lg, coef = sb("lg", [P, NC, E]), sb("coef", [P, NC, 2, E])
        c8 = sb("c8", [P, 3, NC])
        cT, cbeta = sb("cT", [P, N]), sb("cbeta", [P, N])
        w_t, r_t, e_t = ([sb(f"{n}_{i}", [P, N]) for i in range(3)] for n in ("w", "r", "e"))
        u_t, p_t = ([sb(f"{n}_{i}", [P, N]) for i in range(2)] for n in ("u", "p"))
        LEAD = 3
        fetches = [("beta", e) for e in range(LEAD)]
        for e in range(EP):
            fetches += [("beta", e + LEAD)] * (e + LEAD < EP) + [("c", e)]
        rows_of = {fetch: k.wide[f % 2] for f, fetch in enumerate(fetches)}
        ind = sb("ind", [P, N])
        g = sb("g", [P, N])

        s = Ctx()
        s.loaded, s.consts, s.maskT_in_psum, s.x_ready, s.xT_in_psum, s.xT_ready = (
            sem(n) for n in ("loaded", "consts", "maskT_in_psum", "x_ready", "xT_in_psum", "xT_ready"))
        s.hT_in_psum, s.hn_in_psum, s.hT_ready, s.hn_ready, s.node_logits, s.gate_logits = (
            sem(n) for n in ("hT_in_psum", "hn_in_psum", "hT_ready", "hn_ready", "node_logits", "gate_logits"))
        s.logits_copied, s.gate_copied, s.alpha_step, s.alpha_shifted, s.alpha_exp, s.alpha_ready = (
            sem(n) for n in ("logits_copied", "gate_copied", "alpha_step", "alpha_shifted", "alpha_exp", "alpha_ready"))
        s.alphaT_in_psum, s.alphaT_ready, s.agg_in_psum, s.agg_step, s.agg_exp, s.he_ready = (
            sem(n) for n in ("alphaT_in_psum", "alphaT_ready", "agg_in_psum", "agg_step", "agg_exp", "he_ready"))
        s.edge_in_psum, s.tanh_e_ready, s.half_age_ready, s.score_in_psum, s.gate_tanh, s.beta_ready = (
            sem(n) for n in ("edge_in_psum", "tanh_e_ready", "half_age_ready", "score_in_psum", "gate_tanh", "beta_ready"))
        s.beta_hi, s.beta_split, s.coef_step, s.coef_exp, s.coef_masked, s.coef_rinv = (
            sem(n) for n in ("beta_hi", "beta_split", "coef_step", "coef_exp", "coef_masked", "coef_rinv"))
        s.coef_half, s.coef_ready, s.cT_in_psum, s.cT_ready, s.c_split, s.cbeta_ready = (
            sem(n) for n in ("coef_half", "coef_ready", "cT_in_psum", "cT_ready", "c_split", "cbeta_ready"))
        s.hsum_in_psum, s.hsum_ready, s.closed, s.beta_rows, s.c_rows, s.w_done = (
            sem(n) for n in ("hsum_in_psum", "hsum_ready", "closed", "beta_rows", "c_rows", "w_done"))
        s.r_done, s.e_done, s.u_done, s.p_done, s.summed, s.g_ready = (
            sem(n) for n in ("r_done", "e_done", "u_done", "p_done", "summed", "g_ready"))
        s.ind_loaded, s.tanh_i_in_psum, s.tanh_i_ready, s.tanh_g_in_psum, s.tanh_g_ready, s.diff_ready = (
            sem(n) for n in ("ind_loaded", "tanh_i_in_psum", "tanh_i_ready", "tanh_g_in_psum", "tanh_g_ready", "diff_ready"))
        s.mix_in_psum, s.mix_tanh, s.mix_step, s.outT_ready, s.out_in_psum, s.out_stored = (
            sem(n) for n in ("mix_in_psum", "mix_tanh", "mix_step", "outT_ready", "out_in_psum", "out_stored"))

        with nc.Block() as block:
            @block.sync
            def _(sp):
                for i in range(2):
                    sp.dma_start(w_dup[:, i, :], W).then_inc(s.loaded, 16)
                sp.dma_start(fcw[:, :], fcW).then_inc(s.loaded, 16)
                for i, v in enumerate((a_node, a_gn, a_ge, fcb, av)):
                    sp.dma_start(cols[0:v.shape[0], i:i + 1], v.rearrange("(f a) -> f a", a=1), allow_slow_non_contiguous=True).then_inc(s.loaded, 16)
                sp.dma_start(h_raw[:, :, :], H.rearrange("(c p) e -> p c e", p=P)).then_inc(s.loaded, 16)

            @block.vector
            def _(dve):
                dve.wait_ge(s.loaded, 16 * 9)
                nc.vector.tensor_scalar(cols[:, 5:6], cols[:, 4:5], -1.0, None, ALU.mult).then_inc(s.consts, 1)
                for i in range(2):
                    nc.vector.tensor_scalar(mask[:, :, i, :], h_raw[:, :, :], 0.0, None, ALU.is_gt).then_inc(s.consts, 1)
                nc.vector.memset(ones[:, :], 1.0).then_inc(s.consts, 1)
                nc.vector.tensor_tensor(dup_ident[:, :], k.ident[:, 0:E], k.ident[:, E:2 * E], ALU.add).then_inc(s.consts, 1)
                dve.wait_ge(s.consts, 5)
                nc.vector.tensor_scalar(fill[:, :, :], mask[:, :, 0, :], -1.0, -NEG, ALU.add, ALU.mult).then_inc(s.consts, 1)
                for i in range(2):
                    nc.vector.tensor_copy(fold[:, i, :], dup_ident[:, :]).then_inc(s.consts, 1)
                nc.vector.tensor_copy(pick[:, :, :, :], dup_ident[:, :].rearrange("p (j e) -> p e j", j=2).unsqueeze(3).broadcast_to([P, EP, 2, F])).then_inc(s.consts, 1)
                dve.wait_ge(s.maskT_in_psum, 1)
                nc.vector.tensor_copy(maskT[:, :], k.wide[0][:, :]).then_inc(s.consts, 1)
                dve.wait_ge(s.consts, 10)
                nc.vector.tensor_scalar(fillT[:, :], maskT[:, :], -1.0, -NEG, ALU.add, ALU.mult).then_inc(s.consts, 1)

            @block.tensor
            def _(pe):
                pe.wait_ge(s.consts, 5)
                for c in range(NC):
                    last = nc.tensor.transpose(k.wide[0][:, c * P:(c + 1) * P], mask[:, c, :, :].rearrange("p t e -> p (t e)"), k.ident[:, :])
                last.then_inc(s.maskT_in_psum, 1)

            @block.scalar
            def _(act):
                nc.scalar.preload_act_table(ACT.Exp)

        SLOT_AT = {"score_ind": 0, "score_g": 2, "mix": 4, "store": 6, "x": 8, "h": 10, "h_nodes": 12, "logits": 14, "gates": 15,
                   "alphaT": 17, "agg": 19, "elu_agg": 20, "edges": 22, "scores": 24, "coef": 25, "coefT": 27, "hsum": 29}
        FINISH, PREPARE = list(SLOT_AT)[:4], list(SLOT_AT)[4:]
        spare = k.spare

        def run_slots(slot, e, lag, last, following):
            for name, at in SLOT_AT.items():
                if at + lag == e or (e == EP and at + lag >= EP):
                    batch = last if name in FINISH else following
                    if batch is not None:
                        slot(name, batch)

        def over_batches(engine, prepare, batch, finish):
            prepare(0, 0)
            batch(0, 0, None, 1)
            with engine.Fori(1, B - 2, step=2) as b:
                batch(b, 1, b - 1, b + 1)
                batch(b + 1, 0, b, b + 2)
            batch(B - 1, 1, B - 2, None)
            finish(B - 1)

        w_flat = w_dup[:, :, :].rearrange("p t f -> p (t f)")

        with nc.Block() as block:
            @block.sync
            def _(sp):
                def load(b):
                    for i in range(2):
                        sp.dma_start(ind[i * F:(i + 1) * F, :], ind_dram[bass.ds(b, 1), :, :].rearrange("b f n -> (b f) n")).then_inc(s.ind_loaded, 16)

                load(0)
                with sp.Fori(1, B) as b:
                    sp.wait_ge(s.outT_ready, b)
                    load(b)

            @block.tensor
            def _(pe):
                def spread_halves(stationary, moving):
                    for hs in HS:
                        last = nc.tensor.matmul(spare[:, hs], stationary, moving[:, hs], start=True, stop=True)
                    return last

                def slot(name, b, o):
                    if name == "score_ind":
                        pe.wait_ge(s.hsum_ready, b + 1)
                        pe.wait_ge(s.ind_loaded, b * 32 + 32)
                        spread_halves(fcw[:, :], ind[0:F, :]).then_inc(s.tanh_i_in_psum, 1)
                    elif name == "score_g":
                        pe.wait_ge(s.tanh_i_ready, b + 1)
                        pe.wait_ge(s.g_ready, b + 1)
                        spread_halves(fcw[:, :], g[0:F, :]).then_inc(s.tanh_g_in_psum, 1)
                    elif name == "mix":
                        pe.wait_ge(s.diff_ready, b + 1)
                        spread_halves(cols[:, 4:5].broadcast_to([P, P]), t2).then_inc(s.mix_in_psum, 1)
                    elif name == "store":
                        pe.wait_ge(s.outT_ready, b + 1)
                        for c in range(NC):
                            last = nc.tensor.transpose(spare[:, c * P:(c + 1) * P], t1[:, c * P:(c + 1) * P], k.ident[:, :])
                        last.then_inc(s.out_in_psum, 1)
                    elif name == "x":
                        pe.wait_ge(s.x_ready, b + 1)
                        for c in range(NC):
                            last = nc.tensor.transpose(spare[:, c * P:(c + 1) * P], x2[:, c, :], k.ident[:, :])
                        last.then_inc(s.xT_in_psum, 1)
                    elif name == "h":
                        pe.wait_ge(s.xT_ready, b + 1)
                        spread_halves(w_flat, xT[0:F, :]).then_inc(s.hT_in_psum, 1)
                    elif name == "h_nodes":
                        pe.wait_ge(s.hT_ready, b + 1)
                        for c in range(NC):
                            last = nc.tensor.matmul(spare[:, c * P:(c + 1) * P], xT[0:F, c * P:(c + 1) * P], w_flat, start=True, stop=True)
                        last.then_inc(s.hn_in_psum, 1)
                    elif name == "logits":
                        pe.wait_ge(s.hn_ready, b + 1)
                        spread_halves(cols[0:F, 0:1].broadcast_to([F, P]), hT[o][0:F, :]).then_inc(s.node_logits, 1)
                    elif name == "gates":
                        pe.wait_ge(s.logits_copied, b + 1)
                        spread_halves(cols[0:F, 1:2].broadcast_to([F, P]), hT[o][0:F, :]).then_inc(s.gate_logits, 1)
                    elif name == "alphaT":
                        pe.wait_ge(s.gate_copied, b + 1)
                        pe.wait_ge(s.alpha_ready, b + 1)
                        for c in range(NC):
                            last = nc.tensor.transpose(spare[:, c * P:(c + 1) * P], t2[:, c * P:(c + 1) * P], k.ident[:, :])
                        last.then_inc(s.alphaT_in_psum, 1)
                    elif name == "agg":
                        pe.wait_ge(s.alphaT_ready, b + 1)
                        for c in range(NC):
                            nc.tensor.matmul(spare[:, 0:E], hn[:, c, :], alphaT[:, c, 0:E], start=c == 0, stop=c == NC - 1)
                        for c in range(NC):
                            last = nc.tensor.matmul(spare[:, 512:512 + P], alphaT[:, c, :], hn[:, c, :], start=c == 0, stop=c == NC - 1)
                        last.then_inc(s.agg_in_psum, 1)
                    elif name == "edges":
                        pe.wait_ge(s.he_ready, b + 1)
                        nc.tensor.matmul(spare[:, 0:E], fcw[:, :], he[0:F, :], start=True, stop=True)
                        nc.tensor.matmul(spare[:, 512:513], aggT[0:F, :, :].rearrange("p t e -> p (t e)"), cols[0:F, 2:3], start=True, stop=True).then_inc(s.edge_in_psum, 1)
                    elif name == "scores":
                        pe.wait_ge(s.half_age_ready, b + 1)
                        pe.wait_ge(s.tanh_e_ready, b + 1)
                        nc.tensor.matmul(spare[:, 0:E], cols[:, 4:5].broadcast_to([P, P]), tanh_e[:, :], start=True, stop=True).then_inc(s.score_in_psum, 1)
                    elif name == "coefT":
                        pe.wait_ge(s.coef_ready, b + 1)
                        for c in range(NC):
                            last = nc.tensor.transpose(spare[:, c * P:(c + 1) * P], coef[:, c, :, :].rearrange("p t e -> p (t e)"), k.ident[:, :])
                        last.then_inc(s.cT_in_psum, 1)
                    elif name == "hsum":
                        pe.wait_ge(s.cbeta_ready, b + 1)
                        spread_halves(ones[:, :], cbeta[0:E, :]).then_inc(s.hsum_in_psum, 1)

                def batch(b, o, last_b, next_b):
                    def spread(f):
                        kind, e = fetches[f]
                        if f >= 2:
                            before, e2 = fetches[f - 2]
                            if before == "beta":
                                pe.wait_ge(s.w_done, b * EP + e2 + 1)
                            else:
                                pe.wait_ge(s.p_done, b * EP + e2 + 1)
                        src = beta_s[o] if kind == "beta" else c_s[o]
                        for hs in HS:
                            last = nc.tensor.matmul(rows_of[kind, e][:, hs], pick[:, e, :, :].rearrange("p j f -> p (j f)"), src[:, hs], start=True, stop=True)
                        last.then_inc(s.beta_rows if kind == "beta" else s.c_rows, 1)

                    def add_up(e, half):
                        if half == 0:
                            pe.wait_ge(s.p_done, b * EP + e + 1)
                        last = nc.tensor.matmul(k.pair[:, HS[half]], fold[:, :, :].rearrange("p t f -> p (t f)"), p_t[e % 2][:, HS[half]], start=False, stop=e == EP - 1)
                        if half == 1:
                            last.then_inc(s.summed, 1)

                    pe.wait_ge(s.beta_split, b + 1)
                    pe.wait_ge(s.c_split, b + 1)
                    for f in range(LEAD + 1):
                        spread(f)
                    pe.wait_ge(s.cbeta_ready, b + 1)
                    if last_b is not None:
                        pe.wait_ge(s.g_ready, b)
                    for hs in HS:
                        nc.tensor.matmul(k.pair[:, hs], agg_less_1[0:E, :], cT[0:E, hs], start=True, stop=False)
                        last = nc.tensor.matmul(k.pair[:, hs], neg_agg[0:E, :], cbeta[0:E, hs], start=False, stop=False)
                    last.then_inc(s.closed, 1)
                    for e in range(EP):
                        spread(fetches.index(("c", e)))
                        if e >= 1:
                            add_up(e - 1, 0)
                        if e + LEAD + 1 < EP:
                            spread(fetches.index(("beta", e + LEAD + 1)))
                        if e >= 1:
                            add_up(e - 1, 1)
                        run_slots(lambda name, bb: slot(name, bb, 1 - o), e, 0, last_b, next_b)
                    for half in range(2):
                        add_up(EP - 1, half)

                over_batches(pe, lambda b, o: [slot(n, b, o) for n in PREPARE], batch, lambda b: [slot(n, b, 1) for n in FINISH])

            @block.scalar
            def _(act):
                def slot(name, b, o):
                    if name == "score_ind":
                        act.wait_ge(s.tanh_i_in_psum, b + 1)
                        nc.scalar.activation(t0[:, :], spare[:, :], ACT.Tanh, bias=cols[:, 3:4]).then_inc(s.tanh_i_ready, 1)
                    elif name == "score_g":
                        act.wait_ge(s.tanh_g_in_psum, b + 1)
                        nc.scalar.activation(t1[:, :], spare[:, :], ACT.Tanh, bias=cols[:, 3:4]).then_inc(s.tanh_g_ready, 1)
                    elif name == "mix":
                        act.wait_ge(s.mix_in_psum, b + 1)
                        nc.scalar.activation(t0[:, :], spare[:, :], ACT.Tanh, scale=0.5).then_inc(s.mix_tanh, 1)
                    elif name == "x":
                        act.wait_ge(s.xT_in_psum, b + 1)
                        nc.scalar.activation(xT[:, :], spare[:, :], ACT.Copy).then_inc(s.xT_ready, 1)
                    elif name == "h":
                        act.wait_ge(s.hT_in_psum, b + 1)
                        nc.scalar.activation(hT[o][:, :], spare[:, :], ACT.Copy).then_inc(s.hT_ready, 1)
                    elif name == "logits":
                        act.wait_ge(s.node_logits, b + 1)
                        nc.scalar.activation(t0[:, :], spare[:, :], ACT.Copy).then_inc(s.logits_copied, 1)
                    elif name == "gates":
                        act.wait_ge(s.gate_logits, b + 1)
                        nc.scalar.activation(gate[:, :], spare[:, :], ACT.Copy).then_inc(s.gate_copied, 1)
                        act.wait_ge(s.alpha_shifted, b + 1)
                        nc.scalar.activation(t1[:, :], t0[:, :], ACT.Exp, bias=small[:, 0:1], scale=-1.0, accum_out=small[:, 1:2]).then_inc(s.alpha_exp, 1)
                    elif name == "alphaT":
                        act.wait_ge(s.alphaT_in_psum, b + 1)
                        nc.scalar.activation(xT[:, :], spare[:, :], ACT.Copy).then_inc(s.alphaT_ready, 1)
                    elif name == "elu_agg":
                        act.wait_ge(s.agg_step, b * 7 + 7)
                        nc.scalar.activation(agg_min[:, :], agg_min[:, :], ACT.Exp).then_inc(s.agg_exp, 1)
                    elif name == "edges":
                        act.wait_ge(s.edge_in_psum, b + 1)
                        nc.scalar.activation(tanh_e[:, :], spare[:, 0:E], ACT.Tanh, bias=cols[:, 3:4]).then_inc(s.tanh_e_ready, 1)
                    elif name == "scores":
                        act.wait_ge(s.half_age_ready, b + 1)
                        nc.scalar.activation(beta[:, :], gate[:, :], ACT.Tanh, bias=small[:, 3:4], scale=0.5).then_inc(s.gate_tanh, 1)
                    elif name == "coef":
                        act.wait_ge(s.coef_step, b * 4 + 4)
                        nc.scalar.activation(lg[:, :, :], lg[:, :, :], ACT.Exp).then_inc(s.coef_exp, 1)
                        act.wait_ge(s.beta_ready, b + 1)
                        nc.scalar.activation(beta_s[o][:, :], beta[:, :], ACT.Copy).then_inc(s.beta_hi, 1)
                    elif name == "coefT":
                        act.wait_ge(s.cT_in_psum, b + 1)
                        nc.scalar.activation(c_s[o][:, :], spare[:, :], ACT.Copy).then_inc(s.cT_ready, 1)
                        nc.scalar.activation(cT[:, :], spare[:, :], ACT.Copy).then_inc(s.cT_ready, 1)

                def batch(b, o, last_b, next_b):
                    for e in range(EP):
                        act.wait_ge(s.w_done, b * EP + e + 1)
                        if e >= 3:
                            act.wait_ge(s.u_done, b * EP + e - 2)
                        nc.scalar.activation(r_t[e % 3][:, :], w_t[e % 3][:, :], ACT.Relu, bias=nagg_e[o][:, e:e + 1], scale=-1.0).then_inc(s.r_done, 1)
                        act.wait_ge(s.r_done, b * EP + e + 1)
                        nc.scalar.activation(e_t[e % 3][:, :], r_t[e % 3][:, :], ACT.Exp, scale=-1.0).then_inc(s.e_done, 1)
                        run_slots(lambda name, bb: slot(name, bb, 1 - o), e, 3, last_b, next_b)
                    run_slots(lambda name, bb: slot(name, bb, 1 - o), EP, 3, last_b, next_b)

                over_batches(act, lambda b, o: [slot(n, b, o) for n in PREPARE], batch, lambda b: [slot(n, b, 1) for n in FINISH])

            @block.gpsimd
            def _(pool):
                with pool.Fori(0, B) as b:
                    for e in range(EP):
                        pool.wait_ge(s.e_done, b * EP + e + 1)
                        if e >= 2:
                            pool.wait_ge(s.p_done, b * EP + e - 1)
                        nc.gpsimd.tensor_tensor(u_t[e % 2][:, :], r_t[e % 3][:, :], e_t[e % 3][:, :], ALU.add).then_inc(s.u_done, 1)

            @block.vector
            def _(dve):
                def make_x2(b):
                    nc.vector.tensor_copy(x2.rearrange("p c (t f) -> p c t f", t=2),
                                          k.xn[:, :, bass.ds(b, 1), :].broadcast_to([P, NC, 2, F])).then_inc(s.x_ready, 1)

                def slot(name, b, o):
                    if name == "score_g":
                        dve.wait_ge(s.tanh_g_ready, b + 1)
                        nc.vector.tensor_tensor(t2[:, :], t1[:, :], t0[:, :], ALU.subtract).then_inc(s.diff_ready, 1)
                    elif name == "mix":
                        dve.wait_ge(s.diff_ready, b + 1)
                        dve.wait_ge(s.ind_loaded, b * 32 + 32)
                        nc.vector.tensor_tensor(t1[:, :], ind[:, :], g[:, :], ALU.subtract).then_inc(s.mix_step, 1)
                        dve.wait_ge(s.mix_tanh, b + 1)
                        nc.vector.tensor_scalar(t2[:, :], t0[:, :], -0.5, 0.5, ALU.mult, ALU.add).then_inc(s.mix_step, 1)
                        dve.wait_ge(s.mix_step, b * 3 + 2)
                        nc.vector.tensor_tensor(t0[:, :], t1[:, :], t2[:, :], ALU.mult).then_inc(s.mix_step, 1)
                        dve.wait_ge(s.mix_step, b * 3 + 3)
                        nc.vector.tensor_tensor(t1[:, :], t0[:, :], g[:, :], ALU.add).then_inc(s.outT_ready, 1)
                    elif name == "store":
                        dve.wait_ge(s.out_in_psum, b + 1)
                        nc.vector.tensor_copy(k.delta[:, bass.ds(b, 1), :, :].rearrange("p b c f -> p (b c) f"),
                                              spare[:, :].rearrange("p (c f) -> p c f", f=P)[:, :, 0:F]).then_inc(s.out_stored, 1)
                    elif name == "h_nodes":
                        dve.wait_ge(s.hn_in_psum, b + 1)
                        nc.vector.tensor_copy(hn[:, :, :].rearrange("p c f -> p (c f)"), spare[:, :]).then_inc(s.hn_ready, 1)
                    elif name == "logits":
                        dve.wait_ge(s.logits_copied, b + 1)
                        nc.vector.scalar_tensor_tensor(out=t1[:, :], in0=t0[:, :], scalar=0.2, in1=t0[:, :], op0=ALU.mult, op1=ALU.max).then_inc(s.alpha_step, 1)
                        dve.wait_ge(s.alpha_step, b * 4 + 1)
                        nc.vector.tensor_tensor(t2[:, :], t1[:, :], maskT[:, :], ALU.mult).then_inc(s.alpha_step, 1)
                        dve.wait_ge(s.alpha_step, b * 4 + 2)
                        nc.vector.memset(small[:, 4:5], 0.0).then_inc(s.alpha_step, 1)
                        nc.vector.tensor_tensor_reduce(out=t0[:, :], in0=t2[:, :], in1=fillT[:, :], scale=-1.0, scalar=3.0e38,
                                                       op0=ALU.add, op1=ALU.min, accum_out=small[:, 0:1]).then_inc(s.alpha_shifted, 1)
                    elif name == "gates":
                        dve.wait_ge(s.alpha_exp, b + 1)
                        nc.vector.reciprocal(small[:, 2:3], small[:, 1:2]).then_inc(s.alpha_step, 1)
                        dve.wait_ge(s.alpha_step, b * 4 + 4)
                        nc.vector.tensor_scalar(t2[:, :], t1[:, :], small[:, 2:3], None, ALU.mult).then_inc(s.alpha_ready, 1)
                    elif name == "agg":
                        if not (isinstance(b, int) and b == 0):
                            dve.wait_ge(s.closed, b)
                        dve.wait_ge(s.agg_in_psum, b + 1)
                        for i in range(2):
                            nc.vector.tensor_copy(aggT[:, i, :], spare[:, 0:E]).then_inc(s.agg_step, 1)
                        nc.vector.tensor_scalar(agg_less_1[:, :], spare[:, 512:512 + P], -1.0, None, ALU.add).then_inc(s.agg_step, 1)
                        nc.vector.tensor_scalar(neg_agg[:, :], spare[:, 512:512 + P], -1.0, None, ALU.mult).then_inc(s.agg_step, 1)
                        for i in range(2):
                            nc.vector.tensor_copy(agg_e[o][i * F:(i + 1) * F, :], spare[i * F:(i + 1) * F, i * EP:(i + 1) * EP]).then_inc(s.agg_step, 1)
                        nc.vector.tensor_scalar(agg_min[:, :], spare[:, 0:E], 0.0, None, ALU.min).then_inc(s.agg_step, 1)
                    elif name == "elu_agg":
                        dve.wait_ge(s.agg_exp, b + 1)
                        nc.vector.scalar_tensor_tensor(out=he[:, :], in0=aggT[:, 0, :], scalar=0.0, in1=agg_min[:, :], op0=ALU.max, op1=ALU.add).then_inc(s.coef_step, 1)
                        nc.vector.tensor_scalar(nagg_e[o][:, :], agg_e[o][:, :], -1.0, None, ALU.mult).then_inc(s.coef_step, 1)
                        dve.wait_ge(s.coef_step, b * 4 + 1)
                        nc.vector.tensor_scalar(he[:, :], he[:, :], -1.0, None, ALU.add).then_inc(s.he_ready, 1)
                    elif name == "edges":
                        dve.wait_ge(s.edge_in_psum, b + 1)
                        nc.vector.tensor_scalar(small[:, 3:4], spare[:, 512:513], 0.5, None, ALU.mult).then_inc(s.half_age_ready, 1)
                    elif name == "scores":
                        dve.wait_ge(s.score_in_psum, b + 1)
                        nc.vector.tensor_tensor(lg[:, :, :], mask[:, :, 0, :], spare[:, 0:E].unsqueeze(1).broadcast_to([P, NC, E]), ALU.mult).then_inc(s.coef_step, 1)
                        dve.wait_ge(s.coef_step, b * 4 + 3)
                        nc.vector.tensor_tensor(coef[:, :, 0, :], lg[:, :, :], fill[:, :, :], ALU.add).then_inc(s.coef_masked, 1)
                        dve.wait_ge(s.coef_masked, b * 3 + 1)
                        nc.vector.reduce_max(c8[:, 0, :], coef[:, :, 0, :], axis=AX_X).then_inc(s.coef_masked, 1)
                        dve.wait_ge(s.coef_masked, b * 3 + 2)
                        nc.vector.tensor_tensor(lg[:, :, :], coef[:, :, 0, :], c8[:, 0, :].unsqueeze(2).broadcast_to([P, NC, E]), ALU.subtract).then_inc(s.coef_step, 1)
                        dve.wait_ge(s.gate_tanh, b + 1)
                        nc.vector.tensor_scalar(beta[:, :], beta[:, :], 0.5, 0.5, ALU.mult, ALU.add).then_inc(s.beta_ready, 1)
                    elif name == "coef":
                        dve.wait_ge(s.coef_exp, b + 1)
                        nc.vector.reduce_sum(c8[:, 1, :], lg[:, :, :], axis=AX_X).then_inc(s.coef_masked, 1)
                        dve.wait_ge(s.coef_masked, b * 3 + 3)
                        nc.vector.reciprocal(c8[:, 2, :], c8[:, 1, :]).then_inc(s.coef_rinv, 1)
                        dve.wait_ge(s.coef_rinv, b + 1)
                        nc.vector.tensor_tensor(coef[:, :, 0, :], lg[:, :, :], c8[:, 2, :].unsqueeze(2).broadcast_to([P, NC, E]), ALU.mult).then_inc(s.coef_half, 1)
                        nc.vector.tensor_tensor(coef[:, :, 1, :], lg[:, :, :], c8[:, 2, :].unsqueeze(2).broadcast_to([P, NC, E]), ALU.mult).then_inc(s.coef_ready, 1)
                        dve.wait_ge(s.beta_hi, b + 1)
                        nc.vector.tensor_tensor(beta_s[o][E:P, :], beta[E:P, :], f32(beta_s[o][E:P, :]), ALU.subtract).then_inc(s.beta_split, 1)
                    elif name == "coefT":
                        dve.wait_ge(s.cT_ready, b * 2 + 2)
                        nc.vector.tensor_tensor(cbeta[:, :], cT[:, :], beta[:, :], ALU.mult).then_inc(s.cbeta_ready, 1)
                        nc.vector.tensor_tensor(c_s[o][E:P, :], cT[E:P, :], f32(c_s[o][E:P, :]), ALU.subtract).then_inc(s.c_split, 1)
                    elif name == "hsum":
                        dve.wait_ge(s.hsum_in_psum, b + 1)
                        nc.vector.tensor_tensor(hsum[o][:, :], hT[o][:, :], spare[:, :], ALU.mult).then_inc(s.hsum_ready, 1)

                def batch(b, o, last_b, next_b):
                    def gated(e):
                        dve.wait_ge(s.beta_rows, b * EP + e + 1)
                        if e >= 3:
                            dve.wait_ge(s.r_done, b * EP + e - 2)
                        nc.vector.scalar_tensor_tensor(out=w_t[e % 3][:, :], in0=hT[o][:, :], scalar=agg_e[o][:, e:e + 1], in1=rows_of["beta", e][:, :],
                                                       op0=ALU.subtract, op1=ALU.mult).then_inc(s.w_done, 1)

                    for e in range(LEAD):
                        gated(e)
                    for e in range(EP):
                        if e + LEAD < EP:
                            gated(e + LEAD)
                        run_slots(lambda name, bb: slot(name, bb, 1 - o), e, 1, last_b, next_b)
                        if e == SLOT_AT["store"] + 1 and next_b is not None:
                            make_x2(next_b)
                        dve.wait_ge(s.u_done, b * EP + e + 1)
                        dve.wait_ge(s.c_rows, b * EP + e + 1)
                        if e >= 2:
                            dve.wait_ge(s.summed, b * EP + e - 1)
                        nc.vector.tensor_tensor(p_t[e % 2][:, :], u_t[e % 2][:, :], rows_of["c", e][:, :], ALU.mult).then_inc(s.p_done, 1)
                    dve.wait_ge(s.summed, b * EP + EP)
                    nc.vector.tensor_tensor(g[:, :], hsum[o][:, :], k.pair[:, :], ALU.add).then_inc(s.g_ready, 1)

                def prepare(b, o):
                    make_x2(b)
                    for name in PREPARE:
                        slot(name, b, o)

                over_batches(dve, prepare, batch, lambda b: [slot(n, b, 1) for n in FINISH])
                dve.wait_ge(s.out_stored, B)



def build(nc, x, adj, emb, weight, bias, net_params, Wh, bh, W_out, b_out, H, W, W_ind, a_node, a_gn, a_ge, fcW, fcb, av, out):
    k = Ctx()
    k.B, k.N, k.F = x.shape
    k.NC, k.D, k.K = k.N // P, weight.shape[0], weight.shape[1]
    with ExitStack() as ctx:
        def sb(n, s, d=F32):
            return ctx.enter_context(nc.sbuf_tensor(n, s, d))

        def ps(n, s):
            return ctx.enter_context(nc.psum_tensor(n, s, F32))

        in_use = []

        def sem(n):
            in_use.append(nc.alloc_semaphore(name=n))
            return in_use[-1]

        def retire_semaphores():
            with nc.Block() as block:
                @block.gpsimd
                def _(pool):
                    nc.clear_and_free_semaphores(in_use)
            in_use.clear()

        k.sem = sem
        k.wide = [ps("wide0", [P, 1024]), ps("wide1", [P, 1024])]
        k.pair = ps("pair", [P, 1024])
        k.spare = ps("spare", [P, 1024])
        k.bank_u, k.bank_m = k.spare[:, 0:512], k.spare[:, 512:1024]

        k.ident = sb("ident", [P, P])
        k.xn = sb("xn", [P, k.NC, k.B, k.F])
        k.deg = sb("deg", [P, k.NC])
        with ExitStack() as front:
            k.at_hi = front.enter_context(nc.sbuf_tensor("at_hi", [P, k.NC, k.N], F32R))
            k.at_lo = front.enter_context(nc.sbuf_tensor("at_lo", [P, k.NC, k.N], F32R))
            with ExitStack() as inner:
                k.split = [inner.enter_context(nc.sbuf_tensor(f"split{i}", [P, k.NC, k.B, 2, k.F], F32R)) for i in range(1)]
                k.w_split = inner.enter_context(nc.sbuf_tensor("w_split", [P, k.K, 2, k.F * k.D], F32R))
                k.emb = inner.enter_context(nc.sbuf_tensor("emb", [P, k.NC, k.D], F32))
                k.node_bias = inner.enter_context(nc.sbuf_tensor("node_bias", [P, k.NC, k.F], F32))
                load_and_transpose_adjacency(nc, k, adj, x, (emb, weight, bias))
                k.split.append(inner.enter_context(nc.sbuf_tensor("split1", [P, k.NC, k.B, 2, k.F], F32R)))
                node_weight_convolution(nc, k)
            layer_norm(nc, k, "_0")
            with ExitStack() as inner:
                k.split = [inner.enter_context(nc.sbuf_tensor("split2", [P, k.NC, 2, k.B, k.F], F32R))]
                relu_diffusion(nc, k, net_params)
            layer_norm(nc, k, "_1")
        retire_semaphores()
        k.delta = sb("delta", [P, k.B + 1, k.NC, k.F])
        ind_dram = nc.dram_tensor("industry", [k.B, k.F, k.N], F32)
        with ExitStack() as rows:
            k.adj = rows.enter_context(nc.sbuf_tensor("adj_rows2", [P, k.NC, k.N], F32))
            graph_attention(nc, k, adj, Wh, bh, W_out, b_out)
            layer_norm(nc, k, "_2", add=k.delta[:, 1:k.B + 1, :, :].rearrange("p b c f -> p c b f"))
            retire_semaphores()
            industry_messages(nc, k, W_ind, ind_dram)
        hypergraph_attention(nc, k, (H, W, a_node, a_gn, a_ge, fcW, fcb, av), ind_dram)
        layer_norm(nc, k, "_3", add=k.delta[:, 0:k.B, :, :].rearrange("p b c f -> p c b f"))
        stored = k.sem("stored")
        with nc.Block() as block:
            @block.sync
            def _(sp):
                for c in range(k.NC):
                    sp.dma_start(out[:, c * P:(c + 1) * P, :].rearrange("b p f -> p b f"), k.xn[:, c, :, :]).then_inc(stored, 16)
                sp.wait_ge(stored, 16 * k.NC)


_INS = ['x', 'adj', 'L0_gnn_embedding', 'L0_gnn_weight', 'L0_gnn_bias', 'L1_gnn_net_params', 'L2_gnn_Wh', 'L2_gnn_bh',
        'L2_gnn_W_out', 'L2_gnn_b_out', 'L3_gnn_H', 'L3_gnn_W', 'L3_gnn_W_ind', 'L3_gnn_a_node', 'L3_gnn_a_gn',
        'L3_gnn_a_ge', 'L3_gnn_fcW', 'L3_gnn_fcb', 'L3_gnn_av']


def kernel(**inputs):
    import numpy as _np
    import concourse.bacc as _bacc
    from concourse import mybir as _mybir
    from concourse.bass_utils import run_bass_kernel_spmd as _run

    nc = _bacc.Bacc("TRN2", target_bir_lowering=False, num_devices=1)
    arrays, args = {}, []
    for name in _INS:
        a = _np.ascontiguousarray(inputs[name])
        arrays[f"in_{name}_dram"] = a
        args.append(nc.dram_tensor(f"in_{name}_dram", a.shape, _mybir.dt.from_np(a.dtype), kind="ExternalInput").ap())
    args.append(nc.dram_tensor("out_0_dram", inputs["x"].shape, _mybir.dt.float32, kind="ExternalOutput").ap())
    build(nc, *args)
    r = _run(nc, [arrays], core_ids=[0])
    return r.results[0]["out_0_dram"]
```

```python
from contextlib import ExitStack

import concourse.bass as bass
from concourse import mybir

F32 = mybir.dt.float32
F32R = mybir.dt.float32r
ALU = mybir.AluOpType
ACT = mybir.ActivationFunctionType
AX_X = mybir.AxisListType.X

P = 128
EPS = 1e-5
MASKED = -1e16
NEG = -1e9


class Ctx:
    pass



def f32(ap):
    return ap.bitcast(F32)



def load_and_transpose_adjacency(nc, k, adj, x, params):
    N, NC = k.N, k.NC
    emb, weight, bias = params
    D, K, F, O = weight.shape
    with ExitStack() as ctx:
        sb = lambda n, s, d=F32: ctx.enter_context(nc.sbuf_tensor(n, s, d))
        sem = k.sem
        an = sb("adj_rows", [P, NC, N])
        w_raw = sb("w_raw", [P, K, D, O])
        embT = sb("embT", [D, N])
        bias_sb = sb("bias_sb", [D, O])
        adj_loaded = [sem(f"adj_loaded{c}") for c in range(NC)]
        x_loaded, w_loaded = sem("x_loaded"), sem("w_loaded")
        zeroed, ident_ready = sem("ident_zeroed"), sem("ident_ready")
        at_transposed, at_hi_ready, at_lo_ready = sem("at_transposed"), sem("at_hi_ready"), sem("at_lo_ready")
        embT_in_psum, embT_ready, nbias_in_psum, setup_done = (
            sem("embT_in_psum"), sem("embT_ready"), sem("nbias_in_psum"), sem("setup_done"))
        split_ready = sem("split0_hi_ready")

        with nc.Block() as block:
            @block.sync
            def _(sp):
                for c in range(NC):
                    sp.dma_start(an[:, c, :], adj[c * P:(c + 1) * P, :]).then_inc(adj_loaded[c], 16)
                for c in range(NC):
                    sp.dma_start(k.xn[:, c, :, :], x[:, c * P:(c + 1) * P, :].rearrange("b p f -> p b f")).then_inc(x_loaded, 16)

            @block.gpsimd
            def _(pool):
                nc.gpsimd.memset(k.ident[:, :], 0.0).then_inc(zeroed, 1)
                pool.wait_ge(zeroed, 1)
                nc.gpsimd.affine_select(out=k.ident[:, :], in_=k.ident[:, :], compare_op=ALU.not_equal, fill=1.0,
                                        base=0, pattern=[[-1, P]], channel_multiplier=1).then_inc(ident_ready, 1)
                pool.dma_start(k.emb[:, :, :], emb.rearrange("(c p) d -> p c d", p=P)).then_inc(w_loaded, 16)
                pool.dma_start(bias_sb[:, :], bias).then_inc(w_loaded, 16)
                for half in range(2):
                    for t in range(K):
                        pool.dma_start(w_raw[half * F:(half + 1) * F, t, :, :],
                                       weight[:, t, :, :].rearrange("d i o -> i d o")).then_inc(w_loaded, 16)

            @block.tensor
            def _(pe):
                pe.wait_ge(ident_ready, 1)
                for mc in range(NC):
                    if mc == 0:
                        for c in range(NC):
                            pe.wait_ge(adj_loaded[c], 16)
                    if mc >= 2:
                        pe.wait_ge(at_lo_ready, mc - 1)
                    for c in range(NC):
                        last = nc.tensor.transpose(k.wide[mc % 2][:, c * P:(c + 1) * P], an[:, c, mc * P:(mc + 1) * P], k.ident[:, :])
                    last.then_inc(at_transposed, 1)
                pe.wait_ge(w_loaded, 16 * (2 + 2 * K))
                for c in range(NC):
                    last = nc.tensor.transpose(k.pair[0:D, c * P:(c + 1) * P], k.emb[:, c, :], k.ident[:, :])
                last.then_inc(embT_in_psum, 1)
                pe.wait_ge(embT_ready, 1)
                for c in range(NC):
                    last = nc.tensor.matmul(k.bank_u[:, c * O:(c + 1) * O], embT[:, c * P:(c + 1) * P], bias_sb[:, :], start=True, stop=True)
                last.then_inc(nbias_in_psum, 1)

            @block.scalar
            def _(act):
                for mc in range(NC):
                    act.wait_ge(at_transposed, mc + 1)
                    nc.scalar.activation(k.at_hi[:, mc, :], k.wide[mc % 2][:, :], ACT.Copy).then_inc(at_hi_ready, 1)
                act.wait_ge(x_loaded, 16 * NC)
                nc.scalar.activation(k.split[0][:, :, :, 0, :].rearrange("p c b f -> p (c b) f"),
                                     k.xn[:, :, :, :].rearrange("p c b f -> p (c b) f"), ACT.Copy).then_inc(split_ready, 1)
                act.wait_ge(w_loaded, 16 * (2 + 2 * K))
                for t in range(K):
                    nc.scalar.activation(k.w_split[:, t, 0, :].rearrange("p (o d) -> p o d", d=D),
                                         w_raw[:, t, :, :].rearrange("p d o -> p o d"), ACT.Copy).then_inc(split_ready, 1)
                act.wait_ge(embT_in_psum, 1)
                nc.scalar.activation(embT[:, :], k.pair[0:D, :], ACT.Copy).then_inc(embT_ready, 1)
                act.wait_ge(nbias_in_psum, 1)
                nc.scalar.activation(k.node_bias[:, :, :].rearrange("p c o -> p (c o)"), k.bank_u[:, :], ACT.Copy).then_inc(setup_done, 1)

            @block.vector
            def _(dve):
                for mc in range(NC):
                    dve.wait_ge(at_hi_ready, mc + 1)
                    nc.vector.tensor_tensor(k.at_lo[:, mc, :], k.wide[mc % 2][:, :], f32(k.at_hi[:, mc, :]), ALU.subtract).then_inc(at_lo_ready, 1)
                dve.wait_ge(split_ready, 1)
                nc.vector.tensor_tensor(k.split[0][:, :, :, 1, :].rearrange("p c b f -> p (c b) f"),
                                        k.xn[:, :, :, :].rearrange("p c b f -> p (c b) f"),
                                        f32(k.split[0][:, :, :, 0, :]).rearrange("p c b f -> p (c b) f"), ALU.subtract).then_inc(setup_done, 1)
                for t in range(K):
                    dve.wait_ge(split_ready, 2 + t)
                    nc.vector.tensor_tensor(k.w_split[:, t, 1, :].rearrange("p (o d) -> p o d", d=D),
                                            w_raw[:, t, :, :].rearrange("p d o -> p o d"),
                                            f32(k.w_split[:, t, 0, :]).rearrange("p (o d) -> p o d", d=D), ALU.subtract).then_inc(setup_done, 1)



def layer_norm(nc, k, tag, add=None):
    G, F = k.NC * k.B, k.F
    with ExitStack() as ctx:
        sb = lambda n, s, d=F32: ctx.enter_context(nc.sbuf_tensor(n + tag, s, d))
        sem = lambda n: k.sem(n + tag)
        sq = sb("ln_sq", [P, G, F])
        total, mean, var, std, rstd = (sb(n, [P, G]) for n in ("ln_total", "ln_mean", "ln_var", "ln_std", "ln_rstd"))
        step, centred, squared, var_ready, std_ready = (
            sem(n) for n in ("ln_step", "ln_centred", "ln_squared", "ln_var_ready", "ln_std_ready"))
        x = k.xn[:, :, :, :].rearrange("p c b f -> p (c b) f")
        with nc.Block() as block:
            @block.scalar
            def _(act):
                act.wait_ge(centred, 1)
                nc.scalar.activation(sq[:, :, :], x, ACT.Square).then_inc(squared, 1)
                act.wait_ge(var_ready, 1)
                nc.scalar.activation(std[:, :], var[:, :], ACT.Sqrt).then_inc(std_ready, 1)

            @block.vector
            def _(dve):
                n = 0
                if add is not None:
                    nc.vector.tensor_tensor(k.xn[:, :, :, :], k.xn[:, :, :, :], add, ALU.add).then_inc(step, 1)
                    n += 1
                    dve.wait_ge(step, n)
                nc.vector.reduce_sum(total[:, :], x, axis=AX_X).then_inc(step, 1)
                dve.wait_ge(step, n + 1)
                nc.vector.tensor_scalar(mean[:, :], total[:, :], 1.0 / F, None, ALU.mult).then_inc(step, 1)
                dve.wait_ge(step, n + 2)
                nc.vector.tensor_tensor(x, x, mean[:, :].unsqueeze(2).broadcast_to([P, G, F]), ALU.subtract).then_inc(centred, 1)
                dve.wait_ge(squared, 1)
                nc.vector.reduce_sum(total[:, :], sq[:, :, :], axis=AX_X).then_inc(step, 1)
                dve.wait_ge(step, n + 3)
                nc.vector.tensor_scalar(var[:, :], total[:, :], 1.0 / F, EPS, ALU.mult, ALU.add).then_inc(var_ready, 1)
                dve.wait_ge(std_ready, 1)
                nc.vector.reciprocal(rstd[:, :], std[:, :]).then_inc(step, 1)
                dve.wait_ge(step, n + 4)
                nc.vector.tensor_tensor(std[:, :], rstd[:, :], rstd[:, :], ALU.mult).then_inc(step, 1)
                dve.wait_ge(step, n + 5)
                nc.vector.tensor_tensor(std[:, :], std[:, :], var[:, :], ALU.mult).then_inc(step, 1)
                dve.wait_ge(step, n + 6)
                nc.vector.tensor_scalar(std[:, :], std[:, :], -0.5, 1.5, ALU.mult, ALU.add).then_inc(step, 1)
                dve.wait_ge(step, n + 7)
                nc.vector.tensor_tensor(rstd[:, :], rstd[:, :], std[:, :], ALU.mult).then_inc(step, 1)
                dve.wait_ge(step, n + 8)
                nc.vector.tensor_tensor(x, x, rstd[:, :].unsqueeze(2).broadcast_to([P, G, F]), ALU.mult).then_inc(step, 1)



def node_weight_convolution(nc, k):
    NC, B, F, D, K, O = k.NC, k.B, k.F, k.D, k.K, k.F
    CH = O * D // 512
    with ExitStack() as ctx:
        sb = lambda n, s, d=F32: ctx.enter_context(nc.sbuf_tensor(n, s, d))
        sem = k.sem
        cheb1 = k.split[1]
        cheb2 = [sb(f"cheb2_{i}", [P, B, 2, F], F32R) for i in range(2)]
        cheb2_full = sb("cheb2_full", [P, B, F])
        stat = [sb(f"l0_stat{i}", [P, K, P], F32R) for i in range(2)]
        weighted = [sb(f"l0_weighted{i}", [P, O, D]) for i in range(2)]
        summed = [sb(f"l0_summed{i}", [P, B, O]) for i in range(2)]
        prod_ready, hi_ready, cheb1_ready = sem("l0_prod_ready"), sem("l0_hi_ready"), sem("l0_cheb1_ready")
        full_ready, cheb2_ready = sem("l0_full_ready"), sem("l0_cheb2_ready")
        stat_in_psum, stat_ready, y_ready, weighted_ready, summed_ready, step = (
            sem(n) for n in ("l0_stat_in_psum", "l0_stat_ready", "l0_y_ready", "l0_weighted_ready", "l0_summed_ready", "l0_step"))
        prod = [k.bank_u, k.bank_m]
        tpos = [k.pair[:, 0:512], k.pair[:, 512:1024]]

        def product(pe, c, src, bank):
            n = 0
            for a, s in ((k.at_hi, 0), (k.at_hi, 1), (k.at_lo, 0)):
                for mc in range(NC):
                    last = nc.tensor.matmul(bank[:, :].rearrange("p (b f) -> p b f", f=F), a[:, mc, c * P:(c + 1) * P],
                                            src[:, mc, :, s, :], start=n == 0, stop=n == 3 * NC - 1)
                    n += 1
            return last

        with nc.Block() as block:
            @block.tensor
            def _(pe):
                for c in range(NC):
                    if c >= 2:
                        pe.wait_ge(cheb1_ready, c - 1)
                    product(pe, c, k.split[0], prod[c % 2]).then_inc(prod_ready, 1)
                pe.wait_ge(cheb1_ready, NC)
                product(pe, 0, cheb1, prod[0]).then_inc(prod_ready, 1)
                for c in range(NC):
                    if c + 1 < NC:
                        if c >= 1:
                            pe.wait_ge(full_ready, c)
                        product(pe, c + 1, cheb1, prod[(c + 1) % 2]).then_inc(prod_ready, 1)
                    pe.wait_ge(cheb2_ready, c + 1)

                    def turn(t):
                        b = t % B
                        if t >= 2:
                            pe.wait_ge(stat_ready, t - 1)
                        for i, s in enumerate((k.split[0][:, c, b, :, :], cheb1[:, c, b, :, :], cheb2[c % 2][:, b, :, :])):
                            last = nc.tensor.transpose(tpos[t % 2][:, i * P:(i + 1) * P],
                                                       f32(s).rearrange("p s f -> p (s f)"), k.ident[:, :])
                        last.then_inc(stat_in_psum, 1)

                    turn(c * B)
                    for b in range(B):
                        t = c * B + b
                        if b + 1 < B:
                            turn(t + 1)
                        pe.wait_ge(stat_ready, t + 1)
                        if t >= 2:
                            pe.wait_ge(weighted_ready, t - 1)
                        for j in range(CH):
                            for i in range(K):
                                for part in range(2):
                                    last = nc.tensor.matmul(k.wide[t % 2][:, j * 512:(j + 1) * 512], stat[t % 2][:, i, :],
                                                            k.w_split[:, i, part, j * 512:(j + 1) * 512],
                                                            start=i + part == 0, stop=i == K - 1 and part == 1)
                        last.then_inc(y_ready, 1)

            @block.scalar
            def _(act):
                for c in range(NC):
                    act.wait_ge(prod_ready, c + 1)
                    nc.scalar.activation(cheb1[:, c, :, 0, :], prod[c % 2][:, :].rearrange("p (b f) -> p b f", f=F), ACT.Copy).then_inc(hi_ready, 1)

                def cheb2_hi(c):
                    act.wait_ge(full_ready, c + 1)
                    if c >= 2:
                        act.wait_ge(stat_in_psum, (c - 1) * B)
                    nc.scalar.activation(cheb2[c % 2][:, :, 0, :], cheb2_full[:, :, :], ACT.Copy).then_inc(hi_ready, 1)

                cheb2_hi(0)
                for c in range(NC):
                    for b in range(B):
                        t = c * B + b
                        if b == 5 and c + 1 < NC:
                            cheb2_hi(c + 1)
                        act.wait_ge(stat_in_psum, t + 1)
                        if t >= 2:
                            act.wait_ge(y_ready, t - 1)
                        nc.scalar.activation(stat[t % 2][:, :, :].rearrange("p k n -> p (k n)"), tpos[t % 2][:, 0:K * P], ACT.Copy).then_inc(stat_ready, 1)

            @block.vector
            def _(dve):
                for c in range(NC):
                    dve.wait_ge(hi_ready, c + 1)
                    nc.vector.tensor_tensor(cheb1[:, c, :, 1, :], prod[c % 2][:, :].rearrange("p (b f) -> p b f", f=F),
                                            f32(cheb1[:, c, :, 0, :]), ALU.subtract).then_inc(cheb1_ready, 1)

                def cheb2_parts(c):
                    dve.wait_ge(prod_ready, NC + c + 1)
                    if c >= 1:
                        dve.wait_ge(cheb2_ready, c)
                    nc.vector.scalar_tensor_tensor(out=cheb2_full[:, :, :], in0=prod[c % 2][:, :].rearrange("p (b f) -> p b f", f=F),
                                                   scalar=2.0, in1=k.xn[:, c, :, :], op0=ALU.mult, op1=ALU.subtract).then_inc(full_ready, 1)
                    dve.wait_ge(hi_ready, NC + c + 1)
                    if c >= 2:
                        dve.wait_ge(stat_in_psum, (c - 1) * B)
                    nc.vector.tensor_tensor(cheb2[c % 2][:, :, 1, :], cheb2_full[:, :, :], f32(cheb2[c % 2][:, :, 0, :]), ALU.subtract).then_inc(cheb2_ready, 1)

                n = 0
                cheb2_parts(0)
                for c in range(NC):
                    emb_b = k.emb[:, c, :].unsqueeze(1).broadcast_to([P, O, D])
                    for b in range(B):
                        t = c * B + b
                        if b == 5 and c + 1 < NC:
                            cheb2_parts(c + 1)
                        dve.wait_ge(y_ready, t + 1)
                        if t >= 1:
                            dve.wait_ge(summed_ready, t)
                        nc.vector.tensor_tensor(weighted[t % 2][:, :, :], k.wide[t % 2][:, :].rearrange("p (o d) -> p o d", d=D), emb_b, ALU.mult).then_inc(weighted_ready, 1)
                        dve.wait_ge(weighted_ready, t + 1)
                        nc.vector.reduce_sum(summed[c % 2][:, b, :], weighted[t % 2][:, :, :], axis=AX_X).then_inc(summed_ready, 1)
                    dve.wait_ge(summed_ready, (c + 1) * B)
                    nc.vector.tensor_tensor(k.xn[:, c, :, :], k.xn[:, c, :, :], summed[c % 2][:, :, :], ALU.add).then_inc(step, 1)
                    n += 1
                    dve.wait_ge(step, n)
                    nc.vector.tensor_tensor(k.xn[:, c, :, :], k.xn[:, c, :, :],
                                            k.node_bias[:, c, :].unsqueeze(1).broadcast_to([P, B, O]), ALU.add).then_inc(step, 1)
                    n += 1



def product_transposed(nc, k, pe, src, out_bank, bp, half):
    n, NC = 0, k.NC
    for a, s in ((k.at_hi, 0), (k.at_lo, 0), (k.at_hi, 1)):
        for mc in range(NC):
            last = nc.tensor.matmul(out_bank, src[:, mc, s, 2 * bp:2 * bp + 2, :].rearrange("p b f -> p (b f)"),
                                    a[:, mc, half * 512:(half + 1) * 512], start=n == 0, stop=n == 3 * NC - 1)
            n += 1
    return last


def relu_diffusion(nc, k, net_params):
    NC, B, F, L = k.NC, k.B, k.F, 2
    BP, HV = B // 2, k.N // 512
    with ExitStack() as ctx:
        sb = lambda n, s, d=F32: ctx.enter_context(nc.sbuf_tensor(n, s, d))
        sem = k.sem
        w2 = sb("l1_w2", [P, L, P])
        aggT = sb("l1_aggT", [P, BP, k.N])
        zeroed, w_loaded = sem("l1_zeroed"), sem("l1_w_loaded")
        hi_ready, lo_ready, prod_ready, agg_ready, z_in_psum, z_read = (
            sem(n) for n in ("l1_hi_ready", "l1_lo_ready", "l1_prod_ready", "l1_agg_ready", "l1_z_in_psum", "l1_z_read"))
        z = k.split[0]
        prod = [k.bank_u[:, :], k.bank_m[:, :]]
        zb = [k.pair[:, 0:512], k.pair[:, 512:1024]]
        w_dram = net_params.rearrange("(l f g) -> f l g", l=L, f=F)
        with nc.Block() as block:
            @block.sync
            def _(sp):
                sp.wait_ge(zeroed, 1)
                for i in range(2):
                    sp.dma_start(w2[i * F:(i + 1) * F, :, i * F:(i + 1) * F], w_dram).then_inc(w_loaded, 16)

            @block.gpsimd
            def _(pool):
                nc.gpsimd.memset(w2[:, :, :], 0.0).then_inc(zeroed, 1)

            @block.tensor
            def _(pe):
                pe.wait_ge(w_loaded, 32)
                for l in range(L):
                    pe.wait_ge(lo_ready, 1 if l == 0 else 1 + NC)
                    for g in range(BP * HV):
                        t = l * BP * HV + g
                        if t >= 2:
                            pe.wait_ge(agg_ready, t - 1)
                        product_transposed(nc, k, pe, z, prod[t % 2], g // HV, g % HV).then_inc(prod_ready, 1)
                    pe.wait_ge(agg_ready, (l + 1) * BP * HV)
                    for c in range(NC):
                        t = l * NC + c
                        if t >= 2 and t < NC + 2:
                            pe.wait_ge(lo_ready, t)
                        elif t >= 2:
                            pe.wait_ge(z_read, t - NC - 1)
                        for bp in range(BP):
                            last = nc.tensor.matmul(zb[t % 2][:, bp * P:(bp + 1) * P], aggT[:, bp, c * P:(c + 1) * P], w2[:, l, :], start=True, stop=True)
                        last.then_inc(z_in_psum, 1)

            @block.scalar
            def _(act):
                nc.scalar.activation(z[:, :, 0, :, :].rearrange("p c b f -> p c (b f)"),
                                     k.xn[:, :, :, :].rearrange("p c b f -> p c (b f)"), ACT.Copy).then_inc(hi_ready, 1)
                for l in range(L):
                    for g in range(BP * HV):
                        t = l * BP * HV + g
                        act.wait_ge(prod_ready, t + 1)
                        nc.scalar.activation(aggT[:, g // HV, (g % HV) * 512:(g % HV + 1) * 512], prod[t % 2], ACT.Copy).then_inc(agg_ready, 1)
                    if l == 0:
                        for c in range(NC):
                            act.wait_ge(z_in_psum, c + 1)
                            nc.scalar.activation(z[:, c, 0, :, :], zb[c % 2].rearrange("p (b f) -> p b f", f=F), ACT.Relu).then_inc(hi_ready, 1)

            @block.vector
            def _(dve):
                dve.wait_ge(hi_ready, 1)
                nc.vector.tensor_tensor(z[:, :, 1, :, :].rearrange("p c b f -> p c (b f)"),
                                        k.xn[:, :, :, :].rearrange("p c b f -> p c (b f)"),
                                        f32(z[:, :, 0, :, :]).rearrange("p c b f -> p c (b f)"), ALU.subtract).then_inc(lo_ready, 1)
                for c in range(NC):
                    dve.wait_ge(hi_ready, 2 + c)
                    nc.vector.scalar_tensor_tensor(out=z[:, c, 1, :, :], in0=zb[c % 2].rearrange("p (b f) -> p b f", f=F), scalar=0.0,
                                                   in1=f32(z[:, c, 0, :, :]), op0=ALU.max, op1=ALU.subtract).then_inc(lo_ready, 1)
                for c in range(NC):
                    dve.wait_ge(z_in_psum, NC + c + 1)
                    nc.vector.scalar_tensor_tensor(out=k.xn[:, c, :, :], in0=zb[c % 2].rearrange("p (b f) -> p b f", f=F), scalar=0.0,
                                                   in1=k.xn[:, c, :, :], op0=ALU.max, op1=ALU.add).then_inc(z_read, 1)



OUT = "out"


def attention_slots(insts, following):
    slots = []
    for i in range(len(insts) + 1):
        for c in range(8):
            kind, j, h = (("mix", i - 1, 0), ("sums", i - 1, 1), ("project", i + 1, 0), ("project", i + 1, 1),
                          ("head", i - 1, 1), ("mix", i - 1, 1), ("sums", i, 0), ("head", i, 0))[c]
            if following and i == len(insts) and kind == "project":
                kind, j = "next", 0
            if not 0 <= j < len(insts) or (insts[j] == OUT and kind in ("project", "head")):
                continue
            slots.append((8 * i + c, "turn" if kind == "mix" and insts[j] == OUT else kind, j, h))
    return slots


def transpose_x(nc, k, a, pe, at):
    pe.wait_ge(a.x_ready, at("x_ready", 1))
    for c in range(8):
        last = nc.tensor.transpose(k.wide[0][:, c * P:(c + 1) * P], a.x_twice[:, c, :], k.ident[:, :])
    last.then_inc(a.xt_in_psum, 1)


def project_keys(nc, k, a, head, h):
    nc.tensor.matmul(k.bank_m[:, :], a.gram_hi[:, head, :], a.xt[:, h * 512:(h + 1) * 512], start=True, stop=False)
    return nc.tensor.matmul(k.bank_m[:, :], a.gram_lo[:, head, :], a.xt[:, h * 512:(h + 1) * 512], start=False, stop=True)


def copy_xt(nc, k, a, act, at):
    act.wait_ge(a.xt_in_psum, at("xt_in_psum", 1))
    nc.scalar.activation(a.xt[:, :], k.wide[0][:, :], ACT.Copy).then_inc(a.xt_hi_ready, 1)


def keys_hi(nc, k, a, n, h):
    nc.scalar.activation(a.keys_hi[n % 2][:, h * 512:(h + 1) * 512], k.bank_m[:, :], ACT.Copy).then_inc(a.keys_hi_ready, 1)


def make_x_twice(nc, k, a, b):
    nc.vector.tensor_copy(a.x_twice.rearrange("p c (t f) -> p c t f", t=2),
                          k.xn[:, :, bass.ds(b, 1), :].broadcast_to([P, k.NC, 2, k.F])).then_inc(a.x_ready, 1)


def low_parts_of_xt(nc, k, a, dve, at):
    dve.wait_ge(a.xt_hi_ready, at("xt_hi_ready", 1))
    nc.vector.tensor_tensor(a.xt[k.F:P, :], k.wide[0][k.F:P, :], f32(a.xt[k.F:P, :]), ALU.subtract).then_inc(a.xt_lo_ready, 1)


def keys_lo(nc, k, a, n, h):
    nc.vector.tensor_tensor(a.keys_lo[n % 2][:, h * 512:(h + 1) * 512], k.bank_m[:, :],
                            f32(a.keys_hi[n % 2][:, h * 512:(h + 1) * 512]), ALU.subtract).then_inc(a.keys_ready, 1)


def attention_tensor(nc, k, a, pe, insts, b, at, at_next):
    slots = attention_slots(insts, at_next is not None)
    order = [i for i in insts if i != OUT]
    NI, ST = len(insts), 8 * len(insts)

    def nth_head(i):
        return order.index(insts[i])

    def misc_bank_free(m):
        if m == 0:
            return
        _, kind, i, h = slots[m - 1]
        if kind in ("project", "next"):
            pe.wait_ge(a.keys_ready, at("keys_ready", 2 * nth_head(i) + h + 1) if kind == "project" else at_next("keys_ready", h + 1))
        elif kind == "sums":
            pe.wait_ge(a.inv_ready, at("inv_ready", 2 * i + h + 1))
        elif kind == "head":
            pe.wait_ge(a.biased_ready, at("biased_ready", 2 * i + h + 1))
        elif kind == "mix":
            pe.wait_ge(a.mixed, at("mixed", 2 * nth_head(i) + h + 1))
        else:
            pe.wait_ge(a.out_stored, at("out_stored", h + 1))

    def slot(step):
        for m, (st, kind, i, h) in enumerate(slots):
            if st != step:
                continue
            misc_bank_free(m)
            inst = insts[i]
            if kind in ("project", "next"):
                if kind == "next":
                    pe.wait_ge(a.xt_lo_ready, at_next("xt_lo_ready", 1))
                last = project_keys(nc, k, a, inst, h)
            elif kind == "sums":
                pe.wait_ge(a.rinv_ready, at("rinv_ready", 2 * i + h + 1))
                for j in range(4):
                    col = 8 * (i % 2) + 4 * h + j
                    for part in (a.rinv_hi, a.rinv_lo):
                        last = nc.tensor.matmul(k.bank_m[:, j * P:(j + 1) * P], part[:, col:col + 1].broadcast_to([P, P]),
                                                a.ident_r[:, :], start=part is a.rinv_hi, stop=part is a.rinv_lo)
            elif kind == "head":
                pe.wait_ge(a.ctx_ready, at("ctx_ready", 2 * i + h + 1))
                last = nc.tensor.matmul(k.bank_m[:, :], a.wh[:, inst, :], a.ctx[:, :], start=True, stop=True)
            elif kind == "mix":
                pe.wait_ge(a.leaky_ready, at("leaky_ready", 2 * i + h + 1))
                last = nc.tensor.matmul(k.bank_m[:, :], a.wo[:, inst, :, :].rearrange("p t o -> p (t o)"), a.leaky[:, :], start=True, stop=True)
            else:
                pe.wait_ge(a.leaky_ready, at("leaky_ready", 2 * i + h + 1))
                for j in range(4):
                    last = nc.tensor.transpose(k.bank_m[:, j * P:(j + 1) * P], a.leaky[:, j * P:(j + 1) * P], k.ident[:, :])
            last.then_inc(a.slot_done, 1)

    def scores(q):
        i, c = divmod(q, 8)
        out = insts[i] == OUT
        if q < 2:
            if out:
                pe.wait_ge(a.vo_ready, at("vo_ready", 1))
        elif q >= 2:
            pe.wait_ge(a.scaled, at("scaled", q - 1))
        if c == 0:
            if out:
                pe.wait_ge(a.ko_lo_ready, at("ko_lo_ready", 1))
                pe.wait_ge(a.xo_lo_ready, at("xo_lo_ready", 1))
            else:
                pe.wait_ge(a.keys_ready, at("keys_ready", 2 * nth_head(i) + 2))
        xt = a.xo if out else a.xt
        hi, lo = (a.ko_hi, a.ko_lo) if out else (a.keys_hi[nth_head(i) % 2], a.keys_lo[nth_head(i) % 2])
        for j in range(2):
            o = k.wide[q % 2][:, j * 512:(j + 1) * 512]
            nc.tensor.matmul(o, xt[:, c * P:(c + 1) * P], hi[:, j * 512:(j + 1) * 512], start=True, stop=False)
            last = nc.tensor.matmul(o, xt[:, c * P:(c + 1) * P], lo[:, j * 512:(j + 1) * 512], start=False, stop=True)
        last.then_inc(a.scores_ready, 1)

    def turn_probs(q):
        pe.wait_ge(a.probs_ready, at("probs_ready", q + 1))
        if q == 0:
            pe.wait_ge(a.vo_ready, at("vo_ready", 1))
        for j in range(2):
            if q >= 1:
                pe.wait_ge(a.turned_read, at("turned_read", 2 * (q - 1) + j + 1))
            for m in range(4):
                mc = 4 * j + m
                last = nc.tensor.transpose(k.pair[:, mc * P:(mc + 1) * P], a.probs[q % 2][:, mc * P:(mc + 1) * P], k.ident[:, :])
            last.then_inc(a.turned, 1)

    def values(i, g, piece):
        if piece == 0:
            pe.wait_ge(a.turned_read, at("turned_read", 2 * (8 * i + 4 * g + 4)))
            if 2 * i + g >= 1:
                pe.wait_ge(a.ctx_ready, at("ctx_ready", 2 * i + g))
        if piece == 0:
            pe.wait_ge(a.probs_split, at("probs_split", 8 * i + 4 * g + 4))
            if insts[i] != OUT:
                pe.wait_ge(a.v_split, at("v_split", 1))
            for m in range(4):
                if insts[i] == OUT:
                    nc.tensor.matmul(k.bank_u[0:k.F, :], a.vo_hi[:, m, :], a.probs_hi[g][:, m, :], start=m == 0, stop=False)
                    nc.tensor.matmul(k.bank_u[0:k.F, :], a.vo_lo[:, m, :], a.probs_hi[g][:, m, :], start=False, stop=False)
                    nc.tensor.matmul(k.bank_u[0:k.F, :], a.vo_hi[:, m, :], a.probs_lo[g][:, m, :], start=False, stop=False)
                else:
                    parts = a.v_parts[:, m, :, :].rearrange("p t f -> p (t f)")
                    nc.tensor.matmul(k.bank_u[:, :], parts, a.probs_hi[g][:, m, :], start=m == 0, stop=False)
                    nc.tensor.matmul(k.bank_u[:, :], parts, a.probs_lo[g][:, m, :], start=False, stop=False)
        else:
            v, rows = (a.vo, k.F) if insts[i] == OUT else (a.v, P)
            for mc in (2 * piece - 2, 2 * piece - 1):
                last = nc.tensor.matmul(k.bank_u[0:rows, :], v[:, mc, :], a.probsT[g][:, mc, :], start=False, stop=mc == 3)
        if piece == 2:
            last.then_inc(a.values_done, 1)

    if insts[0] != OUT:
        scores(0)
        scores(1)
        pe.wait_ge(a.v_ready, at("v_ready", 1))
    else:
        pe.wait_ge(a.mixed, at("mixed", 0))
    for c in range(8):
        last = nc.tensor.transpose(k.pair[:, c * P:(c + 1) * P], a.h2[:, c * P:(c + 1) * P], k.ident[:, :])
    last.then_inc(a.vo_in_psum, 1)
    if insts[0] == OUT:
        scores(0)
        scores(1)
    scores(2)
    for step in range(ST + 6):
        i, c = divmod(step, 8)
        if step + 3 < ST:
            scores(step + 3)
        if step == ST and at_next is not None:
            transpose_x(nc, k, a, pe, at_next)
        if step < ST:
            turn_probs(step)
        if 4 <= c < 7 and i < NI:
            values(i, 0, c - 4)
        elif c < 3 and i >= 1:
            values(i - 1, 1, c)
        slot(step)


def attention_scalar(nc, k, a, act, insts, b, at, at_next):
    slots = attention_slots(insts, at_next is not None)
    order = [i for i in insts if i != OUT]
    ST = 8 * len(insts)

    def exponentials(q):
        i, c = divmod(q, 8)
        act.wait_ge(a.shifted, at("shifted", q + 1))
        if q >= 2:
            act.wait_ge(a.turned, at("turned", 2 * (q - 2) + 2))
        col = 8 * (i % 2) + c
        nc.scalar.activation(a.probs[q % 2][:, :], a.neg_scores[q % 2][:, :], ACT.Exp, bias=a.neg_max[:, col:col + 1],
                             scale=-1.0, accum_out=a.sums[:, col:col + 1]).then_inc(a.probs_ready, 1)

    def read_turned(q):
        i, c = divmod(q, 8)
        g = c // 4
        if c % 4 == 0 and i >= 1:
            act.wait_ge(a.values_done, at("values_done", 2 * (i - 1) + g + 1))
        columns = slice((c % 4) * P, (c % 4 + 1) * P)
        for j in range(2):
            act.wait_ge(a.turned, at("turned", 2 * q + j + 1))
            src = k.pair[:, j * 512:(j + 1) * 512].rearrange("p (m n) -> p m n", n=P)
            if j == 0:
                last = nc.scalar.activation(a.probsT[g][:, :, columns], src, ACT.Copy)
            else:
                if q >= 1:
                    act.wait_ge(a.probs_split, at("probs_split", q))
                nc.scalar.activation(a.probs_whole[:, :, :], src, ACT.Copy)
                last = nc.scalar.activation(a.probs_hi[g][:, :, columns], src, ACT.Copy)
            last.then_inc(a.turned_read, 1)

    def slot(step):
        for m, (st, kind, i, h) in enumerate(slots):
            if st != step:
                continue
            inst = insts[i]
            if kind in ("project", "next"):
                act.wait_ge(a.slot_done, at("slot_done", m + 1))
                keys_hi(nc, k, a, order.index(inst), h)
            elif kind == "sums":
                if 2 * i + h >= 1:
                    act.wait_ge(a.ctx_ready, at("ctx_ready", 2 * i + h))
                act.wait_ge(a.slot_done, at("slot_done", m + 1))
                nc.scalar.activation(a.inv[:, :], k.bank_m[:, :], ACT.Copy).then_inc(a.inv_ready, 1)
            elif kind == "head":
                act.wait_ge(a.slot_done, at("slot_done", m + 1))
                nc.scalar.activation(a.biased[:, :], k.bank_m[:, :], ACT.Identity, bias=a.bh[:, inst:inst + 1]).then_inc(a.biased_ready, 1)
        i, c = divmod(step, 8)
        h, i = (0, i) if c == 7 else (1, i - 1)
        if c in (7, 4) and 0 <= i < len(insts) and insts[i] == OUT:
            act.wait_ge(a.ctx_ready, at("ctx_ready", 2 * i + h + 1))
            nc.scalar.activation(a.biased[0:k.F, :], a.ctx[0:k.F, :], ACT.Identity, bias=a.b_out[:, 0:1]).then_inc(a.biased_ready, 1)

    if insts[0] != OUT:
        act.wait_ge(a.v_ready, at("v_ready", 1))
    else:
        act.wait_ge(a.mixed, at("mixed", 0))
    nc.scalar.activation(a.ko_hi[:, :], a.h2[:, :], ACT.Copy).then_inc(a.ko_hi_ready, 1)
    act.wait_ge(a.vo_in_psum, at("vo_in_psum", 1))
    vo = k.pair[:, :].rearrange("p (c f) -> p c f", f=P)[:, :, 0:k.F]
    nc.scalar.activation(a.vo[:, :, :], vo[:, 0:k.NC // 2, :], ACT.Copy)
    nc.scalar.activation(a.vo_hi[:, :, :], vo[:, k.NC // 2:, :], ACT.Copy).then_inc(a.vo_hi_ready, 1)
    exponentials(0)
    for step in range(ST + 7):
        if step >= 1:
            slot(step - 1)
        if step + 1 < ST:
            exponentials(step + 1)
        if step < ST:
            read_turned(step)
        elif step == ST and at_next is not None:
            copy_xt(nc, k, a, act, at_next)


def attention_vector(nc, k, a, dve, insts, b, at, at_next):
    slots = attention_slots(insts, at_next is not None)
    order = [i for i in insts if i != OUT]
    NI, ST = len(insts), 8 * len(insts)

    def scaled_scores(q):
        dve.wait_ge(a.scores_ready, at("scores_ready", q + 1))
        if q >= 2:
            dve.wait_ge(a.shifted, at("shifted", q - 1))
        nc.vector.tensor_tensor(a.scaled_scores[q % 2][:, :], k.wide[q % 2][:, :], k.adj[:, q % 8, :], ALU.mult).then_inc(a.scaled, 1)

    def shifted_scores(q):
        i, c = divmod(q, 8)
        dve.wait_ge(a.scaled, at("scaled", q + 1))
        if q >= 2:
            dve.wait_ge(a.probs_ready, at("probs_ready", q - 1))
        nc.vector.tensor_scalar(a.neg_scores[q % 2][:, :], a.scaled_scores[q % 2][:, :], 0.0, MASKED, ALU.is_equal, ALU.mult).then_inc(a.filled, 1)
        if q + 1 < ST:
            scaled_scores(q + 1)
        dve.wait_ge(a.filled, 1)
        dve.wait_ge(a.filled, at("filled", q + 1))
        col = 8 * (i % 2) + c
        nc.vector.tensor_tensor_reduce(out=a.neg_scores[q % 2][:, :], in0=a.scaled_scores[q % 2][:, :], in1=a.neg_scores[q % 2][:, :], scale=-1.0,
                                       scalar=3.0e38, op0=ALU.add, op1=ALU.min, accum_out=a.neg_max[:, col:col + 1]).then_inc(a.shifted, 1)

    def rinv(i, g):
        dve.wait_ge(a.probs_ready, at("probs_ready", 8 * i + 4 * g + 4))
        col = 8 * (i % 2) + 4 * g
        nc.vector.reciprocal(a.rinv[:, col:col + 4], a.sums[:, col:col + 4]).then_inc(a.rinv_step, 1)
        dve.wait_ge(a.rinv_step, at("rinv_step", 4 * i + 2 * g + 1))
        nc.vector.tensor_copy(a.rinv_hi[:, col:col + 4], a.rinv[:, col:col + 4]).then_inc(a.rinv_step, 1)
        dve.wait_ge(a.rinv_step, at("rinv_step", 4 * i + 2 * g + 2))
        nc.vector.tensor_tensor(a.rinv_lo[:, col:col + 4], a.rinv[:, col:col + 4], f32(a.rinv_hi[:, col:col + 4]), ALU.subtract).then_inc(a.rinv_ready, 1)

    def context(i, g):
        dve.wait_ge(a.values_done, at("values_done", 2 * i + g + 1))
        dve.wait_ge(a.inv_ready, at("inv_ready", 2 * i + g + 1))
        rows = k.F if insts[i] == OUT else P
        nc.vector.tensor_tensor(a.ctx[0:rows, :], k.bank_u[0:rows, :], a.inv[0:rows, :], ALU.mult).then_inc(a.ctx_ready, 1)

    def leaky(i, g):
        dve.wait_ge(a.biased_ready, at("biased_ready", 2 * i + g + 1))
        rows = k.F if insts[i] == OUT else P
        nc.vector.scalar_tensor_tensor(out=a.leaky[0:rows, :], in0=a.biased[0:rows, :], scalar=0.01, in1=a.biased[0:rows, :],
                                       op0=ALU.mult, op1=ALU.max).then_inc(a.leaky_ready, 1)

    def own_steps(step):
        i, c = divmod(step, 8)
        if c == 0 and i >= 1:
            rinv(i - 1, 1)
            context(i - 1, 0)
        elif c == 1 and i >= 1:
            leaky(i - 1, 0)
        elif c == 4:
            if i < NI:
                rinv(i, 0)
            if i >= 1:
                context(i - 1, 1)
        elif c == 6 and i >= 1:
            leaky(i - 1, 1)

    def slot(step):
        for m, (st, kind, j, h) in enumerate(slots):
            if st != step or kind in ("sums", "head"):
                continue
            inst = insts[j]
            if kind in ("project", "next"):
                n = order.index(inst)
                dve.wait_ge(a.keys_hi_ready, at("keys_hi_ready", 2 * n + h + 1) if kind == "project" else at_next("keys_hi_ready", h + 1))
                keys_lo(nc, k, a, n, h)
            elif kind == "mix":
                dve.wait_ge(a.slot_done, at("slot_done", m + 1))
                acc = a.h2[:, h * 512:(h + 1) * 512]
                if inst == order[0]:
                    nc.vector.tensor_copy(acc, k.bank_m[:, :]).then_inc(a.mixed, 1)
                else:
                    nc.vector.tensor_tensor(acc, acc, k.bank_m[:, :], ALU.add).then_inc(a.mixed, 1)
                dve.wait_ge(a.mixed, at("mixed", 2 * order.index(inst) + h + 1))
            else:
                dve.wait_ge(a.slot_done, at("slot_done", m + 1))
                slot_b = bass.ds(b, 1) if not isinstance(b, int) else slice(b, b + 1)
                nc.vector.tensor_copy(a.delta[:, slot_b, 4 * h:4 * h + 4, :].rearrange("p b c f -> p (b c) f"),
                                      k.bank_m[:, :].rearrange("p (c f) -> p c f", f=P)[:, :, 0:k.F]).then_inc(a.out_stored, 1)

    if insts[0] != OUT:
        nc.vector.tensor_copy(a.v_parts[:, :, 0, :], k.xn[:, k.NC // 2:, bass.ds(b, 1), :].rearrange("p c b f -> p (c b) f")).then_inc(a.v_hi_ready, 1)
        nc.vector.tensor_copy(a.v[:, :, 0:k.F], k.xn[:, 0:k.NC // 2, bass.ds(b, 1), :].rearrange("p c b f -> p (c b) f")).then_inc(a.v_ready, 1)
        scaled_scores(0)
        shifted_scores(0)
    dve.wait_ge(a.vo_hi_ready, at("vo_hi_ready", 1))
    nc.vector.tensor_tensor(a.vo_lo[:, :, :], k.pair[:, :].rearrange("p (c f) -> p c f", f=P)[:, k.NC // 2:, 0:k.F],
                            f32(a.vo_hi[:, :, :]), ALU.subtract).then_inc(a.vo_ready, 1)
    dve.wait_ge(a.ko_hi_ready, at("ko_hi_ready", 1))
    nc.vector.tensor_copy(a.xo[0:k.F, :], f32(a.ko_hi[0:k.F, :])).then_inc(a.xo_hi_ready, 1)
    nc.vector.tensor_tensor(a.ko_lo[:, :], a.h2[:, :], f32(a.ko_hi[:, :]), ALU.subtract).then_inc(a.ko_lo_ready, 1)
    dve.wait_ge(a.ko_lo_ready, at("ko_lo_ready", 1))
    nc.vector.tensor_copy(a.xo[k.F:P, :], f32(a.ko_lo[k.F:P, :])).then_inc(a.xo_lo_ready, 1)
    if insts[0] == OUT:
        scaled_scores(0)
        shifted_scores(0)
    for step in range(ST + 8):
        if step == ST and at_next is not None:
            dve.wait_ge(a.shifted, at("shifted", ST))
            make_x_twice(nc, k, a, b + 1)
        own_steps(step)
        if step == ST + 1 and at_next is not None:
            low_parts_of_xt(nc, k, a, dve, at_next)
        if step >= 2:
            slot(step - 2)
        if step + 1 < ST:
            shifted_scores(step + 1)


def attention_gpsimd(nc, k, a, pool, insts, b, at):
    if insts[0] != OUT:
        x_half = k.xn[:, k.NC // 2:, bass.ds(b, 1), :].rearrange("p c b f -> p (c b) f")
        pool.wait_ge(a.v_hi_ready, at("v_hi_ready", 1))
        nc.gpsimd.tensor_tensor(a.v_parts[:, :, 1, :], x_half, f32(a.v_parts[:, :, 0, :]), ALU.subtract).then_inc(a.v_split, 1)
    for q in range(8 * len(insts)):
        g, columns = q % 8 // 4, slice((q % 4) * P, (q % 4 + 1) * P)
        pool.wait_ge(a.turned_read, at("turned_read", 2 * q + 2))
        nc.gpsimd.tensor_tensor(a.probs_lo[g][:, :, columns], a.probs_whole[:, :, :], f32(a.probs_hi[g][:, :, columns]), ALU.subtract).then_inc(a.probs_split, 1)


def graph_attention(nc, k, adj, Wh, bh, W_out, b_out):
    NC, B, N, F, HEADS = k.NC, k.B, k.N, k.F, Wh.shape[0]
    with ExitStack() as ctx:
        def sb(n, s, d=F32):
            return ctx.enter_context(nc.sbuf_tensor("l2_" + n, s, d))

        def sem(n):
            return k.sem("l2_" + n)

        a = Ctx()
        a.gram_hi, a.gram_lo = sb("gram_hi", [P, HEADS, P], F32R), sb("gram_lo", [P, HEADS, P], F32R)
        a.wh, a.wo = sb("wh", [P, HEADS, P]), sb("wo", [P, HEADS, 2, F])
        a.v_parts, a.ident_r = sb("v_parts", [P, NC // 2, 2, F], F32R), sb("ident_r", [P, P], F32R)
        a.probs_hi, a.probs_lo = ([sb(f"probs_{w}{i}", [P, NC // 2, 512], F32R) for i in range(2)] for w in ("hi", "lo"))
        a.rinv_hi, a.rinv_lo = sb("rinv_hi", [P, 16], F32R), sb("rinv_lo", [P, 16], F32R)
        a.bh, a.b_out = sb("bh", [P, HEADS]), sb("b_out", [F, 1])
        a.v, a.vo = sb("v", [P, NC // 2, P]), sb("vo", [P, NC // 2, F])
        a.vo_hi, a.vo_lo = sb("vo_hi", [P, NC // 2, F], F32R), sb("vo_lo", [P, NC // 2, F], F32R)
        a.xt, a.xo = sb("xt", [P, N], F32R), sb("xo", [P, N], F32R)
        a.keys_hi, a.keys_lo = ([sb(f"keys_{w}{i}", [P, N], F32R) for i in range(2)] for w in ("hi", "lo"))
        a.ko_hi, a.ko_lo = sb("ko_hi", [P, N], F32R), sb("ko_lo", [P, N], F32R)
        a.scaled_scores = [sb(f"scaled_scores{i}", [P, N]) for i in range(2)]
        a.neg_scores = [sb(f"neg_scores{i}", [P, N]) for i in range(2)]
        a.probs = [sb(f"probs{i}", [P, N]) for i in range(2)]
        a.probsT = [sb(f"probsT{i}", [P, NC // 2, 512]) for i in range(2)]
        a.probs_whole = sb("probs_whole", [P, NC // 2, P])
        a.neg_max, a.sums, a.rinv = sb("neg_max", [P, 16]), sb("sums", [P, 16]), sb("rinv", [P, 16])
        a.inv, a.ctx = sb("inv", [P, 512]), sb("ctx", [P, 512])
        a.biased, a.h2 = sb("biased", [P, 512]), sb("h2", [P, N])
        a.leaky = a.biased
        a.x_twice = a.scaled_scores[1][:, :].rearrange("p (c f) -> p c f", f=P)
        a.delta = k.delta
        whT = a.scaled_scores[1][:, :].rearrange("p (h t c) -> p h t c", t=2, c=F)

        insts = a.insts = [0, OUT] + list(range(1, HEADS))
        ni, nh = len(insts), HEADS
        per = {"keys_ready": 2 * nh, "keys_hi_ready": 2 * nh, "inv_ready": 2 * ni, "biased_ready": 2 * ni, "mixed": 2 * nh,
               "out_stored": 2, "xt_lo_ready": 1, "xt_hi_ready": 1, "rinv_ready": 2 * ni, "ctx_ready": 2 * ni,
               "leaky_ready": 2 * ni, "vo_ready": 1, "scaled": 8 * ni, "ko_lo_ready": 1, "xo_lo_ready": 1,
               "probs_ready": 8 * ni, "turned_read": 16 * ni, "v_ready": 1, "turned": 16 * ni, "shifted": 8 * ni,
               "scores_ready": 8 * ni, "filled": 8 * ni, "values_done": 2 * ni, "slot_done": len(attention_slots(insts, True)),
               "rinv_step": 4 * ni, "v_hi_ready": 1, "x_ready": 1, "v_split": 1, "probs_split": 8 * ni, "vo_hi_ready": 1, "xt_in_psum": 1, "vo_in_psum": 1, "ko_hi_ready": 1, "xo_hi_ready": 1}
        a.keys_ready, a.keys_hi_ready, a.inv_ready, a.biased_ready, a.mixed, a.out_stored = (
            sem(n) for n in ("keys_ready", "keys_hi_ready", "inv_ready", "biased_ready", "mixed", "out_stored"))
        a.xt_lo_ready, a.xt_hi_ready, a.rinv_ready, a.ctx_ready, a.leaky_ready, a.vo_ready = (
            sem(n) for n in ("xt_lo_ready", "xt_hi_ready", "rinv_ready", "ctx_ready", "leaky_ready", "vo_ready"))
        a.scaled, a.ko_lo_ready, a.xo_lo_ready, a.probs_ready, a.turned_read, a.v_ready = (
            sem(n) for n in ("scaled", "ko_lo_ready", "xo_lo_ready", "probs_ready", "turned_read", "v_ready"))
        a.turned, a.shifted, a.scores_ready, a.filled, a.values_done, a.slot_done = (
            sem(n) for n in ("turned", "shifted", "scores_ready", "filled", "values_done", "slot_done"))
        a.xt_in_psum, a.vo_in_psum, a.ko_hi_ready, a.xo_hi_ready = (
            sem(n) for n in ("xt_in_psum", "vo_in_psum", "ko_hi_ready", "xo_hi_ready"))
        a.rinv_step, a.v_hi_ready, a.v_split, a.probs_split, a.x_ready, a.vo_hi_ready = (
            sem(n) for n in ("rinv_step", "v_hi_ready", "v_split", "probs_split", "x_ready", "vo_hi_ready"))
        adj_loaded, w_loaded, h2_zeroed, whT_in_psum, whT_ready, gram_in_psum, gram_hi_ready, gram_ready = (
            sem(n) for n in ("adj_loaded", "w_loaded", "h2_zeroed", "whT_in_psum", "whT_ready", "gram_in_psum", "gram_hi_ready", "gram_ready"))

        def counted(b, ahead=2):
            return lambda name, n: b * per[name] + n + (ahead if name == "slot_done" else 0)

        with nc.Block() as block:
            @block.sync
            def _(sp):
                for t in range(2):
                    sp.dma_start(a.wh[t * F:(t + 1) * F, :, :], Wh.rearrange("h c d -> c h d")).then_inc(w_loaded, 16)
                for t in range(2):
                    sp.dma_start(a.wo[:, :, t, :], W_out.rearrange("(h d) o -> d h o", d=P)).then_inc(w_loaded, 16)
                sp.dma_start(a.bh[:, :], bh.rearrange("h d -> d h"), allow_slow_non_contiguous=True).then_inc(w_loaded, 16)
                sp.dma_start(a.b_out[:, :], b_out.rearrange("(o a) -> o a", a=1), allow_slow_non_contiguous=True).then_inc(w_loaded, 16)
                for c in range(NC):
                    sp.dma_start(k.adj[:, c, :], adj[c * P:(c + 1) * P, :]).then_inc(adj_loaded, 16)

            @block.tensor
            def _(pe):
                pe.wait_ge(w_loaded, 96)
                for h in range(HEADS):
                    last = nc.tensor.transpose(k.bank_u[:, h * F:(h + 1) * F], a.wh[0:F, h, :], k.ident[0:F, 0:F])
                last.then_inc(whT_in_psum, 1)
                pe.wait_ge(whT_ready, 2)
                for h in range(HEADS):
                    w = whT[:, h, :, :].rearrange("p t c -> p (t c)")
                    last = nc.tensor.matmul(k.wide[0][:, h * P:(h + 1) * P], w, w, start=True, stop=True)
                last.then_inc(gram_in_psum, 1)

            @block.scalar
            def _(act):
                act.wait_ge(whT_in_psum, 1)
                for t in range(2):
                    nc.scalar.activation(whT[:, :, t, :], k.bank_u[:, :].rearrange("p (h c) -> p h c", c=F), ACT.Copy).then_inc(whT_ready, 1)
                act.wait_ge(gram_in_psum, 1)
                nc.scalar.activation(a.gram_hi[:, :, :].rearrange("p h c -> p (h c)"), k.wide[0][:, :], ACT.Copy).then_inc(gram_hi_ready, 1)
                nc.scalar.preload_act_table(ACT.Exp)

            @block.vector
            def _(dve):
                nc.vector.memset(a.h2[:, :], 0.0).then_inc(h2_zeroed, 1)
                nc.vector.memset(a.v[:, :, F:], 0.0).then_inc(h2_zeroed, 1)
                nc.vector.tensor_copy(a.ident_r[:, :], k.ident[:, :]).then_inc(h2_zeroed, 1)
                dve.wait_ge(gram_hi_ready, 1)
                nc.vector.tensor_tensor(a.gram_lo[:, :, :].rearrange("p h c -> p (h c)"), k.wide[0][:, :],
                                        f32(a.gram_hi[:, :, :]).rearrange("p h c -> p (h c)"), ALU.subtract).then_inc(gram_ready, 1)
                dve.wait_ge(adj_loaded, 16 * NC)

        def over_batches(engine, part):
            with engine.Fori(0, B - 1) as b:
                part(insts, b, counted(b), counted(b + 1))
            part(insts, B - 1, counted(B - 1), None)
            part([OUT], B, counted(B, ahead=0), None)

        with nc.Block() as block:
            @block.tensor
            def _(pe):
                transpose_x(nc, k, a, pe, counted(0))
                pe.wait_ge(a.xt_lo_ready, 1)
                for h in range(2):
                    if h == 1:
                        pe.wait_ge(a.keys_ready, 1)
                    project_keys(nc, k, a, 0, h).then_inc(a.slot_done, 1)
                over_batches(pe, lambda *args: attention_tensor(nc, k, a, pe, *args))

            @block.scalar
            def _(act):
                copy_xt(nc, k, a, act, counted(0))
                for h in range(2):
                    act.wait_ge(a.slot_done, h + 1)
                    keys_hi(nc, k, a, 0, h)
                over_batches(act, lambda *args: attention_scalar(nc, k, a, act, *args))

            @block.vector
            def _(dve):
                make_x_twice(nc, k, a, 0)
                low_parts_of_xt(nc, k, a, dve, counted(0))
                for h in range(2):
                    dve.wait_ge(a.keys_hi_ready, h + 1)
                    keys_lo(nc, k, a, 0, h)
                over_batches(dve, lambda *args: attention_vector(nc, k, a, dve, *args))

            @block.gpsimd
            def _(pool):
                over_batches(pool, lambda insts, b, at, at_next: attention_gpsimd(nc, k, a, pool, insts, b, at))



def industry_messages(nc, k, W_ind, ind_dram):
    NC, B, F, N = k.NC, k.B, k.F, k.N
    BP, HV = B // 2, N // 512
    with ExitStack() as ctx:
        sb = lambda n, s, d=F32: ctx.enter_context(nc.sbuf_tensor("ind_" + n, s, d))
        sem = lambda n: k.sem("ind_" + n)
        k.at_hi, k.at_lo = sb("at_hi", [P, NC, N], F32R), sb("at_lo", [P, NC, N], F32R)
        z = sb("split", [P, NC, 2, B, F], F32R)
        w2, deg, rdeg = sb("w2", [P, P]), sb("deg", [P, NC]), sb("rdeg", [P, NC])
        deg_ready = sem("deg_ready")
        agg = [sb(f"agg{i}", [P, 512]) for i in range(2)]
        ind = [sb(f"ind{i}", [P, 512]) for i in range(2)]
        rdeg_rows = sb("rdeg_rows", [P, N])
        zeroed, w_loaded, transposed, hi_ready, lo_ready, z_hi, z_lo, rdeg_ready, rdeg_in_psum, rdeg_rows_ready = (
            sem(n) for n in ("zeroed", "w_loaded", "transposed", "hi_ready", "lo_ready", "z_hi", "z_lo", "rdeg_ready", "rdeg_in_psum", "rdeg_rows_ready"))
        prod_ready, agg_ready, ind_in_psum, ind_ready = (sem(n) for n in ("prod_ready", "agg_ready", "ind_in_psum", "ind_ready"))
        stored = [sem(f"stored{i}") for i in range(2)]
        prod = [k.bank_u[:, :], k.bank_m[:, :]]
        indp = [k.pair[:, 0:512], k.pair[:, 512:1024]]
        with nc.Block() as block:
            @block.sync
            def _(sp):
                sp.wait_ge(zeroed, 1)
                for i in range(2):
                    sp.dma_start(w2[i * F:(i + 1) * F, i * F:(i + 1) * F], W_ind).then_inc(w_loaded, 16)
                for g in range(BP * HV):
                    bp, half = g // HV, g % HV
                    sp.wait_ge(ind_ready, g + 1)
                    sp.dma_start(ind_dram[2 * bp:2 * bp + 2, :, half * 512:(half + 1) * 512].rearrange("b f n -> (b f) n"),
                                 ind[g % 2][:, :]).then_inc(stored[g % 2], 16)
                for i in range(2):
                    sp.wait_ge(stored[i], 16 * BP * HV // 2)

            @block.gpsimd
            def _(pool):
                nc.gpsimd.memset(w2[:, :], 0.0).then_inc(zeroed, 1)

            @block.tensor
            def _(pe):
                for mc in range(NC):
                    if mc >= 2:
                        pe.wait_ge(lo_ready, mc - 1)
                    for c in range(NC):
                        last = nc.tensor.transpose(k.wide[mc % 2][:, c * P:(c + 1) * P], k.adj[:, c, mc * P:(mc + 1) * P], k.ident[:, :])
                    last.then_inc(transposed, 1)
                pe.wait_ge(w_loaded, 32)
                pe.wait_ge(lo_ready, NC)
                pe.wait_ge(z_lo, 1)

                def message(g):
                    pe.wait_ge(agg_ready, g + 1)
                    if g >= 2:
                        pe.wait_ge(ind_ready, g - 1)
                    nc.tensor.matmul(indp[g % 2], w2[:, :], agg[g % 2][:, :], start=True, stop=True).then_inc(ind_in_psum, 1)

                for g in range(BP * HV):
                    if g >= 2:
                        pe.wait_ge(agg_ready, g - 1)
                    product_transposed(nc, k, pe, z, prod[g % 2], g // HV, g % HV).then_inc(prod_ready, 1)
                    if g == 0:
                        pe.wait_ge(rdeg_ready, 2)
                        for c in range(NC):
                            last = nc.tensor.matmul(k.pair[:, c * P:(c + 1) * P], rdeg[:, c:c + 1].broadcast_to([P, P]), k.ident[:, :], start=True, stop=True)
                        last.then_inc(rdeg_in_psum, 1)
                    if g == 1:
                        pe.wait_ge(rdeg_rows_ready, 1)
                    if g >= 1:
                        message(g - 1)
                message(BP * HV - 1)

            @block.scalar
            def _(act):
                nc.scalar.activation(z[:, :, 0, :, :].rearrange("p c b f -> p c (b f)"),
                                     k.xn[:, :, :, :].rearrange("p c b f -> p c (b f)"), ACT.Copy).then_inc(z_hi, 1)
                for mc in range(NC):
                    act.wait_ge(transposed, mc + 1)
                    nc.scalar.activation(k.at_hi[:, mc, :], k.wide[mc % 2][:, :], ACT.Copy).then_inc(hi_ready, 1)
                for g in range(BP * HV):
                    act.wait_ge(prod_ready, g + 1)
                    if g >= 2:
                        act.wait_ge(ind_in_psum, g - 1)
                    nc.scalar.activation(agg[g % 2][:, :], prod[g % 2], ACT.Copy).then_inc(agg_ready, 1)
                    if g == 0:
                        act.wait_ge(rdeg_in_psum, 1)
                        nc.scalar.activation(rdeg_rows[:, :], k.pair[:, :], ACT.Copy).then_inc(rdeg_rows_ready, 1)

            @block.vector
            def _(dve):
                dve.wait_ge(z_hi, 1)
                nc.vector.tensor_tensor(z[:, :, 1, :, :].rearrange("p c b f -> p c (b f)"),
                                        k.xn[:, :, :, :].rearrange("p c b f -> p c (b f)"),
                                        f32(z[:, :, 0, :, :]).rearrange("p c b f -> p c (b f)"), ALU.subtract).then_inc(z_lo, 1)
                for mc in range(NC):
                    dve.wait_ge(hi_ready, mc + 1)
                    nc.vector.tensor_tensor(k.at_lo[:, mc, :], k.wide[mc % 2][:, :], f32(k.at_hi[:, mc, :]), ALU.subtract).then_inc(lo_ready, 1)
                for c in range(NC):
                    nc.vector.reduce_sum(deg[:, c:c + 1], k.adj[:, c, :], axis=AX_X).then_inc(deg_ready, 1)
                dve.wait_ge(deg_ready, NC)
                nc.vector.tensor_scalar(rdeg[:, :], deg[:, :], 1.0, None, ALU.max).then_inc(rdeg_ready, 1)
                dve.wait_ge(rdeg_ready, 1)
                nc.vector.reciprocal(rdeg[:, :], rdeg[:, :]).then_inc(rdeg_ready, 1)
                for g in range(BP * HV):
                    dve.wait_ge(ind_in_psum, g + 1)
                    if g >= 2:
                        dve.wait_ge(stored[g % 2], 16 * (g // 2))
                    half = g % HV
                    nc.vector.tensor_tensor(ind[g % 2][:, :], indp[g % 2], rdeg_rows[:, half * 512:(half + 1) * 512], ALU.mult).then_inc(ind_ready, 1)


def hypergraph_attention(nc, k, params, ind_dram):
    H, W, a_node, a_gn, a_ge, fcW, fcb, av = params
    NC, B, F, N, E = k.NC, k.B, k.F, k.N, H.shape[1]
    EP = E // 2
    HS = [slice(0, 512), slice(512, 1024)]
    with ExitStack() as ctx:
        sb = lambda n, s, d=F32: ctx.enter_context(nc.sbuf_tensor("l3_" + n, s, d))
        sem = lambda n: k.sem("l3_" + n)
        w_dup, fcw = sb("w_dup", [F, 2, F]), sb("fcw", [F, P])
        cols = sb("cols", [P, 8])
        h_raw = sb("h_raw", [P, NC, E])
        mask, fill = sb("mask", [P, NC, 2, E]), sb("fill", [P, NC, E])
        maskT, fillT = sb("maskT", [P, N]), sb("fillT", [P, N])
        pick, fold, ones = sb("pick", [P, EP, 2, F], F32R), sb("fold", [P, 2, F]), sb("ones", [F, P])
        dup_ident = sb("dup_ident", [P, E])
        xT, hn = sb("xT", [P, N]), sb("hn", [P, NC, P])
        hT, hsum, beta_s, c_s = ([sb(f"{n}{i}", [P, N], d) for i in range(2)] for n, d in (("hT", F32), ("hsum", F32), ("beta_s", F32R), ("c_s", F32R)))
        agg_e, nagg_e = ([sb(f"{n}{i}", [P, EP]) for i in range(2)] for n in ("agg_e", "nagg_e"))
        t0, t1, t2 = sb("t0", [P, N]), sb("t1", [P, N]), sb("t2", [P, N])
        x2 = t1[:, :].rearrange("p (c f) -> p c f", f=P)
        alphaT = xT[:, :].rearrange("p (c e) -> p c e", e=P)
        small = sb("small", [P, 16])
        aggT = sb("aggT", [P, 2, E])
        agg_less_1, neg_agg = sb("agg_less_1", [P, P]), sb("neg_agg", [P, P])
        agg_min, he, tanh_e = sb("agg_min", [P, E]), sb("he", [P, E]), sb("tanh_e", [P, E])
        beta, gate = sb("beta", [P, N]), sb("gate", [P, N])
        lg, coef = sb("lg", [P, NC, E]), sb("coef", [P, NC, 2, E])
        c8 = sb("c8", [P, 3, NC])
        cT, cbeta = sb("cT", [P, N]), sb("cbeta", [P, N])
        w_t, r_t, e_t = ([sb(f"{n}_{i}", [P, N]) for i in range(3)] for n in ("w", "r", "e"))
        u_t, p_t = ([sb(f"{n}_{i}", [P, N]) for i in range(2)] for n in ("u", "p"))
        LEAD = 3
        fetches = [("beta", e) for e in range(LEAD)]
        for e in range(EP):
            fetches += [("beta", e + LEAD)] * (e + LEAD < EP) + [("c", e)]
        rows_of = {fetch: k.wide[f % 2] for f, fetch in enumerate(fetches)}
        ind = sb("ind", [P, N])
        g = sb("g", [P, N])

        s = Ctx()
        s.loaded, s.consts, s.maskT_in_psum, s.x_ready, s.xT_in_psum, s.xT_ready = (
            sem(n) for n in ("loaded", "consts", "maskT_in_psum", "x_ready", "xT_in_psum", "xT_ready"))
        s.hT_in_psum, s.hn_in_psum, s.hT_ready, s.hn_ready, s.node_logits, s.gate_logits = (
            sem(n) for n in ("hT_in_psum", "hn_in_psum", "hT_ready", "hn_ready", "node_logits", "gate_logits"))
        s.logits_copied, s.gate_copied, s.alpha_step, s.alpha_shifted, s.alpha_exp, s.alpha_ready = (
            sem(n) for n in ("logits_copied", "gate_copied", "alpha_step", "alpha_shifted", "alpha_exp", "alpha_ready"))
        s.alphaT_in_psum, s.alphaT_ready, s.agg_in_psum, s.agg_step, s.agg_exp, s.he_ready = (
            sem(n) for n in ("alphaT_in_psum", "alphaT_ready", "agg_in_psum", "agg_step", "agg_exp", "he_ready"))
        s.edge_in_psum, s.tanh_e_ready, s.half_age_ready, s.score_in_psum, s.gate_tanh, s.beta_ready = (
            sem(n) for n in ("edge_in_psum", "tanh_e_ready", "half_age_ready", "score_in_psum", "gate_tanh", "beta_ready"))
        s.beta_hi, s.beta_split, s.coef_step, s.coef_exp, s.coef_masked, s.coef_rinv = (
            sem(n) for n in ("beta_hi", "beta_split", "coef_step", "coef_exp", "coef_masked", "coef_rinv"))
        s.coef_half, s.coef_ready, s.cT_in_psum, s.cT_ready, s.c_split, s.cbeta_ready = (
            sem(n) for n in ("coef_half", "coef_ready", "cT_in_psum", "cT_ready", "c_split", "cbeta_ready"))
        s.hsum_in_psum, s.hsum_ready, s.closed, s.beta_rows, s.c_rows, s.w_done = (
            sem(n) for n in ("hsum_in_psum", "hsum_ready", "closed", "beta_rows", "c_rows", "w_done"))
        s.r_done, s.e_done, s.u_done, s.p_done, s.summed, s.g_ready = (
            sem(n) for n in ("r_done", "e_done", "u_done", "p_done", "summed", "g_ready"))
        s.ind_loaded, s.tanh_i_in_psum, s.tanh_i_ready, s.tanh_g_in_psum, s.tanh_g_ready, s.diff_ready = (
            sem(n) for n in ("ind_loaded", "tanh_i_in_psum", "tanh_i_ready", "tanh_g_in_psum", "tanh_g_ready", "diff_ready"))
        s.mix_in_psum, s.mix_tanh, s.mix_step, s.outT_ready, s.out_in_psum, s.out_stored = (
            sem(n) for n in ("mix_in_psum", "mix_tanh", "mix_step", "outT_ready", "out_in_psum", "out_stored"))

        with nc.Block() as block:
            @block.sync
            def _(sp):
                for i in range(2):
                    sp.dma_start(w_dup[:, i, :], W).then_inc(s.loaded, 16)
                sp.dma_start(fcw[:, :], fcW).then_inc(s.loaded, 16)
                for i, v in enumerate((a_node, a_gn, a_ge, fcb, av)):
                    sp.dma_start(cols[0:v.shape[0], i:i + 1], v.rearrange("(f a) -> f a", a=1), allow_slow_non_contiguous=True).then_inc(s.loaded, 16)
                sp.dma_start(h_raw[:, :, :], H.rearrange("(c p) e -> p c e", p=P)).then_inc(s.loaded, 16)

            @block.vector
            def _(dve):
                dve.wait_ge(s.loaded, 16 * 9)
                nc.vector.tensor_scalar(cols[:, 5:6], cols[:, 4:5], -1.0, None, ALU.mult).then_inc(s.consts, 1)
                for i in range(2):
                    nc.vector.tensor_scalar(mask[:, :, i, :], h_raw[:, :, :], 0.0, None, ALU.is_gt).then_inc(s.consts, 1)
                nc.vector.memset(ones[:, :], 1.0).then_inc(s.consts, 1)
                nc.vector.tensor_tensor(dup_ident[:, :], k.ident[:, 0:E], k.ident[:, E:2 * E], ALU.add).then_inc(s.consts, 1)
                dve.wait_ge(s.consts, 5)
                nc.vector.tensor_scalar(fill[:, :, :], mask[:, :, 0, :], -1.0, -NEG, ALU.add, ALU.mult).then_inc(s.consts, 1)
                for i in range(2):
                    nc.vector.tensor_copy(fold[:, i, :], dup_ident[:, :]).then_inc(s.consts, 1)
                nc.vector.tensor_copy(pick[:, :, :, :], dup_ident[:, :].rearrange("p (j e) -> p e j", j=2).unsqueeze(3).broadcast_to([P, EP, 2, F])).then_inc(s.consts, 1)
                dve.wait_ge(s.maskT_in_psum, 1)
                nc.vector.tensor_copy(maskT[:, :], k.wide[0][:, :]).then_inc(s.consts, 1)
                dve.wait_ge(s.consts, 10)
                nc.vector.tensor_scalar(fillT[:, :], maskT[:, :], -1.0, -NEG, ALU.add, ALU.mult).then_inc(s.consts, 1)

            @block.tensor
            def _(pe):
                pe.wait_ge(s.consts, 5)
                for c in range(NC):
                    last = nc.tensor.transpose(k.wide[0][:, c * P:(c + 1) * P], mask[:, c, :, :].rearrange("p t e -> p (t e)"), k.ident[:, :])
                last.then_inc(s.maskT_in_psum, 1)

            @block.scalar
            def _(act):
                nc.scalar.preload_act_table(ACT.Exp)

        SLOT_AT = {"score_ind": 0, "score_g": 1, "mix": 3, "store": 5, "x": 7, "h": 9, "h_nodes": 10, "logits": 12, "gates": 13,
                   "alphaT": 15, "agg": 17, "elu_agg": 18, "edges": 20, "scores": 22, "coef": 24, "coefT": 26, "hsum": 28}
        FINISH, PREPARE = list(SLOT_AT)[:4], list(SLOT_AT)[4:]
        spare = k.spare

        def run_slots(slot, e, lag, last, following):
            for name, at in SLOT_AT.items():
                if at + lag == e or (e == EP and at + lag >= EP):
                    batch = last if name in FINISH else following
                    if batch is not None:
                        slot(name, batch)

        def over_batches(engine, prepare, batch, finish):
            prepare(0, 0)
            batch(0, 0, None, 1)
            with engine.Fori(1, B - 2, step=2) as b:
                batch(b, 1, b - 1, b + 1)
                batch(b + 1, 0, b, b + 2)
            batch(B - 1, 1, B - 2, None)
            finish(B - 1)

        w_flat = w_dup[:, :, :].rearrange("p t f -> p (t f)")

        with nc.Block() as block:
            @block.sync
            def _(sp):
                def load(b):
                    for i in range(2):
                        sp.dma_start(ind[i * F:(i + 1) * F, :], ind_dram[bass.ds(b, 1), :, :].rearrange("b f n -> (b f) n")).then_inc(s.ind_loaded, 16)

                load(0)
                with sp.Fori(1, B) as b:
                    sp.wait_ge(s.outT_ready, b)
                    load(b)

            @block.tensor
            def _(pe):
                def spread_halves(stationary, moving):
                    for hs in HS:
                        last = nc.tensor.matmul(spare[:, hs], stationary, moving[:, hs], start=True, stop=True)
                    return last

                def slot(name, b, o):
                    if name == "score_ind":
                        pe.wait_ge(s.hsum_ready, b + 1)
                        pe.wait_ge(s.ind_loaded, b * 32 + 32)
                        spread_halves(fcw[:, :], ind[0:F, :]).then_inc(s.tanh_i_in_psum, 1)
                    elif name == "score_g":
                        pe.wait_ge(s.tanh_i_ready, b + 1)
                        pe.wait_ge(s.g_ready, b + 1)
                        spread_halves(fcw[:, :], g[0:F, :]).then_inc(s.tanh_g_in_psum, 1)
                    elif name == "mix":
                        pe.wait_ge(s.diff_ready, b + 1)
                        spread_halves(cols[:, 4:5].broadcast_to([P, P]), t2).then_inc(s.mix_in_psum, 1)
                    elif name == "store":
                        pe.wait_ge(s.outT_ready, b + 1)
                        for c in range(NC):
                            last = nc.tensor.transpose(spare[:, c * P:(c + 1) * P], t1[:, c * P:(c + 1) * P], k.ident[:, :])
                        last.then_inc(s.out_in_psum, 1)
                    elif name == "x":
                        pe.wait_ge(s.x_ready, b + 1)
                        for c in range(NC):
                            last = nc.tensor.transpose(spare[:, c * P:(c + 1) * P], x2[:, c, :], k.ident[:, :])
                        last.then_inc(s.xT_in_psum, 1)
                    elif name == "h":
                        pe.wait_ge(s.xT_ready, b + 1)
                        spread_halves(w_flat, xT[0:F, :]).then_inc(s.hT_in_psum, 1)
                    elif name == "h_nodes":
                        pe.wait_ge(s.hT_ready, b + 1)
                        for c in range(NC):
                            last = nc.tensor.matmul(spare[:, c * P:(c + 1) * P], xT[0:F, c * P:(c + 1) * P], w_flat, start=True, stop=True)
                        last.then_inc(s.hn_in_psum, 1)
                    elif name == "logits":
                        pe.wait_ge(s.hn_ready, b + 1)
                        spread_halves(cols[0:F, 0:1].broadcast_to([F, P]), hT[o][0:F, :]).then_inc(s.node_logits, 1)
                    elif name == "gates":
                        pe.wait_ge(s.logits_copied, b + 1)
                        spread_halves(cols[0:F, 1:2].broadcast_to([F, P]), hT[o][0:F, :]).then_inc(s.gate_logits, 1)
                    elif name == "alphaT":
                        pe.wait_ge(s.gate_copied, b + 1)
                        pe.wait_ge(s.alpha_ready, b + 1)
                        for c in range(NC):
                            last = nc.tensor.transpose(spare[:, c * P:(c + 1) * P], t2[:, c * P:(c + 1) * P], k.ident[:, :])
                        last.then_inc(s.alphaT_in_psum, 1)
                    elif name == "agg":
                        pe.wait_ge(s.alphaT_ready, b + 1)
                        for c in range(NC):
                            nc.tensor.matmul(spare[:, 0:E], hn[:, c, :], alphaT[:, c, 0:E], start=c == 0, stop=c == NC - 1)
                        for c in range(NC):
                            last = nc.tensor.matmul(spare[:, 512:512 + P], alphaT[:, c, :], hn[:, c, :], start=c == 0, stop=c == NC - 1)
                        last.then_inc(s.agg_in_psum, 1)
                    elif name == "edges":
                        pe.wait_ge(s.he_ready, b + 1)
                        nc.tensor.matmul(spare[:, 0:E], fcw[:, :], he[0:F, :], start=True, stop=True)
                        nc.tensor.matmul(spare[:, 512:513], aggT[0:F, :, :].rearrange("p t e -> p (t e)"), cols[0:F, 2:3], start=True, stop=True).then_inc(s.edge_in_psum, 1)
                    elif name == "scores":
                        pe.wait_ge(s.half_age_ready, b + 1)
                        pe.wait_ge(s.tanh_e_ready, b + 1)
                        nc.tensor.matmul(spare[:, 0:E], cols[:, 4:5].broadcast_to([P, P]), tanh_e[:, :], start=True, stop=True).then_inc(s.score_in_psum, 1)
                    elif name == "coefT":
                        pe.wait_ge(s.coef_ready, b + 1)
                        for c in range(NC):
                            last = nc.tensor.transpose(spare[:, c * P:(c + 1) * P], coef[:, c, :, :].rearrange("p t e -> p (t e)"), k.ident[:, :])
                        last.then_inc(s.cT_in_psum, 1)
                    elif name == "hsum":
                        pe.wait_ge(s.cbeta_ready, b + 1)
                        spread_halves(ones[:, :], cbeta[0:E, :]).then_inc(s.hsum_in_psum, 1)

                def batch(b, o, last_b, next_b):
                    def spread(f):
                        kind, e = fetches[f]
                        if f >= 2:
                            before, e2 = fetches[f - 2]
                            if before == "beta":
                                pe.wait_ge(s.w_done, b * EP + e2 + 1)
                            else:
                                pe.wait_ge(s.p_done, b * EP + e2 + 1)
                        src = beta_s[o] if kind == "beta" else c_s[o]
                        for hs in HS:
                            last = nc.tensor.matmul(rows_of[kind, e][:, hs], pick[:, e, :, :].rearrange("p j f -> p (j f)"), src[:, hs], start=True, stop=True)
                        last.then_inc(s.beta_rows if kind == "beta" else s.c_rows, 1)

                    def add_up(e, half):
                        if half == 0:
                            pe.wait_ge(s.p_done, b * EP + e + 1)
                        last = nc.tensor.matmul(k.pair[:, HS[half]], fold[:, :, :].rearrange("p t f -> p (t f)"), p_t[e % 2][:, HS[half]], start=False, stop=e == EP - 1)
                        if half == 1:
                            last.then_inc(s.summed, 1)

                    pe.wait_ge(s.beta_split, b + 1)
                    pe.wait_ge(s.c_split, b + 1)
                    for f in range(LEAD + 1):
                        spread(f)
                    pe.wait_ge(s.cbeta_ready, b + 1)
                    if last_b is not None:
                        pe.wait_ge(s.g_ready, b)
                    for hs in HS:
                        nc.tensor.matmul(k.pair[:, hs], agg_less_1[0:E, :], cT[0:E, hs], start=True, stop=False)
                        last = nc.tensor.matmul(k.pair[:, hs], neg_agg[0:E, :], cbeta[0:E, hs], start=False, stop=False)
                    last.then_inc(s.closed, 1)
                    for e in range(EP):
                        spread(fetches.index(("c", e)))
                        if e >= 1:
                            add_up(e - 1, 0)
                        if e + LEAD + 1 < EP:
                            spread(fetches.index(("beta", e + LEAD + 1)))
                        if e >= 1:
                            add_up(e - 1, 1)
                        run_slots(lambda name, bb: slot(name, bb, 1 - o), e, 0, last_b, next_b)
                    for half in range(2):
                        add_up(EP - 1, half)

                over_batches(pe, lambda b, o: [slot(n, b, o) for n in PREPARE], batch, lambda b: [slot(n, b, 1) for n in FINISH])

            @block.scalar
            def _(act):
                def slot(name, b, o):
                    if name == "score_ind":
                        act.wait_ge(s.tanh_i_in_psum, b + 1)
                        nc.scalar.activation(t0[:, :], spare[:, :], ACT.Tanh, bias=cols[:, 3:4]).then_inc(s.tanh_i_ready, 1)
                    elif name == "score_g":
                        act.wait_ge(s.tanh_g_in_psum, b + 1)
                        nc.scalar.activation(t1[:, :], spare[:, :], ACT.Tanh, bias=cols[:, 3:4]).then_inc(s.tanh_g_ready, 1)
                    elif name == "mix":
                        act.wait_ge(s.mix_in_psum, b + 1)
                        nc.scalar.activation(t0[:, :], spare[:, :], ACT.Tanh, scale=0.5).then_inc(s.mix_tanh, 1)
                    elif name == "x":
                        act.wait_ge(s.xT_in_psum, b + 1)
                        nc.scalar.activation(xT[:, :], spare[:, :], ACT.Copy).then_inc(s.xT_ready, 1)
                    elif name == "h":
                        act.wait_ge(s.hT_in_psum, b + 1)
                        nc.scalar.activation(hT[o][:, :], spare[:, :], ACT.Copy).then_inc(s.hT_ready, 1)
                    elif name == "logits":
                        act.wait_ge(s.node_logits, b + 1)
                        nc.scalar.activation(t0[:, :], spare[:, :], ACT.Copy).then_inc(s.logits_copied, 1)
                    elif name == "gates":
                        act.wait_ge(s.gate_logits, b + 1)
                        nc.scalar.activation(gate[:, :], spare[:, :], ACT.Copy).then_inc(s.gate_copied, 1)
                        act.wait_ge(s.alpha_shifted, b + 1)
                        nc.scalar.activation(t1[:, :], t0[:, :], ACT.Exp, bias=small[:, 0:1], scale=-1.0, accum_out=small[:, 1:2]).then_inc(s.alpha_exp, 1)
                    elif name == "alphaT":
                        act.wait_ge(s.alphaT_in_psum, b + 1)
                        nc.scalar.activation(xT[:, :], spare[:, :], ACT.Copy).then_inc(s.alphaT_ready, 1)
                    elif name == "elu_agg":
                        act.wait_ge(s.agg_step, b * 7 + 7)
                        nc.scalar.activation(agg_min[:, :], agg_min[:, :], ACT.Exp).then_inc(s.agg_exp, 1)
                    elif name == "edges":
                        act.wait_ge(s.edge_in_psum, b + 1)
                        nc.scalar.activation(tanh_e[:, :], spare[:, 0:E], ACT.Tanh, bias=cols[:, 3:4]).then_inc(s.tanh_e_ready, 1)
                    elif name == "scores":
                        act.wait_ge(s.half_age_ready, b + 1)
                        nc.scalar.activation(beta[:, :], gate[:, :], ACT.Tanh, bias=small[:, 3:4], scale=0.5).then_inc(s.gate_tanh, 1)
                    elif name == "coef":
                        act.wait_ge(s.coef_step, b * 4 + 4)
                        nc.scalar.activation(lg[:, :, :], lg[:, :, :], ACT.Exp).then_inc(s.coef_exp, 1)
                        act.wait_ge(s.beta_ready, b + 1)
                        nc.scalar.activation(beta_s[o][:, :], beta[:, :], ACT.Copy).then_inc(s.beta_hi, 1)
                    elif name == "coefT":
                        act.wait_ge(s.cT_in_psum, b + 1)
                        nc.scalar.activation(c_s[o][:, :], spare[:, :], ACT.Copy).then_inc(s.cT_ready, 1)
                        nc.scalar.activation(cT[:, :], spare[:, :], ACT.Copy).then_inc(s.cT_ready, 1)

                def batch(b, o, last_b, next_b):
                    for e in range(EP):
                        act.wait_ge(s.w_done, b * EP + e + 1)
                        if e >= 3:
                            act.wait_ge(s.u_done, b * EP + e - 2)
                        nc.scalar.activation(r_t[e % 3][:, :], w_t[e % 3][:, :], ACT.Relu, bias=nagg_e[o][:, e:e + 1], scale=-1.0).then_inc(s.r_done, 1)
                        act.wait_ge(s.r_done, b * EP + e + 1)
                        nc.scalar.activation(e_t[e % 3][:, :], r_t[e % 3][:, :], ACT.Exp, scale=-1.0).then_inc(s.e_done, 1)
                        run_slots(lambda name, bb: slot(name, bb, 1 - o), e, 4, last_b, next_b)
                    run_slots(lambda name, bb: slot(name, bb, 1 - o), EP, 4, last_b, next_b)

                over_batches(act, lambda b, o: [slot(n, b, o) for n in PREPARE], batch, lambda b: [slot(n, b, 1) for n in FINISH])

            @block.gpsimd
            def _(pool):
                with pool.Fori(0, B) as b:
                    for e in range(EP):
                        pool.wait_ge(s.e_done, b * EP + e + 1)
                        if e >= 2:
                            pool.wait_ge(s.p_done, b * EP + e - 1)
                        nc.gpsimd.tensor_tensor(u_t[e % 2][:, :], r_t[e % 3][:, :], e_t[e % 3][:, :], ALU.add).then_inc(s.u_done, 1)

            @block.vector
            def _(dve):
                def make_x2(b):
                    nc.vector.tensor_copy(x2.rearrange("p c (t f) -> p c t f", t=2),
                                          k.xn[:, :, bass.ds(b, 1), :].broadcast_to([P, NC, 2, F])).then_inc(s.x_ready, 1)

                def slot(name, b, o):
                    if name == "score_g":
                        dve.wait_ge(s.tanh_g_ready, b + 1)
                        nc.vector.tensor_tensor(t2[:, :], t1[:, :], t0[:, :], ALU.subtract).then_inc(s.diff_ready, 1)
                    elif name == "mix":
                        dve.wait_ge(s.diff_ready, b + 1)
                        dve.wait_ge(s.ind_loaded, b * 32 + 32)
                        nc.vector.tensor_tensor(t1[:, :], ind[:, :], g[:, :], ALU.subtract).then_inc(s.mix_step, 1)
                        dve.wait_ge(s.mix_tanh, b + 1)
                        nc.vector.tensor_scalar(t2[:, :], t0[:, :], -0.5, 0.5, ALU.mult, ALU.add).then_inc(s.mix_step, 1)
                        dve.wait_ge(s.mix_step, b * 3 + 2)
                        nc.vector.tensor_tensor(t0[:, :], t1[:, :], t2[:, :], ALU.mult).then_inc(s.mix_step, 1)
                        dve.wait_ge(s.mix_step, b * 3 + 3)
                        nc.vector.tensor_tensor(t1[:, :], t0[:, :], g[:, :], ALU.add).then_inc(s.outT_ready, 1)
                    elif name == "store":
                        dve.wait_ge(s.out_in_psum, b + 1)
                        nc.vector.tensor_copy(k.delta[:, bass.ds(b, 1), :, :].rearrange("p b c f -> p (b c) f"),
                                              spare[:, :].rearrange("p (c f) -> p c f", f=P)[:, :, 0:F]).then_inc(s.out_stored, 1)
                    elif name == "h_nodes":
                        dve.wait_ge(s.hn_in_psum, b + 1)
                        nc.vector.tensor_copy(hn[:, :, :].rearrange("p c f -> p (c f)"), spare[:, :]).then_inc(s.hn_ready, 1)
                    elif name == "logits":
                        dve.wait_ge(s.logits_copied, b + 1)
                        nc.vector.scalar_tensor_tensor(out=t1[:, :], in0=t0[:, :], scalar=0.2, in1=t0[:, :], op0=ALU.mult, op1=ALU.max).then_inc(s.alpha_step, 1)
                        dve.wait_ge(s.alpha_step, b * 4 + 1)
                        nc.vector.tensor_tensor(t2[:, :], t1[:, :], maskT[:, :], ALU.mult).then_inc(s.alpha_step, 1)
                        dve.wait_ge(s.alpha_step, b * 4 + 2)
                        nc.vector.memset(small[:, 4:5], 0.0).then_inc(s.alpha_step, 1)
                        nc.vector.tensor_tensor_reduce(out=t0[:, :], in0=t2[:, :], in1=fillT[:, :], scale=-1.0, scalar=3.0e38,
                                                       op0=ALU.add, op1=ALU.min, accum_out=small[:, 0:1]).then_inc(s.alpha_shifted, 1)
                    elif name == "gates":
                        dve.wait_ge(s.alpha_exp, b + 1)
                        nc.vector.reciprocal(small[:, 2:3], small[:, 1:2]).then_inc(s.alpha_step, 1)
                        dve.wait_ge(s.alpha_step, b * 4 + 4)
                        nc.vector.tensor_scalar(t2[:, :], t1[:, :], small[:, 2:3], None, ALU.mult).then_inc(s.alpha_ready, 1)
                    elif name == "agg":
                        if not (isinstance(b, int) and b == 0):
                            dve.wait_ge(s.closed, b)
                        dve.wait_ge(s.agg_in_psum, b + 1)
                        for i in range(2):
                            nc.vector.tensor_copy(aggT[:, i, :], spare[:, 0:E]).then_inc(s.agg_step, 1)
                        nc.vector.tensor_scalar(agg_less_1[:, :], spare[:, 512:512 + P], -1.0, None, ALU.add).then_inc(s.agg_step, 1)
                        nc.vector.tensor_scalar(neg_agg[:, :], spare[:, 512:512 + P], -1.0, None, ALU.mult).then_inc(s.agg_step, 1)
                        for i in range(2):
                            nc.vector.tensor_copy(agg_e[o][i * F:(i + 1) * F, :], spare[i * F:(i + 1) * F, i * EP:(i + 1) * EP]).then_inc(s.agg_step, 1)
                        nc.vector.tensor_scalar(agg_min[:, :], spare[:, 0:E], 0.0, None, ALU.min).then_inc(s.agg_step, 1)
                    elif name == "elu_agg":
                        dve.wait_ge(s.agg_exp, b + 1)
                        nc.vector.scalar_tensor_tensor(out=he[:, :], in0=aggT[:, 0, :], scalar=0.0, in1=agg_min[:, :], op0=ALU.max, op1=ALU.add).then_inc(s.coef_step, 1)
                        nc.vector.tensor_scalar(nagg_e[o][:, :], agg_e[o][:, :], -1.0, None, ALU.mult).then_inc(s.coef_step, 1)
                        dve.wait_ge(s.coef_step, b * 4 + 1)
                        nc.vector.tensor_scalar(he[:, :], he[:, :], -1.0, None, ALU.add).then_inc(s.he_ready, 1)
                    elif name == "edges":
                        dve.wait_ge(s.edge_in_psum, b + 1)
                        nc.vector.tensor_scalar(small[:, 3:4], spare[:, 512:513], 0.5, None, ALU.mult).then_inc(s.half_age_ready, 1)
                    elif name == "scores":
                        dve.wait_ge(s.score_in_psum, b + 1)
                        nc.vector.tensor_tensor(lg[:, :, :], mask[:, :, 0, :], spare[:, 0:E].unsqueeze(1).broadcast_to([P, NC, E]), ALU.mult).then_inc(s.coef_step, 1)
                        dve.wait_ge(s.coef_step, b * 4 + 3)
                        nc.vector.tensor_tensor(coef[:, :, 0, :], lg[:, :, :], fill[:, :, :], ALU.add).then_inc(s.coef_masked, 1)
                        dve.wait_ge(s.coef_masked, b * 3 + 1)
                        nc.vector.reduce_max(c8[:, 0, :], coef[:, :, 0, :], axis=AX_X).then_inc(s.coef_masked, 1)
                        dve.wait_ge(s.coef_masked, b * 3 + 2)
                        nc.vector.tensor_tensor(lg[:, :, :], coef[:, :, 0, :], c8[:, 0, :].unsqueeze(2).broadcast_to([P, NC, E]), ALU.subtract).then_inc(s.coef_step, 1)
                        dve.wait_ge(s.gate_tanh, b + 1)
                        nc.vector.tensor_scalar(beta[:, :], beta[:, :], 0.5, 0.5, ALU.mult, ALU.add).then_inc(s.beta_ready, 1)
                    elif name == "coef":
                        dve.wait_ge(s.coef_exp, b + 1)
                        nc.vector.reduce_sum(c8[:, 1, :], lg[:, :, :], axis=AX_X).then_inc(s.coef_masked, 1)
                        dve.wait_ge(s.coef_masked, b * 3 + 3)
                        nc.vector.reciprocal(c8[:, 2, :], c8[:, 1, :]).then_inc(s.coef_rinv, 1)
                        dve.wait_ge(s.coef_rinv, b + 1)
                        nc.vector.tensor_tensor(coef[:, :, 0, :], lg[:, :, :], c8[:, 2, :].unsqueeze(2).broadcast_to([P, NC, E]), ALU.mult).then_inc(s.coef_half, 1)
                        nc.vector.tensor_tensor(coef[:, :, 1, :], lg[:, :, :], c8[:, 2, :].unsqueeze(2).broadcast_to([P, NC, E]), ALU.mult).then_inc(s.coef_ready, 1)
                        dve.wait_ge(s.beta_hi, b + 1)
                        nc.vector.tensor_tensor(beta_s[o][E:P, :], beta[E:P, :], f32(beta_s[o][E:P, :]), ALU.subtract).then_inc(s.beta_split, 1)
                    elif name == "coefT":
                        dve.wait_ge(s.cT_ready, b * 2 + 2)
                        nc.vector.tensor_tensor(cbeta[:, :], cT[:, :], beta[:, :], ALU.mult).then_inc(s.cbeta_ready, 1)
                        nc.vector.tensor_tensor(c_s[o][E:P, :], cT[E:P, :], f32(c_s[o][E:P, :]), ALU.subtract).then_inc(s.c_split, 1)
                    elif name == "hsum":
                        dve.wait_ge(s.hsum_in_psum, b + 1)
                        nc.vector.tensor_tensor(hsum[o][:, :], hT[o][:, :], spare[:, :], ALU.mult).then_inc(s.hsum_ready, 1)

                def batch(b, o, last_b, next_b):
                    def gated(e):
                        dve.wait_ge(s.beta_rows, b * EP + e + 1)
                        if e >= 3:
                            dve.wait_ge(s.r_done, b * EP + e - 2)
                        nc.vector.scalar_tensor_tensor(out=w_t[e % 3][:, :], in0=hT[o][:, :], scalar=agg_e[o][:, e:e + 1], in1=rows_of["beta", e][:, :],
                                                       op0=ALU.subtract, op1=ALU.mult).then_inc(s.w_done, 1)

                    for e in range(LEAD):
                        gated(e)
                    for e in range(EP):
                        if e + LEAD < EP:
                            gated(e + LEAD)
                        run_slots(lambda name, bb: slot(name, bb, 1 - o), e, 2, last_b, next_b)
                        if e == SLOT_AT["store"] + 2 and next_b is not None:
                            make_x2(next_b)
                        dve.wait_ge(s.u_done, b * EP + e + 1)
                        dve.wait_ge(s.c_rows, b * EP + e + 1)
                        if e >= 2:
                            dve.wait_ge(s.summed, b * EP + e - 1)
                        nc.vector.tensor_tensor(p_t[e % 2][:, :], u_t[e % 2][:, :], rows_of["c", e][:, :], ALU.mult).then_inc(s.p_done, 1)
                    dve.wait_ge(s.summed, b * EP + EP)
                    nc.vector.tensor_tensor(g[:, :], hsum[o][:, :], k.pair[:, :], ALU.add).then_inc(s.g_ready, 1)

                def prepare(b, o):
                    make_x2(b)
                    for name in PREPARE:
                        slot(name, b, o)

                over_batches(dve, prepare, batch, lambda b: [slot(n, b, 1) for n in FINISH])
                dve.wait_ge(s.out_stored, B)



def build(nc, x, adj, emb, weight, bias, net_params, Wh, bh, W_out, b_out, H, W, W_ind, a_node, a_gn, a_ge, fcW, fcb, av, out):
    k = Ctx()
    k.B, k.N, k.F = x.shape
    k.NC, k.D, k.K = k.N // P, weight.shape[0], weight.shape[1]
    with ExitStack() as ctx:
        def sb(n, s, d=F32):
            return ctx.enter_context(nc.sbuf_tensor(n, s, d))

        def ps(n, s):
            return ctx.enter_context(nc.psum_tensor(n, s, F32))

        in_use = []

        def sem(n):
            in_use.append(nc.alloc_semaphore(name=n))
            return in_use[-1]

        def retire_semaphores():
            with nc.Block() as block:
                @block.gpsimd
                def _(pool):
                    nc.clear_and_free_semaphores(in_use)
            in_use.clear()

        k.sem = sem
        k.wide = [ps("wide0", [P, 1024]), ps("wide1", [P, 1024])]
        k.pair = ps("pair", [P, 1024])
        k.spare = ps("spare", [P, 1024])
        k.bank_u, k.bank_m = k.spare[:, 0:512], k.spare[:, 512:1024]

        k.ident = sb("ident", [P, P])
        k.xn = sb("xn", [P, k.NC, k.B, k.F])
        with ExitStack() as front:
            k.at_hi = front.enter_context(nc.sbuf_tensor("at_hi", [P, k.NC, k.N], F32R))
            k.at_lo = front.enter_context(nc.sbuf_tensor("at_lo", [P, k.NC, k.N], F32R))
            with ExitStack() as inner:
                k.split = [inner.enter_context(nc.sbuf_tensor(f"split{i}", [P, k.NC, k.B, 2, k.F], F32R)) for i in range(1)]
                k.w_split = inner.enter_context(nc.sbuf_tensor("w_split", [P, k.K, 2, k.F * k.D], F32R))
                k.emb = inner.enter_context(nc.sbuf_tensor("emb", [P, k.NC, k.D], F32))
                k.node_bias = inner.enter_context(nc.sbuf_tensor("node_bias", [P, k.NC, k.F], F32))
                load_and_transpose_adjacency(nc, k, adj, x, (emb, weight, bias))
                k.split.append(inner.enter_context(nc.sbuf_tensor("split1", [P, k.NC, k.B, 2, k.F], F32R)))
                node_weight_convolution(nc, k)
            layer_norm(nc, k, "_0")
            with ExitStack() as inner:
                k.split = [inner.enter_context(nc.sbuf_tensor("split2", [P, k.NC, 2, k.B, k.F], F32R))]
                relu_diffusion(nc, k, net_params)
            layer_norm(nc, k, "_1")
        retire_semaphores()
        k.delta = sb("delta", [P, k.B + 1, k.NC, k.F])
        ind_dram = nc.dram_tensor("industry", [k.B, k.F, k.N], F32)
        with ExitStack() as rows:
            k.adj = rows.enter_context(nc.sbuf_tensor("adj_rows2", [P, k.NC, k.N], F32))
            graph_attention(nc, k, adj, Wh, bh, W_out, b_out)
            layer_norm(nc, k, "_2", add=k.delta[:, 1:k.B + 1, :, :].rearrange("p b c f -> p c b f"))
            retire_semaphores()
            industry_messages(nc, k, W_ind, ind_dram)
        hypergraph_attention(nc, k, (H, W, a_node, a_gn, a_ge, fcW, fcb, av), ind_dram)
        layer_norm(nc, k, "_3", add=k.delta[:, 0:k.B, :, :].rearrange("p b c f -> p c b f"))
        stored = k.sem("stored")
        with nc.Block() as block:
            @block.sync
            def _(sp):
                for c in range(k.NC):
                    sp.dma_start(out[:, c * P:(c + 1) * P, :].rearrange("b p f -> p b f"), k.xn[:, c, :, :]).then_inc(stored, 16)
                sp.wait_ge(stored, 16 * k.NC)


_INS = ['x', 'adj', 'L0_gnn_embedding', 'L0_gnn_weight', 'L0_gnn_bias', 'L1_gnn_net_params', 'L2_gnn_Wh', 'L2_gnn_bh',
        'L2_gnn_W_out', 'L2_gnn_b_out', 'L3_gnn_H', 'L3_gnn_W', 'L3_gnn_W_ind', 'L3_gnn_a_node', 'L3_gnn_a_gn',
        'L3_gnn_a_ge', 'L3_gnn_fcW', 'L3_gnn_fcb', 'L3_gnn_av']


def kernel(**inputs):
    import numpy as _np
    import concourse.bacc as _bacc
    from concourse import mybir as _mybir
    from concourse.bass_utils import run_bass_kernel_spmd as _run

    nc = _bacc.Bacc("TRN2", target_bir_lowering=False, num_devices=1)
    arrays, args = {}, []
    for name in _INS:
        a = _np.ascontiguousarray(inputs[name])
        arrays[f"in_{name}_dram"] = a
        args.append(nc.dram_tensor(f"in_{name}_dram", a.shape, _mybir.dt.from_np(a.dtype), kind="ExternalInput").ap())
    args.append(nc.dram_tensor("out_0_dram", inputs["x"].shape, _mybir.dt.float32, kind="ExternalOutput").ap())
    build(nc, *args)
    r = _run(nc, [arrays], core_ids=[0])
    return r.results[0]["out_0_dram"]
```
